# Optimizing a Trainium2 kernel written in Bass

```python
import numpy as np
import jax
import jax.numpy as jnp

def _softmax(x, axis=-1):
    return jax.nn.softmax(x, axis=axis)

def _gelu(x):
    return jax.nn.gelu(x, approximate=True)

def _silu(x):
    return jax.nn.silu(x)

def _sigmoid(x):
    return jax.nn.sigmoid(x)

def _layernorm(x, axis=-1, eps=1e-05):
    m = jnp.mean(x, axis=axis, keepdims=True)
    v = jnp.var(x, axis=axis, keepdims=True)
    return (x - m) / jnp.sqrt(v + eps)

def _scatter_add(tgt, idx, src, axis=0):
    return tgt.at[idx].add(src)

def _segment_sum(src, seg, n):
    return jax.ops.segment_sum(src, seg, n)
kernel_name = 'mk_macaron_d2_jaxref_r8_5c6e75'

def setup_inputs(seed: int=0):
    np.random.seed(seed)
    _w = jnp.asarray

    def _L0_attn_setup():
        import jax, jax.numpy as jnp
        import numpy as np
        key = jax.random.key(seed)
        ks = jax.random.split(key, 6)
        Bsz, S, H, N = (4, 512, 128, 32)
        return {'x': jax.random.normal(ks[0], (Bsz, S, H), jnp.float32), 'A': jax.random.normal(ks[1], (N, N), jnp.float32) * 0.01, 'Bm': jax.random.normal(ks[2], (N, N), jnp.float32) * 0.01, 'C': jax.random.normal(ks[3], (H, N), jnp.float32) * 0.01, 'D': jnp.full((H,), 0.01, jnp.float32), 'W_in': jax.random.normal(ks[4], (N, H), jnp.float32) / np.sqrt(H).astype(np.float32), 'b_in': jnp.zeros((N,), jnp.float32)}
    _L0_attn_in = _L0_attn_setup()

    def _L0_ffn_setup():
        import jax, jax.numpy as jnp
        import numpy as np
        B, S, H, E, DFF = (4, 512, 128, 8, 512)
        key = jax.random.key(seed)
        k0, k1, k2, k3 = jax.random.split(key, 4)
        hidden_states = jax.random.normal(k0, (B, S, H), dtype=jnp.float32)
        gate_w = jax.random.normal(k1, (E, H), dtype=jnp.float32) * 0.02
        w1 = jax.random.normal(k2, (E, H, DFF), dtype=jnp.float32) * 0.02
        b1 = jnp.zeros((E, DFF), dtype=jnp.float32)
        w2 = jax.random.normal(k3, (E, DFF, H), dtype=jnp.float32) * 0.02
        b2 = jnp.zeros((E, H), dtype=jnp.float32)
        return {'hidden_states': hidden_states, 'gate_w': gate_w, 'w1': w1, 'b1': b1, 'w2': w2, 'b2': b2}
    _L0_ffn_in = _L0_ffn_setup()

    def _L1_attn_setup():
        import jax, jax.numpy as jnp
        import numpy as np
        N_HEADS = 16
        ROPE_BASE = 10000.0

        def _rope_tables(seq_len, d_head, dtype):
            inv_freq = 1.0 / ROPE_BASE ** (jnp.arange(0, d_head, 2, dtype=jnp.float32) / d_head)
            t = jnp.arange(seq_len, dtype=jnp.float32)
            freqs = t[:, None] * inv_freq[None, :]
            return (jnp.cos(freqs).astype(dtype), jnp.sin(freqs).astype(dtype))

        def _apply_rope(x, cos, sin):
            half = x.shape[-1] // 2
            x1, x2 = (x[..., :half], x[..., half:])
            return jnp.concatenate([x1 * cos - x2 * sin, x2 * cos + x1 * sin], axis=-1)
        key = jax.random.key(seed)
        k1, k2, k3 = jax.random.split(key, 3)
        d_model = 128
        x = jax.random.normal(k1, (2, 256, d_model), dtype=jnp.float32)
        w_qkv = jax.random.normal(k2, (d_model, 3 * d_model), dtype=jnp.float32) * d_model ** (-0.5)
        w_out = jax.random.normal(k3, (d_model, d_model), dtype=jnp.float32) * d_model ** (-0.5)
        return {'x': x, 'w_qkv': w_qkv, 'w_out': w_out}
    _L1_attn_in = _L1_attn_setup()

    def _L1_ffn_setup():
        import jax, jax.numpy as jnp
        import numpy as np
        LN_EPS = 1e-05
        NORM_EPS = 1e-12

        def _layernorm(x, gamma, beta):
            mu = x.mean(axis=-1, keepdims=True)
            var = ((x - mu) ** 2).mean(axis=-1, keepdims=True)
            return (x - mu) * jax.lax.rsqrt(var + LN_EPS) * gamma + beta

        def _l2norm(x, axis):
            n = jnp.sqrt((x ** 2).sum(axis=axis, keepdims=True))
            return x / jnp.maximum(n, NORM_EPS)
        key = jax.random.key(seed)
        ks = jax.random.split(key, 4)
        B, N, D, E, S, H = (64, 32, 128, 16, 16, 32)
        x = jax.random.normal(ks[0], (B, N, D), dtype=jnp.float32)
        mu = jax.random.normal(ks[1], (D, E, S), dtype=jnp.float32) / np.sqrt(D)
        w1 = jax.random.normal(ks[2], (E, D, H), dtype=jnp.float32) * np.sqrt(2.0 / D)
        w2 = jax.random.normal(ks[3], (E, H, D), dtype=jnp.float32) * np.sqrt(2.0 / (H + D))
        return {'x': x, 'ln_gamma': jnp.ones((D,), jnp.float32), 'ln_beta': jnp.zeros((D,), jnp.float32), 'mu': mu, 'scale': jnp.ones((1,), jnp.float32), 'w1': w1, 'b1': jnp.zeros((E, H), jnp.float32), 'w2': w2, 'b2': jnp.zeros((E, D), jnp.float32)}
    _L1_ffn_in = _L1_ffn_setup()
    _d = {'L0_attn_x': _L0_attn_in['x'], 'L0_attn_A': _L0_attn_in['A'], 'L0_attn_Bm': _L0_attn_in['Bm'], 'L0_attn_C': _L0_attn_in['C'], 'L0_attn_D': _L0_attn_in['D'], 'L0_attn_W_in': _L0_attn_in['W_in'], 'L0_attn_b_in': _L0_attn_in['b_in'], 'L0_ffn_gate_w': _L0_ffn_in['gate_w'], 'L0_ffn_w1': _L0_ffn_in['w1'], 'L0_ffn_b1': _L0_ffn_in['b1'], 'L0_ffn_w2': _L0_ffn_in['w2'], 'L0_ffn_b2': _L0_ffn_in['b2'], 'L1_attn_w_qkv': _L1_attn_in['w_qkv'], 'L1_attn_w_out': _L1_attn_in['w_out'], 'L1_ffn_ln_gamma': _L1_ffn_in['ln_gamma'], 'L1_ffn_ln_beta': _L1_ffn_in['ln_beta'], 'L1_ffn_mu': _L1_ffn_in['mu'], 'L1_ffn_scale': _L1_ffn_in['scale'], 'L1_ffn_w1': _L1_ffn_in['w1'], 'L1_ffn_b1': _L1_ffn_in['b1'], 'L1_ffn_w2': _L1_ffn_in['w2'], 'L1_ffn_b2': _L1_ffn_in['b2']}
    _x0 = _d['L0_attn_x']
    _d['L0_attn_x'] = jax.random.normal(jax.random.fold_in(jax.random.key(seed), 1), (8, 512, 128), dtype=_x0.dtype)
    del _x0
    return _d

def reference(L0_attn_x, L0_attn_A, L0_attn_Bm, L0_attn_C, L0_attn_D, L0_attn_W_in, L0_attn_b_in, L0_ffn_gate_w, L0_ffn_w1, L0_ffn_b1, L0_ffn_w2, L0_ffn_b2, L1_attn_w_qkv, L1_attn_w_out, L1_ffn_ln_gamma, L1_ffn_ln_beta, L1_ffn_mu, L1_ffn_scale, L1_ffn_w1, L1_ffn_b1, L1_ffn_w2, L1_ffn_b2):

    def _L0_attn_ref(x, A, Bm, C, D, W_in, b_in):
        import jax, jax.numpy as jnp
        import numpy as np
        u = jnp.einsum('bsh,nh->bsn', x, W_in) + b_in
        uB = jnp.einsum('bsn,mn->bsm', u, Bm)

        def step(h, uB_t):
            h = h @ A + uB_t
            return (h, h)
        h0 = jnp.zeros((x.shape[0], A.shape[0]), x.dtype)
        _, hs = jax.lax.scan(step, h0, jnp.swapaxes(uB, 0, 1))
        hs = jnp.swapaxes(hs, 0, 1)
        return jnp.einsum('bsn,hn->bsh', hs, C) + D

    def _L0_ffn_ref(hidden_states, gate_w, w1, b1, w2, b2):
        import jax, jax.numpy as jnp
        import numpy as np
        B, S, H, E, DFF = (4, 512, 128, 8, 512)
        b, s, h = hidden_states.shape
        x = hidden_states.reshape(-1, h)
        gate_logits = x @ gate_w.T
        gate_probs = jax.nn.softmax(gate_logits, axis=-1)
        expert_idx = jnp.argmax(gate_probs, axis=-1)
        expert_w = jnp.take_along_axis(gate_probs, expert_idx[:, None], axis=1)[:, 0]
        out = jnp.zeros_like(x)
        n_experts = w1.shape[0]
        for e in range(n_experts):
            ye = jax.nn.relu(x @ w1[e] + b1[e]) @ w2[e] + b2[e]
            sel = (expert_idx == e)[:, None]
            out = out + jnp.where(sel, ye * expert_w[:, None], 0.0)
        return out.reshape(b, s, h)

    def _L1_attn_ref(x, w_qkv, w_out):
        import jax, jax.numpy as jnp
        import numpy as np
        N_HEADS = 16
        ROPE_BASE = 10000.0

        def _rope_tables(seq_len, d_head, dtype):
            inv_freq = 1.0 / ROPE_BASE ** (jnp.arange(0, d_head, 2, dtype=jnp.float32) / d_head)
            t = jnp.arange(seq_len, dtype=jnp.float32)
            freqs = t[:, None] * inv_freq[None, :]
            return (jnp.cos(freqs).astype(dtype), jnp.sin(freqs).astype(dtype))

        def _apply_rope(x, cos, sin):
            half = x.shape[-1] // 2
            x1, x2 = (x[..., :half], x[..., half:])
            return jnp.concatenate([x1 * cos - x2 * sin, x2 * cos + x1 * sin], axis=-1)
        B, S, D = x.shape
        H = N_HEADS
        dh = D // H
        scale = dh ** (-0.5)
        qkv = x @ w_qkv
        q, k, v = jnp.split(qkv, 3, axis=-1)

        def to_heads(t):
            return t.reshape(B, S, H, dh).transpose(0, 2, 1, 3)
        q, k, v = (to_heads(q), to_heads(k), to_heads(v))
        cos, sin = _rope_tables(S, dh, x.dtype)
        q = _apply_rope(q, cos, sin)
        k = _apply_rope(k, cos, sin)
        scores = jnp.einsum('bhqd,bhkd->bhqk', q, k) * scale
        causal = jnp.tril(jnp.ones((S, S), dtype=bool))
        scores = jnp.where(causal, scores, jnp.finfo(scores.dtype).min)
        attn = jax.nn.softmax(scores, axis=-1)
        out = jnp.einsum('bhqk,bhkd->bhqd', attn, v)
        out = out.transpose(0, 2, 1, 3).reshape(B, S, D)
        return out @ w_out

    def _L1_ffn_ref(x, ln_gamma, ln_beta, mu, scale, w1, b1, w2, b2):
        import jax, jax.numpy as jnp
        import numpy as np
        LN_EPS = 1e-05
        NORM_EPS = 1e-12

        def _layernorm(x, gamma, beta):
            mu = x.mean(axis=-1, keepdims=True)
            var = ((x - mu) ** 2).mean(axis=-1, keepdims=True)
            return (x - mu) * jax.lax.rsqrt(var + LN_EPS) * gamma + beta

        def _l2norm(x, axis):
            n = jnp.sqrt((x ** 2).sum(axis=axis, keepdims=True))
            return x / jnp.maximum(n, NORM_EPS)
        B, N, D = x.shape
        _, E, S = mu.shape
        xn = _layernorm(x, ln_gamma, ln_beta)
        x_unit = _l2norm(xn, axis=-1)
        mu_unit = _l2norm(mu, axis=0)
        logits = jnp.einsum('bnd,des->bnes', x_unit * scale, mu_unit)
        dispatch = jax.nn.softmax(logits, axis=1)
        combine = jax.nn.softmax(logits.reshape(B, N, E * S), axis=-1).reshape(B, N, E, S)
        slot_in = jnp.einsum('bnd,bnes->besd', xn, dispatch)
        h = jax.nn.gelu(jnp.einsum('besd,edh->besh', slot_in, w1) + b1[None, :, None, :], approximate=False)
        slot_out = jnp.einsum('besh,ehd->besd', h, w2) + b2[None, :, None, :]
        out = jnp.einsum('besd,bnes->bnd', slot_out, combine)
        return out
    x = L0_attn_x
    x = x + 0.5 * _L0_ffn_ref(_layernorm(x, axis=-1), L0_ffn_gate_w, L0_ffn_w1, L0_ffn_b1, L0_ffn_w2, L0_ffn_b2)
    x = x + _L0_attn_ref(_layernorm(x, axis=-1), L0_attn_A, L0_attn_Bm, L0_attn_C, L0_attn_D, L0_attn_W_in, L0_attn_b_in)
    x = x + 0.5 * _L0_ffn_ref(_layernorm(x, axis=-1), L0_ffn_gate_w, L0_ffn_w1, L0_ffn_b1, L0_ffn_w2, L0_ffn_b2)
    x = x + 0.5 * _L1_ffn_ref(_layernorm(x, axis=-1), L1_ffn_ln_gamma, L1_ffn_ln_beta, L1_ffn_mu, L1_ffn_scale, L1_ffn_w1, L1_ffn_b1, L1_ffn_w2, L1_ffn_b2)
    x = x + _L1_attn_ref(_layernorm(x, axis=-1), L1_attn_w_qkv, L1_attn_w_out)
    x = x + 0.5 * _L1_ffn_ref(_layernorm(x, axis=-1), L1_ffn_ln_gamma, L1_ffn_ln_beta, L1_ffn_mu, L1_ffn_scale, L1_ffn_w1, L1_ffn_b1, L1_ffn_w2, L1_ffn_b2)
    return x

_drawn_inputs = setup_inputs


def setup_inputs(seed=0):
    import zlib

    import numpy as np

    out = dict(_drawn_inputs(seed))
    spreads = {'L0_attn_D': (0.009999999776482582, 0.6),
     'L0_attn_b_in': (0.0, 0.8),
     'L0_ffn_b1': (0.0, 0.8),
     'L0_ffn_b2': (0.0, 0.426),
     'L1_ffn_ln_gamma': (1.0, 0.6),
     'L1_ffn_ln_beta': (0.0, 0.661),
     'L1_ffn_b1': (0.0, 0.8),
     'L1_ffn_b2': (0.0, 0.946)}
    factors = {'L0_attn_A': 8.0,
     'L0_attn_Bm': 8.0,
     'L0_attn_C': 8.0,
     'L0_attn_W_in': 8.0,
     'L0_ffn_w1': 5.046,
     'L0_ffn_w2': 3.909,
     'L1_ffn_mu': 28.151,
     'L1_ffn_w1': 4.048,
     'L1_ffn_w2': 3.497}
    for name, (base, spread) in spreads.items():
        noise = np.random.default_rng([zlib.crc32(name.encode()), seed]).standard_normal(out[name].shape)
        drawn = base * np.exp(spread * noise) if base else spread * noise
        out[name] = jnp.asarray(drawn.astype(out[name].dtype))
    for name, factor in factors.items():
        out[name] = (out[name] * factor).astype(out[name].dtype)
    return out
```

```python
from contextlib import ExitStack

import concourse.bass as bass
import numpy as np
from concourse import mybir

F32 = mybir.dt.float32
BF16 = mybir.dt.bfloat16
I32 = mybir.dt.int32
ALU = mybir.AluOpType
ACT = mybir.ActivationFunctionType
AX = mybir.AxisListType

P = 128
B, S, D = 8, 512, 128
T = B * S // P
TB = S // P
N = 32
NJ = P // N
LEVELS = 9
E, F = 8, 512
FC = F // P
ROWS = T + E - 1
ME, MS, MH = 16, 16, 32
SLOTS = ME * MS
MG = P // MH
H, DH = 16, 8
Q_PART, K_PART = (0, 0, 1, 0, 2, 1), (0, 1, 0, 2, 0, 1)
STACK = DH * len(Q_PART)
E_AT = (0, 512, 1024, 896)
E_LEN = 1280
BIG = 1e30
ONE_ONE = float(np.array([0x3F803F80], np.uint32).view(np.float32)[0])
AHEAD = 6
NOWHERE = 8192
EPS = 1e-5

C_ID, C_EM, C_TILE, C_TCOL, C_P1, C_TRI, C_IOTA, C_ONE = 0, 128, 384, 423, 455, 456, 584, 712
C_ALL = C_ONE + 256
R_COS, R_SIN, R_MQ, R_MK, R_ALL = 0, S, 2 * S, 2 * S + P, 2 * S + 2 * P


def shape_constants():
    c = np.zeros((P, C_ALL), np.float32)
    p = np.arange(P)
    c[:, C_ID:C_ID + P] = np.eye(P)
    c[:, C_EM:C_EM + E * T] = np.repeat(np.arange(E) - E, T)
    c[:, C_TILE:C_TILE + ROWS] = np.arange(ROWS)
    c[:, C_TCOL:C_TCOL + T] = np.arange(T)
    c[:, C_P1] = p + 1
    c[:, C_TRI:C_TRI + P] = p[:, None] < p[None, :]
    c[:, C_IOTA:C_IOTA + P] = p
    c[:, C_ONE:C_ONE + 256] = 1.0
    return c


def rotary_constants():
    c = np.zeros((P, R_ALL), np.float32)
    inv_freq = (1.0 / np.float32(10000.0) ** (np.arange(0, DH, 2, dtype=np.float32) / DH)).astype(np.float32)
    freqs = np.arange(S, dtype=np.float32)[None, :] * inv_freq[:, None]
    dim = (np.arange(P) // (H // 2)) % DH % (DH // 2)
    c[:, R_COS:R_COS + S] = np.cos(freqs)[dim]
    c[:, R_SIN:R_SIN + S] = np.sin(freqs)[dim]
    p = np.arange(P)
    c[:, R_MQ:R_MQ + P] = np.where(p[None, :] > p[:, None], -BIG, 0)
    c[:, R_MK:R_MK + P] = np.where(p[:, None] > p[None, :], -BIG, 0)
    return c


def later(i):
    return not isinstance(i, int) or i > 0


def peeled(engine, start, stop, body):
    body(start)
    with engine.Fori(start + 1, stop) as i:
        body(i)


class Chain:

    def __init__(self, engine, sem, n=0):
        self.engine, self.sem, self.n = engine, sem, n

    def mark(self, instruction):
        instruction.then_inc(self.sem, 1)
        self.n += 1

    def sync(self):
        self.engine.wait_ge(self.sem, self.n)

    def __call__(self, instruction):
        self.mark(instruction)
        self.sync()


def build(nc, a, consts, rotary, out, xhat_dram, yrow_dram, stages="fsf"):
    ctx = ExitStack()
    with ctx:
        def sb(name, shape, dt=F32):
            return ctx.enter_context(nc.sbuf_tensor(name, shape, dt))

        def sem(name):
            return ctx.enter_context(nc.semaphore(name))

        psum = ctx.enter_context(nc.psum_tensor("psum", [P, 8 * 512], F32))
        bank = [psum[:, 512 * i:512 * i + 512] for i in range(8)]
        psum_pair = [psum[:, 1024 * i + 1024:1024 * i + 2048] for i in range(2)]

        x = sb("x", [P, T, D])
        cst = sb("cst", [P, C_ALL])
        ident = cst[:, C_ID:C_ID + P]
        tri = sb("tri", [P, P], BF16)
        ones_bf = sb("ones_bf", [P, P], BF16)
        iota_bf = sb("iota_bf", [P, P], BF16)
        half_stats = sb("half_stats", [P, T, 6])
        st = sb("st", [P, 10, T])
        mean, rstd = st[:, 0, :], st[:, 1, :]
        xh = sb("xh", [P, 8, D])
        xT = sb("xT", [P, 2, S])

        arena = sb("arena", [P, 2 * B * S])

        arena2 = sb("arena2", [P, 10752])
        arena3 = sb("arena3", [P, 2 * TB * E_LEN])
        arena4 = sb("arena4", [P, 8192])

        def carve(area, at, shape, dt=F32):
            n = int(np.prod(shape)) * (2 if dt == BF16 else 4) // 4
            v = area[:, at:at + n]
            if dt != F32:
                v = v.bitcast(dt)
            names = "abcde"[:len(shape)]
            return v.rearrange(f"p ({' '.join(names)}) -> p {' '.join(names)}", **dict(zip(names[1:], shape[1:]))) if len(shape) > 1 else v

        w1 = arena2[:, 0:4096].rearrange("p (e f) -> p e f", e=E)
        w2 = arena2[:, 4096:8192].rearrange("p (e c d) -> p e c d", e=E, c=FC)
        b1rows = arena2[:, 8192:10240].bitcast(BF16)
        b2rows = arena2[:, 10240:10752].bitcast(BF16)
        ones3 = sb("ones3", [P, P], BF16)
        bsplit = carve(arena4, 6100, (2, 2, 32))
        bparts = carve(arena4, 6228, (2, 3, 32), BF16)
        gateT = sb("gateT", [P, E])
        gate_rows = arena4[0:E, 6400:6400 + D]
        r_log = carve(arena4, 0, (E, T))
        r_exp = carve(arena4, 256, (E, T))
        r_eq = carve(arena4, 512, (E, T))
        r_one = carve(arena4, 768, (E, T))
        r_onebf = carve(arena4, 5840, (E, T), BF16)
        r_tot = carve(arena4, 1024, (E, T))
        r_scan = carve(arena4, 1280, (E, T))
        r_t = carve(arena4, 1536, (8, T))
        r_e = sb("r_e", [P, 8, E])
        r_ti = sb("r_ti", [P, 3, T], I32)
        r_ei = sb("r_ei", [P, 2, E], I32)
        expert_cmp = carve(arena4, 5248, (ROWS, E))[0:1]
        expert_f = sb("expert_f", [1, ROWS])
        expert_of = sb("expert_of", [1, ROWS], I32)
        lane_hot = arena[:, 4096:6144].bitcast(BF16).rearrange("p (t l) -> p t l", t=T)
        tile_hot = arena[:, 6144:6144 + 3 * T * ROWS // 2].bitcast(BF16).rearrange("p (m t r) -> p m t r", m=3, t=T)
        inv = arena4[:, 5600:5600 + 2 * ROWS]
        inv_v = carve(arena4, 5700, (3, ROWS))
        gather_row = sb("gather_row", [P, ROWS], I32)
        scatter_row = sb("scatter_row", [P, ROWS], I32)
        xg = carve(arena4, 1792, (AHEAD, D))
        xgT = carve(arena4, 2560, (2, P))
        hid = carve(arena4, 2816, (2, F))
        hidT = carve(arena4, 3840, (2, FC, P))
        yg = carve(arena4, 4864, (3, D))
        yback = arena[:, 0:T * D].rearrange("p (t d) -> p t d", t=T)

        win_rows = arena3[0:N, 9600:9728]
        win_z = carve(arena3, 8448, (NJ, P))
        bm_rows = carve(arena3, 9472, (NJ, N))[0:N]
        bm_diag = arena3[:, 9216:9344]
        c_rows = carve(arena3, 9344, (NJ, N))
        c_diag = carve(arena3, 7936, (NJ, D))
        b_in = sb("b_in", [P, 1])
        d_rep = arena3[:, 9728:9856]
        a_pow = carve(arena3, 6144, (LEVELS, 64 + P))
        a_powT = carve(arena3, 8960, (2, P))
        u1 = carve(arena, 0, (B, P))
        state = carve(arena, 1024, (B, P))

        mu = sb("mu", [P, SLOTS])
        mu_t = carve(arena, 0, (2, SLOTS))
        gamma = sb("gamma", [P, D])
        beta = sb("beta", [P, D])
        mscale = sb("mscale", [P, 1])
        mw1 = sb("mw1", [P, ME, MH])
        mw2 = sb("mw2", [P, MG, D])
        mb1 = sb("mb1", [P, MG])
        mb2 = sb("mb2", [P, 2, D])
        xn = carve(arena3, 0, (T, D))
        square = arena2[:, 10496:10496 + D]
        comb = arena2[:, 0:2048].rearrange("p (h k s) -> p h k s", h=2, k=TB)
        disp_s = arena2[:, 2048:4096].rearrange("p (h j t) -> p h j t", h=2, j=2)
        combT = arena[:].rearrange("p (h b t) -> p h b t", h=2, b=B)
        disp = arena2[:, 4096:6144].rearrange("p (h k s) -> p h k s", h=2, k=TB)
        slot_in = carve(arena2, 10240, (2, D))
        slotT = arena2[:, 6144:8192].rearrange("p (e b s) -> p e b s", e=ME, b=B)
        hid_diag = carve(arena3, 4096, (MG, B, MG, MS))
        slot_out = arena2[:, 8192:10240].rearrange("p (h b d) -> p h b d", h=2, b=B)
        neg_c = sb("neg_c", [P, B, TB])
        neg_d = sb("neg_d", [P, B, 2])
        sum_c = sb("sum_c", [P, T])
        inv_c = sb("inv_c", [P, T])
        sum_d = sb("sum_d", [P, B, 2])
        inv_d = sb("inv_d", [P, B, 2])

        rot = sb("rot", [P, R_ALL])
        cos, sin = rot[:, R_COS:R_COS + S], rot[:, R_SIN:R_SIN + S]
        mask_q = sb("mask_q", [P, P], BF16)
        mask_k = sb("mask_k", [P, P], BF16)
        ident_bf = sb("ident_bf", [P, P], BF16)
        wqkv = sb("wqkv", [P, 3 * D])
        wqk = sb("wqk", [P, 4, P])
        wout = sb("wout", [P, D])
        q_stack = [carve(arena, 4096 * i, (H, S), BF16) for i in range(2)]
        k_stack = [carve(arena2, 4096 * i, (H, S), BF16) for i in range(2)]
        prob_e = [carve(arena3, TB * E_LEN * i, (TB, E_LEN)) for i in range(2)]
        v_aug = [carve(arena4, 2048 * i, (TB, H, 32)) for i in range(2)]
        o_t = [carve(arena4, 4096 + 2048 * i, (TB, S)) for i in range(2)]
        raw = sb("raw", [P, 2, S])
        rope = carve(arena2, 8192, (2, S))
        cut = sb("cut", [P, 2, 3, S], BF16)
        neg_m = sb("neg_m", [P, 2, TB, H])
        m_left = sb("m_left", [P, TB, DH])
        m_cut = sb("m_cut", [P, 2, TB, 3, H // 2], BF16)
        m_rows = carve(arena2, 10240, (2, S), BF16)[0:3 * H // 2]
        o_den = sb("o_den", [P, H])
        o_tok = carve(arena2, 9216, (TB, D))
        o_hd = arena2[:, 9728:9728 + S]
        attw_in, att_w = sem("attw_in"), sem("att_w")

        mixw_in, mix_set = sem("mixw_in"), [sem(f"mix_set{i}") for i in range(4)]
        x_in = [sem(f"x_in{i}") for i in range(4)]
        cst_in, w1_in, w2_in, bias_in, biasrow_in = (sem(n) for n in (
            "cst_in", "w1_in", "w2_in", "bias_in", "biasrow_in"))
        gate_in, scanw_in, a_in = sem("gate_in"), sem("scanw_in"), sem("a_in")
        bf_ready, zeroed, bias_cut, turned_w, placed_w = (sem(n) for n in (
            "bf_ready", "zeroed", "bias_cut", "turned_w", "placed_w"))
        pow_mm, pow_kept = sem("pow_mm"), sem("pow_kept")
        stored_out, rows_zeroed = sem("stored_out"), sem("rows_zeroed")
        x_done = [sem(f"x_done{i}") for i in range(len(stages) + 1)]

        def mix_loads(sp):
            if "a" in stages:
                sp.dma_start(rot[:], rotary).then_inc(attw_in, 16)
                sp.dma_start(wqkv[:], a["L1_attn_w_qkv"]).then_inc(attw_in, 16)
                sp.dma_start(wout[:], a["L1_attn_w_out"]).then_inc(attw_in, 16)
            if "m" in stages:
                sp.dma_start(mu[:], a["L1_ffn_mu"].rearrange("d e s -> d (e s)")).then_inc(mixw_in, 16)
                sp.dma_start(gamma[:], a["L1_ffn_ln_gamma"].partition_broadcast(P)).then_inc(mixw_in, 16)
                sp.dma_start(beta[:], a["L1_ffn_ln_beta"].partition_broadcast(P)).then_inc(mixw_in, 16)
                sp.dma_start(mscale[:], a["L1_ffn_scale"].partition_broadcast(P)).then_inc(mixw_in, 16)
                sp.dma_start(mw1[:], a["L1_ffn_w1"].rearrange("e d h -> d e h")).then_inc(mixw_in, 16)
                for q in range(MG):
                    sp.dma_start(mw2[MH * q:MH * q + MH], a["L1_ffn_w2"].rearrange("(g q) h d -> q h g d", q=MG)[q]).then_inc(mixw_in, 16)
                    sp.dma_start(mb1[MH * q:MH * q + MH], a["L1_ffn_b1"].rearrange("(g q) h -> q h g", q=MG)[q],
                                 allow_slow_non_contiguous=True).then_inc(mixw_in, 16)
                for e in range(ME):
                    h, r = e // 8, MS * (e % 8)
                    sp.dma_start(mb2[r:r + MS, h, :], a["L1_ffn_b2"][e].partition_broadcast(MS)).then_inc(mixw_in, 16)

        def load_sync(sp):
            xin = a["L0_attn_x"].rearrange("b (k p) d -> p (b k) d", p=P)
            sp.dma_start(cst[:], consts).then_inc(cst_in, 16)
            for i in range(4):
                sp.dma_start(x[:, 8 * i:8 * i + 8, :], xin[:, 8 * i:8 * i + 8, :]).then_inc(x_in[i], 16)
            if "f" not in stages:
                mix_loads(sp)
                return
            sp.dma_start(bsplit[:, 0, 0, :], a["L0_ffn_b1"].rearrange("e f -> (e f)").rearrange("(p i) -> p i", p=P)).then_inc(bias_in, 16)
            sp.dma_start(bsplit[:, 1, 0, 0:8], a["L0_ffn_b2"].rearrange("e f -> (e f)").rearrange("(p i) -> p i", p=P)).then_inc(bias_in, 16)
            mix_loads(sp)
            sp.dma_start(w1[:], a["L0_ffn_w1"].rearrange("e d f -> d e f")).then_inc(w1_in, 16)
            sp.wait_ge(bias_cut, 1)
            sp.wait_ge(rows_zeroed, 2)
            for r in range(3):
                sp.dma_start(b1rows[r:r + 1, :], bparts[:, 0, r, :]).then_inc(biasrow_in, 16)
                sp.dma_start(b2rows[r:r + 1, :], bparts[:, 1, r, 0:8]).then_inc(biasrow_in, 16)

        def load_scalar(act):
            act.dma_start(gate_rows[:], a["L0_ffn_gate_w"]).then_inc(gate_in, 16)
            if "s" in stages:
                act.dma_start(win_rows[:], a["L0_attn_W_in"]).then_inc(scanw_in, 16)
                for j in range(NJ):
                    act.dma_start(bm_rows[:, j, :], a["L0_attn_Bm"]).then_inc(scanw_in, 16)
                    act.dma_start(c_rows[:, j, :], a["L0_attn_C"]).then_inc(scanw_in, 16)
                    act.dma_start(b_in[N * j:N * j + N, :], a["L0_attn_b_in"].rearrange("(n o) -> n o", o=1)).then_inc(scanw_in, 16)
                act.dma_start(d_rep[:], a["L0_attn_D"].partition_broadcast(P)).then_inc(scanw_in, 16)
                act.wait_ge(zeroed, 1)
                for j in range(NJ):
                    act.dma_start(a_pow[N * j:N * j + N, 0, 64 + N * j:64 + N * j + N], a["L0_attn_A"]).then_inc(a_in, 16)
            if "f" in stages:
                act.dma_start(w2[:], a["L0_ffn_w2"].rearrange("e (c f) d -> f e c d", f=P)).then_inc(w2_in, 16)

        def setup_gpsimd(pool):
            if "f" in stages:
                pool.memset(b1rows[:], 0.0).then_inc(rows_zeroed, 1)
                pool.memset(b2rows[:], 0.0).then_inc(rows_zeroed, 1)
            pool.memset(a_pow[:], 0.0).then_inc(zeroed, 1)
            pool.memset(win_z[:], 0.0)
            pool.memset(bm_diag[:], 0.0)
            pool.memset(c_diag[:], 0.0).then_inc(zeroed, 1)

        def setup_vector(dve, chain):
            dve.wait_ge(cst_in, 16)
            nc.vector.tensor_copy(tri[:], cst[:, C_TRI:C_TRI + P])
            nc.vector.tensor_copy(iota_bf[:], cst[:, C_IOTA:C_IOTA + P])
            nc.vector.memset(ones_bf[:], 1.0)
            chain(nc.vector.memset(ones3[:], 0.0))
            nc.vector.memset(ones3[0:3, :], 1.0).then_inc(bf_ready, 1)
            if "f" in stages:
                dve.wait_ge(bias_in, 32)
            for w, n in ((0, 32), (1, 8)) if "f" in stages else ():
                v, left = bsplit[:, w, 0, 0:n], bsplit[:, w, 1, 0:n]
                part = [bparts[:, w, r, 0:n] for r in range(3)]
                chain(nc.vector.tensor_copy(part[0], v))
                chain(nc.vector.tensor_tensor(left, v, part[0], ALU.subtract))
                chain(nc.vector.tensor_copy(part[1], left))
                chain(nc.vector.tensor_tensor(part[2], left, part[1], ALU.subtract))
            dve.sem_inc(bias_cut, 1)
            dve.wait_ge(turned_w, 1)
            chain(nc.vector.tensor_copy(gateT[:], bank[0][:, 0:E]))
            dve.sem_inc(placed_w, 1)
            if "s" in stages:
                dve.wait_ge(zeroed, 2)
                dve.wait_ge(turned_w, 2)
                for j in range(NJ):
                    rows, cols = slice(N * j, N * j + N), slice(N * j, N * j + N)
                    chain(nc.vector.tensor_copy(win_z[:, j, cols], bank[1][:, 0:N]))
                    chain(nc.vector.tensor_copy(bm_diag[rows, cols], bank[1][rows, 128:128 + N]))
                    chain(nc.vector.tensor_copy(c_diag[rows, j, :], bank[1][rows, 256:256 + D]))
                chain(nc.vector.tensor_copy(a_powT[:, 0, :], bank[1][:, 384:512]))
                dve.sem_inc(placed_w, 1)
                for l in range(1, LEVELS):
                    dve.wait_ge(pow_mm, l)
                    chain(nc.vector.tensor_copy(a_pow[:, l, 64:], bank[2 + l % 2][:, 0:P]))
                    chain(nc.vector.tensor_copy(a_powT[:, l % 2, :], bank[2 + l % 2][:, P:2 * P]))
                    dve.sem_inc(pow_kept, 1)

        def setup_tensor(pe):
            pe.wait_ge(cst_in, 16)
            pe.wait_ge(gate_in, 16)
            pe.transpose(bank[0][:, 0:E], gate_rows[:], ident[0:E, 0:E]).then_inc(turned_w, 1)
            if "s" in stages:
                pe.wait_ge(scanw_in, 16 * (2 + 3 * NJ))
                pe.wait_ge(a_in, 16 * NJ)
                pe.transpose(bank[1][:, 0:N], win_rows[:], ident[0:N, 0:N])
                pe.transpose(bank[1][:, 128:128 + N], bm_rows[:].rearrange("m j n -> m (j n)"), ident[0:N, 0:N])
                pe.transpose(bank[1][:, 256:256 + D], c_rows[:].rearrange("m j n -> m (j n)"), ident)
                pe.transpose(bank[1][:, 384:512], a_pow[:, 0, 64:], ident).then_inc(turned_w, 1)
                pe.wait_ge(placed_w, 2)
                for l in range(1, LEVELS):
                    if l > 1:
                        pe.wait_ge(pow_kept, l - 1)
                    last, lastT = a_pow[:, l - 1, 64:], a_powT[:, (l - 1) % 2, :]
                    pe.matmul(bank[2 + l % 2][:, 0:P], lastT, last, start=True, stop=True)
                    pe.matmul(bank[2 + l % 2][:, P:2 * P], last, lastT, start=True, stop=True).then_inc(pow_mm, 1)

        def stats_vector(dve, chain, n, s, at):
            if n == 0:
                for i in range(4):
                    dve.wait_ge(x_in[i], 16)
            else:
                dve.wait_ge(x_done[n], T)
            with dve.Fori(0, 4) as i:
                for r in range(8):
                    nc.vector.bn_stats(half_stats[:, bass.ds(8 * i + r, 1), :], x[:, bass.ds(8 * i + r, 1), :]).then_inc(s["stat"], 1)
            dve.wait_ge(s["stat"], at["stat"] + T)
            me, m2e, mo, m2o = (half_stats[:, :, c] for c in (1, 2, 4, 5))
            nc.vector.tensor_tensor(st[:, 2, :], me, mo, ALU.add)
            nc.vector.tensor_tensor(st[:, 3, :], me, mo, ALU.subtract)
            chain(nc.vector.tensor_tensor(st[:, 4, :], m2e, m2o, ALU.add))
            nc.vector.tensor_scalar(mean, st[:, 2, :], 0.5, None, ALU.mult)
            chain(nc.vector.scalar_tensor_tensor(st[:, 5, :], st[:, 3, :], float(P // 4), st[:, 3, :], ALU.mult, ALU.mult))
            chain(nc.vector.tensor_tensor(st[:, 6, :], st[:, 4, :], st[:, 5, :], ALU.add))
            nc.vector.tensor_scalar(st[:, 7, :], st[:, 6, :], 1.0 / P, EPS, ALU.mult, ALU.add).then_inc(s["var"], 1)
            dve.wait_ge(s["sqrt"], at["sqrt"] + 1)
            chain(nc.vector.reciprocal(rstd, st[:, 8, :]))

        def stats_scalar(act, s, at):
            act.wait_ge(s["var"], at["var"] + 1)
            nc.scalar.activation(st[:, 8, :], st[:, 7, :], ACT.Sqrt).then_inc(s["sqrt"], 1)

        FFN_COUNTS = dict(stat=T, var=1, sqrt=1, v=0, normed=T, turned=T, xT_ready=B, gated=B, log_ready=1, exp_ready=1,
                          one_ready=1, ranked=1, hot_ready=1, inverted=1, rows_ready=1, expert_ready=1, g_turned=ROWS,
                          xgT=ROWS, h_mm=ROWS, h_relu=ROWS, h_turned=ROWS, hT_ready=ROWS, y_mm=ROWS, y_ready=ROWS)
        RING_COUNTS = dict(stored=[16 * 4] * 2, gathered=[16 * len(range(i, ROWS, AHEAD)) for i in range(AHEAD)],
                           scattered=[16 * len(range(i, ROWS, 3)) for i in range(3)], back=[16] * 4)
        ffn_sems = {k: sem(f"f_{k}") for k in FFN_COUNTS}
        ffn_rings = {k: [sem(f"f_{k}{i}") for i in range(len(v))] for k, v in RING_COUNTS.items()}
        chains = {"f": 0, "m": 0}

        def ffn(n):
            s, at = ffn_sems, {k: v * stages[:n].count("f") for k, v in FFN_COUNTS.items()}
            stored, gathered, scattered, back = (ffn_rings[k] for k in RING_COUNTS)
            for k, counts in RING_COUNTS.items():
                at[k] = [v * stages[:n].count("f") for v in counts]

            def sync(sp):
                rows = xhat_dram.rearrange("(t p) d -> p t d", p=P)
                with sp.Fori(0, 4) as i:
                    for h in range(2):
                        sp.wait_ge(s["normed"], at["normed"] + 8 * i + 4 * h + 4)
                        sp.dma_start(rows[:, bass.ds(8 * i + 4 * h, 4), :], xh[:, 4 * h:4 * h + 4, :]).then_inc(stored[h], 16)
                for q in range(3):
                    sp.wait_ge(scattered[q], at["scattered"][q] + 16 * (ROWS // 3))
                for q in range(4):
                    sp.dma_start(yback[:, 8 * q:8 * q + 8, :],
                                 yrow_dram.rearrange("(t p) d -> p t d", p=P)[:, 8 * q:8 * q + 8, :]).then_inc(back[q], 16)

            def vector(dve):
                chain = Chain(dve, s["v"], chains["f"])
                stats_vector(dve, chain, n, s, at)

                def normalise(i):
                    for r in range(8):
                        if r % 4 == 0 and later(i):
                            dve.wait_ge(s["turned"], at["turned"] + 8 * i)
                            dve.wait_ge(stored[r // 4], at["stored"][r // 4] + 16 * i)
                        t = bass.ds(8 * i + r, 1)
                        nc.vector.tensor_scalar(xh[:, r, :], x[:, t, :], mean[:, t], rstd[:, t],
                                                ALU.subtract, ALU.mult).then_inc(s["normed"], 1)

                peeled(dve, 0, 4, normalise)
                dve.wait_ge(s["gated"], at["gated"] + B)
                chain(nc.vector.tensor_copy(r_log[:], bank[2][:, 0:T * E].rearrange("p (t e) -> p e t", e=E)))
                by_token = lambda v: v.rearrange("p e t -> p t e")
                over_e = lambda v: v.unsqueeze(1).to_broadcast([P, E, T])
                over_t = lambda v: v.unsqueeze(2).to_broadcast([P, E, T])
                top, esum, prob, first, dest, lane, row = (r_t[:, k, :] for k in range(7))
                em = cst[:, C_EM:C_EM + E * T].rearrange("p (e t) -> p e t", e=E)
                chain(nc.vector.tensor_reduce(top, by_token(r_log[:]), AX.X, ALU.max))
                nc.vector.tensor_tensor(r_exp[:], r_log[:], over_e(top), ALU.subtract).then_inc(s["log_ready"], 1)
                chain(nc.vector.tensor_tensor(r_eq[:], r_log[:], over_e(top), ALU.is_equal))
                chain(nc.vector.tensor_tensor(r_scan[:], r_eq[:], em, ALU.mult))
                chain(nc.vector.tensor_reduce(first, by_token(r_scan[:]), AX.X, ALU.min))
                chain(nc.vector.tensor_tensor(r_one[:], em, over_e(first), ALU.is_equal))
                nc.vector.tensor_copy(r_onebf[:], r_one[:]).then_inc(s["one_ready"], 1)
                dve.wait_ge(s["exp_ready"], at["exp_ready"] + 1)
                chain(nc.vector.tensor_reduce(esum, by_token(r_log[:]), AX.X, ALU.add))
                chain(nc.vector.reciprocal(prob, esum))
                chain(nc.vector.tensor_scalar(prob, prob, 0.5, None, ALU.mult))
                dve.wait_ge(s["ranked"], at["ranked"] + 1)
                chain(nc.vector.tensor_copy(r_tot[:], bank[3][:, 256:512].rearrange("p (e t) -> p e t", e=E)))
                flat = lambda v: v.rearrange("p e t -> p (e t)")
                one = cst[:, C_ONE:C_ONE + 256]
                cnt, tiles, tiles_to, cnt_to, r_a, r_b, off = (r_e[:, k, :] for k in range(7))
                nc.vector.tensor_tensor_scan(flat(r_scan[:]), one, flat(r_tot[:]), 0.0, ALU.mult, ALU.add)
                chain(nc.vector.tensor_reduce(cnt, r_tot[:], AX.X, ALU.add))
                chain(nc.vector.tensor_scalar(r_ei[:, 0, :], cnt, float(P - 1), None, ALU.add))
                chain(nc.vector.tensor_scalar(r_ei[:, 1, :], r_ei[:, 0, :], 7, None, ALU.logical_shift_right))
                chain(nc.vector.tensor_copy(tiles, r_ei[:, 1, :]))
                nc.vector.tensor_tensor_scan(tiles_to, one[:, 0:E], tiles, 0.0, ALU.mult, ALU.add)
                chain(nc.vector.tensor_tensor_scan(cnt_to, one[:, 0:E], cnt, 0.0, ALU.mult, ALU.add))
                nc.vector.tensor_tensor(r_a, tiles_to, tiles, ALU.subtract)
                chain(nc.vector.tensor_tensor(r_b, cnt_to, cnt, ALU.subtract))
                chain(nc.vector.scalar_tensor_tensor(off, r_a, float(P), r_b, ALU.mult, ALU.subtract))
                chain(nc.vector.tensor_tensor(r_scan[:], r_scan[:], r_tot[:], ALU.subtract))
                chain(nc.vector.tensor_tensor(r_scan[:], r_scan[:], over_t(off), ALU.add))
                chain(nc.vector.tensor_tensor(flat(r_scan[:]), flat(r_scan[:]), bank[3][:, 0:256], ALU.add))
                chain(nc.vector.tensor_tensor(r_scan[:], r_scan[:], r_one[:], ALU.mult))
                chain(nc.vector.tensor_reduce(dest, by_token(r_scan[:]), AX.X, ALU.add))
                chain(nc.vector.tensor_copy(r_ti[:, 0, :], dest))
                nc.vector.tensor_scalar(r_ti[:, 1, :], r_ti[:, 0, :], P - 1, None, ALU.bitwise_and)
                chain(nc.vector.tensor_scalar(r_ti[:, 2, :], r_ti[:, 0, :], 7, None, ALU.logical_shift_right))
                nc.vector.tensor_copy(lane, r_ti[:, 1, :])
                chain(nc.vector.tensor_copy(row, r_ti[:, 2, :]))
                with dve.Fori(0, 4) as i:
                    for r in range(8):
                        t = bass.ds(8 * i + r, 1)
                        nc.vector.tensor_scalar(lane_hot[:, t, :], iota_bf[:], lane[:, t], None, ALU.is_equal)
                ramp = cst[:, C_TILE:C_TILE + ROWS].unsqueeze(1).to_broadcast([P, T, ROWS])
                tcol = cst[:, C_TCOL:C_TCOL + T].unsqueeze(2).to_broadcast([P, T, ROWS])
                chain(nc.vector.tensor_tensor(tile_hot[:, 2], ramp, row.unsqueeze(2).to_broadcast([P, T, ROWS]), ALU.is_equal))
                nc.vector.tensor_tensor(tile_hot[:, 0], tile_hot[:, 2], tcol, ALU.mult)
                nc.vector.tensor_scalar(tile_hot[:, 1], tile_hot[:, 2], cst[:, C_P1:C_P1 + 1], None, ALU.mult).then_inc(s["hot_ready"], 1)
                ends = r_e[0:1, 2, :].unsqueeze(1).to_broadcast([1, ROWS, E])
                tile_no = cst[0:1, C_TILE:C_TILE + ROWS].unsqueeze(2).to_broadcast([1, ROWS, E])
                chain(nc.vector.tensor_tensor(expert_cmp[:], ends, tile_no, ALU.is_le))
                chain(nc.vector.tensor_reduce(expert_f[:], expert_cmp[:], AX.X, ALU.add))
                nc.vector.tensor_scalar(expert_of[:], expert_f[:], float(E - 1), None, ALU.min).then_inc(s["expert_ready"], 1)
                dve.wait_ge(s["inverted"], at["inverted"] + 1)
                chain(nc.vector.tensor_copy(inv[:], bank[2][:, 0:2 * ROWS]))
                token, pad = inv_v[:, 0, :], inv_v[:, 1, :]
                chain(nc.vector.scalar_tensor_tensor(token, inv[:, 0:ROWS], float(P), inv[:, ROWS:], ALU.mult, ALU.add))
                chain(nc.vector.tensor_scalar(pad, token, 0.0, float(NOWHERE), ALU.is_equal, ALU.mult))
                nc.vector.tensor_scalar(gather_row[:], token, -1.0, 0.0, ALU.add, ALU.max)
                nc.vector.scalar_tensor_tensor(scatter_row[:], token, -1.0, pad, ALU.add, ALU.add).then_inc(s["rows_ready"], 1)

                chains["f"] = chain.n

                def hidden(j, k):
                    dve.wait_ge(s["h_turned"], at["h_turned"] + j + 1)
                    nc.vector.tensor_copy(hidT[:, k % 2].rearrange("p c m -> p (c m)"), bank[4 + k % 2][:]).then_inc(s["hT_ready"], 1)

                def result(j, k, used):
                    dve.wait_ge(s["y_mm"], at["y_mm"] + j + 1)
                    if later(used):
                        dve.wait_ge(scattered[k % 3], at["scattered"][k % 3] + used)
                    nc.vector.tensor_copy(yg[:, k % 3, :], bank[6 + k % 2][:, 0:D]).then_inc(s["y_ready"], 1)

                def six(i):
                    for k in range(6):
                        hidden(6 * i + k + 1, k + 1)
                        result(6 * i + k, k, 16 * (2 * i + k // 3))

                hidden(0, 0)
                peeled(dve, 0, 6, six)
                for j in range(36, ROWS):
                    if j + 1 < ROWS:
                        hidden(j + 1, j + 1)
                    result(j, j, 16 * (j // 3))
                for q in range(4):
                    dve.wait_ge(back[q], at["back"][q] + 16)
                with dve.Fori(0, 4) as i:
                    for r in range(8):
                        t = bass.ds(8 * i + r, 1)
                        nc.vector.scalar_tensor_tensor(x[:, t, :], yback[:, t, :], prob[:, t], x[:, t, :],
                                                       ALU.mult, ALU.add).then_inc(x_done[n + 1], 1)

            def scalar(act):
                stats_scalar(act, s, at)
                with act.Fori(0, 4) as i:
                    for h in range(2):
                        act.wait_ge(s["turned"], at["turned"] + 8 * i + 4 * h + 4)
                        nc.scalar.copy(xT[:, h, :], bank[h][:]).then_inc(s["xT_ready"], 1)
                act.wait_ge(s["one_ready"], at["one_ready"] + 1)
                nc.scalar.activation(r_log[:], r_exp[:], ACT.Exp).then_inc(s["exp_ready"], 1)

                def tokens(j, k):
                    act.wait_ge(s["g_turned"], at["g_turned"] + j + 1)
                    nc.scalar.copy(xgT[:, k % 2, :], bank[k % 2][:, 0:P]).then_inc(s["xgT"], 1)

                def relu(j, k):
                    act.wait_ge(s["h_mm"], at["h_mm"] + j + 1)
                    nc.scalar.activation(hid[:, k % 2, :], bank[2 + k % 2][:], ACT.Relu).then_inc(s["h_relu"], 1)

                tokens(0, 0)
                with act.Fori(0, 6) as i:
                    for k in range(6):
                        tokens(6 * i + k + 1, k + 1)
                        relu(6 * i + k, k)
                for j in range(36, ROWS):
                    if j + 1 < ROWS:
                        tokens(j + 1, j + 1)
                    relu(j, j)

            def tensor(pe):
                if n == stages.index("f"):
                    pe.wait_ge(placed_w, 1)
                with pe.Fori(0, 4) as i:
                    for h in range(2):
                        for k in range(TB):
                            pe.wait_ge(s["normed"], at["normed"] + 8 * i + 4 * h + k + 1)
                            pe.transpose(bank[h][:, k * P:k * P + P], xh[:, 4 * h + k, :], ident).then_inc(s["turned"], 1)
                    for h in range(2):
                        pe.wait_ge(s["xT_ready"], at["xT_ready"] + 2 * i + h + 1)
                        for k in range(TB):
                            last = pe.matmul(bank[2][:, bass.ds((8 * i + 4 * h + k) * E, E)], xT[:, h, k * P:k * P + P],
                                             gateT[:], start=True, stop=True)
                        last.then_inc(s["gated"], 1)
                pe.wait_ge(bf_ready, 1)
                pe.wait_ge(s["one_ready"], at["one_ready"] + 1)
                one_hot = r_onebf[:].rearrange("p e t -> p (e t)")
                pe.matmul(bank[3][:, 0:256], tri[:], one_hot, start=True, stop=True)
                pe.matmul(bank[3][:, 256:512], ones_bf[:], one_hot, start=True, stop=True).then_inc(s["ranked"], 1)
                pe.wait_ge(s["hot_ready"], at["hot_ready"] + 1)
                pe.matmul(bank[2][:, 0:2 * ROWS], lane_hot[:, 0, :], tile_hot[:, 0:2, 0, :], start=True, stop=False)
                with pe.Fori(1, T - 1) as t:
                    pe.matmul(bank[2][:, 0:2 * ROWS], lane_hot[:, bass.ds(t, 1), :], tile_hot[:, 0:2, bass.ds(t, 1), :], start=False, stop=False)
                pe.matmul(bank[2][:, 0:2 * ROWS], lane_hot[:, T - 1, :], tile_hot[:, 0:2, T - 1, :], start=False, stop=True).then_inc(s["inverted"], 1)

                pe.wait_ge(s["rows_ready"], at["rows_ready"] + 1)
                pe.wait_ge(s["expert_ready"], at["expert_ready"] + 1)
                pe.wait_ge(w1_in, 16)
                pe.wait_ge(w2_in, 16)
                pe.wait_ge(biasrow_in, 16 * 6)

                def turn_in(j, k, have):
                    pe.wait_ge(gathered[k % AHEAD], at["gathered"][k % AHEAD] + have)
                    pe.transpose(bank[k % 2][:, 0:P], xg[:, k % AHEAD, :], ident).then_inc(s["g_turned"], 1)

                def up(j, k):
                    e = pe.value_load(expert_of[0:1, bass.ds(j, 1)], min_val=0, max_val=E - 1)
                    pe.wait_ge(s["xgT"], at["xgT"] + j + 1)
                    pe.matmul(bank[2 + k % 2][:], ones3[:], b1rows[:, bass.ds(e * F, F)], start=True, stop=False)
                    pe.matmul(bank[2 + k % 2][:], xgT[:, k % 2, :], w1[:, bass.ds(e, 1), :], start=False, stop=True).then_inc(s["h_mm"], 1)

                def turn_hidden(j, k):
                    pe.wait_ge(s["h_relu"], at["h_relu"] + j + 1)
                    for c in range(FC):
                        last = pe.transpose(bank[4 + k % 2][:, c * P:c * P + P], hid[:, k % 2, c * P:c * P + P], ident)
                    last.then_inc(s["h_turned"], 1)

                def down(j, k):
                    e = pe.value_load(expert_of[0:1, bass.ds(j, 1)], min_val=0, max_val=E - 1)
                    pe.wait_ge(s["hT_ready"], at["hT_ready"] + j + 1)
                    if later(j):
                        pe.wait_ge(s["y_ready"], at["y_ready"] + j)
                    pe.matmul(bank[6 + k % 2][:, 0:D], ones3[:], b2rows[:, bass.ds(e * D, D)], start=True, stop=False)
                    for c in range(FC):
                        last = pe.matmul(bank[6 + k % 2][:, 0:D], hidT[:, k % 2, c, :], w2[:, bass.ds(e, 1), c, :],
                                         start=False, stop=(c == FC - 1))
                    last.then_inc(s["y_mm"], 1)

                for j in range(3):
                    turn_in(j, j, 16)
                    if j >= 1:
                        up(j - 1, j - 1)
                    if j >= 2:
                        turn_hidden(j - 2, j - 2)

                def six(i):
                    for k in range(6):
                        turn_in(6 * i + k + 3, k + 3, 16 * (i + (k + 3) // AHEAD + 1))
                        up(6 * i + k + 2, k + 2)
                        turn_hidden(6 * i + k + 1, k + 1)
                        down(6 * i + k, k)

                peeled(pe, 0, 6, six)
                for j in range(ROWS, ROWS + 3):
                    if j - 1 < ROWS:
                        up(j - 1, j - 1)
                    if j - 2 < ROWS:
                        turn_hidden(j - 2, j - 2)
                    down(j - 3, j - 3)

            def gpsimd(pool):
                pool.wait_ge(s["rows_ready"], at["rows_ready"] + 1)
                for h in range(2):
                    pool.wait_ge(stored[h], at["stored"][h] + 16 * 4)

                def gather(j):
                    if j >= AHEAD:
                        pool.wait_ge(s["g_turned"], at["g_turned"] + j - AHEAD + 1)
                    pool.indirect_dma_start(xg[:, j % AHEAD, :], None, xhat_dram, bass.IndirectOffsetOnAxis(gather_row[:, j:j + 1], 0)).then_inc(gathered[j % AHEAD], 16)

                for j in range(AHEAD):
                    gather(j)
                for j in range(ROWS):
                    pool.wait_ge(s["y_ready"], at["y_ready"] + j + 1)
                    pool.indirect_dma_start(yrow_dram, bass.IndirectOffsetOnAxis(scatter_row[:, j:j + 1], 0), yg[:, j % 3, :], None,
                                            bounds_check=T * P - 1, oob_is_err=False).then_inc(scattered[j % 3], 16)
                    if j + AHEAD < ROWS:
                        gather(j + AHEAD)

            return dict(sync=sync, vector=vector, scalar=scalar, tensor=tensor, gpsimd=gpsimd)

        def scan(n):
            s = {k: sem(f"s{n}_{k}") for k in (
                "stat var sqrt v normed turned xT_ready u_mm u_kept ub_mm level_mm level_done d_added y_mm").split()}
            at = dict.fromkeys(s, 0)

            def vector(dve):
                chain = Chain(dve, s["v"])
                stats_vector(dve, chain, n, s, at)

                def normalise(i):
                    for r in range(8):
                        if r % 4 == 0 and later(i):
                            dve.wait_ge(s["turned"], 8 * i)
                        t = bass.ds(8 * i + r, 1)
                        nc.vector.tensor_scalar(xh[:, r, :], x[:, t, :], mean[:, t], rstd[:, t],
                                                ALU.subtract, ALU.mult).then_inc(s["normed"], 1)

                peeled(dve, 0, 4, normalise)
                for g in range(2):
                    dve.wait_ge(s["ub_mm"], g + 1)
                    nc.vector.tensor_copy(half(state, g), bank[4 + g][:]).then_inc(s["level_done"], 1)
                for l in range(LEVELS):
                    for g in range(2):
                        dve.wait_ge(s["level_mm"], 2 * l + g + 1)
                        dve.wait_ge(s["level_done"], 2 * l + g + 1)
                        nc.vector.tensor_tensor(half(state, g), half(state, g), bank[6 + g][:], ALU.add).then_inc(s["level_done"], 1)
                for b in range(B):
                    dve.wait_ge(s["y_mm"], b + 1)
                    dve.wait_ge(s["d_added"], b + 1)
                    tiles = x[:, TB * b:TB * b + TB, :].rearrange("p t d -> p (t d)")
                    nc.vector.tensor_tensor(tiles, tiles, bank[b % 4][:], ALU.add).then_inc(x_done[n + 1], TB)

            def half(v, g):
                return v[:, 4 * g:4 * g + 4, :].rearrange("p b c -> p (b c)")

            def gpsimd(pool):
                pool.wait_ge(scanw_in, 16 * (2 + 3 * NJ))
                with pool.Fori(0, B) as b:
                    pool.wait_ge(s["normed"], TB * b + TB)
                    tiles = x[:, bass.ds(TB * b, TB), :]
                    pool.tensor_tensor(tiles, tiles, d_rep[:].unsqueeze(1).to_broadcast([P, TB, D]), ALU.add).then_inc(s["d_added"], 1)

            def scalar(act):
                stats_scalar(act, s, at)
                with act.Fori(0, 4) as i:
                    for h in range(2):
                        act.wait_ge(s["turned"], 8 * i + 4 * h + 4)
                        nc.scalar.copy(xT[:, h, :], bank[h][:]).then_inc(s["xT_ready"], 1)
                act.wait_ge(scanw_in, 16 * (2 + 3 * NJ))
                for g in range(2):
                    act.wait_ge(s["u_mm"], 4 * g + 4)
                    nc.scalar.activation(half(u1, g), bank[2 + g][:], ACT.Identity, bias=b_in[:, 0:1]).then_inc(s["u_kept"], 1)

            def tensor(pe):
                for g in range(2):
                    with pe.Fori(0, 2) as i:
                        for h in range(2):
                            for k in range(TB):
                                pe.wait_ge(s["normed"], 16 * g + 8 * i + 4 * h + k + 1)
                                pe.transpose(bank[h][:, k * P:k * P + P], xh[:, 4 * h + k, :], ident).then_inc(s["turned"], 1)
                        for h in range(2):
                            pe.wait_ge(s["xT_ready"], 4 * g + 2 * i + h + 1)
                            for k in range(TB):
                                last = pe.matmul(bank[2 + g][:, bass.ds((2 * i + h) * P, P)], win_z[:, k, :],
                                                 xT[:, h, k * P:k * P + P], start=(k == 0), stop=(k == TB - 1))
                            last.then_inc(s["u_mm"], 1)
                for g in range(2):
                    pe.wait_ge(s["u_kept"], g + 1)
                    pe.matmul(bank[4 + g][:], bm_diag[:], half(u1, g), start=True, stop=True).then_inc(s["ub_mm"], 1)
                for l in range(LEVELS):
                    step = 1 << l
                    for g in range(2):
                        pe.wait_ge(s["level_done"], 2 * l + g + 1)
                        to = bank[6 + g][:].rearrange("p (b c) -> p b c", b=4)
                        h = state[:, 4 * g:4 * g + 4, :]
                        if step < P:
                            pe.matmul(to[:, :, step:], a_pow[:, l, 64:], h[:, :, 0:P - step], start=True, stop=True)
                            last = pe.matmul(to[:, :, 0:step], a_pow[:, l, 32:160], h[:, :, P - step:], start=True, stop=True)
                        else:
                            shift = N * step // P
                            last = pe.matmul(to, a_pow[:, l, 64 - shift:192 - shift], h, start=True, stop=True)
                        last.then_inc(s["level_mm"], 1)
                for b in range(B):
                    if b % 4 == 0:
                        pe.wait_ge(s["level_done"], 2 * LEVELS + b // 4 + 1)
                    if b >= 4:
                        pe.wait_ge(x_done[n + 1], TB * (b - 3))
                    pe.matmul(bank[b % 4][:], state[:, b, :], c_diag[:].rearrange("p j d -> p (j d)"), start=True, stop=True).then_inc(s["y_mm"], 1)

            return dict(sync=lambda sp: None, vector=vector, scalar=scalar, tensor=tensor, gpsimd=gpsimd)


        MIX_COUNTS = dict(stat=T, var=1, sqrt=1, v=0, centered=T, scaled=B, xn=B, squared=T, norm_sqrt=1, unit=T, turned=T,
                          xT_ready=B, logit_c=2 * B, logit_d=2 * B, max_c=2 * B, max_d=2 * B, exp_c=T, exp_d=2 * B,
                          turn_c0=B, turn_c1=B, turn_d0=B, turn_d1=B, kept_c0=B, kept_c1=B, kept_d0=B, kept_d1=B,
                          in_mm=B, in_kept=2 * B, in_turned=B, slotT=B, h_mm=MG, h_gelu=MG * MG, out_mm=4, out_kept=4,
                          y_mm=B, var2=1, sqrt2=1, weights=B, cleared=1)
        mix_sems = {k: sem(f"m_{k}") for k in MIX_COUNTS}
        MIXW = 16 * (5 + 2 * MG + ME)

        def mix_setup_vector(dve, chain):
            dve.wait_ge(mixw_in, MIXW)
            nc.vector.tensor_tensor(mu_t[:, 0], mu[:], mu[:], ALU.mult).then_inc(mix_set[0], 1)
            dve.wait_ge(mix_set[2], 1)
            chain(nc.vector.tensor_scalar(mu_t[:, 0], mu_t[:, 1], 1e-12, None, ALU.max))
            chain(nc.vector.reciprocal(mu_t[:, 1], mu_t[:, 0]))
            nc.vector.tensor_tensor(mu[:], mu[:], mu_t[:, 1], ALU.mult).then_inc(mix_set[3], 1)

        def mix(n):
            s, at = mix_sems, {k: v * stages[:n].count("m") for k, v in MIX_COUNTS.items()}

            def vector(dve):
                chain = Chain(dve, s["v"], chains["m"])
                if n == stages.index("m"):
                    if n:
                        dve.wait_ge(x_done[n], T)
                    mix_setup_vector(dve, chain)
                stats_vector(dve, chain, n, s, at)
                v2, sq = st[:, 2, :], st[:, 3, :]
                chain(nc.vector.tensor_tensor(v2, rstd, rstd, ALU.mult))
                chain(nc.vector.scalar_tensor_tensor(v2, st[:, 6, :], 1.0 / P, v2, ALU.mult, ALU.mult))
                nc.vector.tensor_scalar(sq, v2, EPS, None, ALU.add).then_inc(s["var2"], 1)
                dve.wait_ge(s["sqrt2"], at["sqrt2"] + 1)
                chain(nc.vector.reciprocal(v2, st[:, 4, :]))
                chain(nc.vector.tensor_tensor(rstd, rstd, v2, ALU.mult))
                with dve.Fori(0, 4) as i:
                    for r in range(8):
                        t = bass.ds(8 * i + r, 1)
                        nc.vector.tensor_scalar(xn[:, t, :], x[:, t, :], mean[:, t], rstd[:, t],
                                                ALU.subtract, ALU.mult).then_inc(s["centered"], 1)
                with dve.Fori(0, B) as b:
                    dve.wait_ge(s["scaled"], at["scaled"] + b + 1)
                    tiles = xn[:, bass.ds(TB * b, TB), :]
                    nc.vector.tensor_tensor(tiles, tiles, beta[:].unsqueeze(1).to_broadcast([P, TB, D]), ALU.add).then_inc(s["xn"], 1)
                norm, unit = st[:, 3, :], st[:, 4, :]
                dve.wait_ge(s["norm_sqrt"], at["norm_sqrt"] + 1)
                chain(nc.vector.tensor_scalar(norm, st[:, 2, :], 1e-12, None, ALU.max))
                chain(nc.vector.reciprocal(unit, norm))
                chain(nc.vector.tensor_scalar(unit, unit, mscale[:, 0:1], None, ALU.mult))

                def units(b, h):
                    for k in range(TB):
                        t = bass.ds(TB * b + k, 1)
                        nc.vector.tensor_scalar(xh[:, 4 * h + k, :], xn[:, t, :], unit[:, t], None, ALU.mult).then_inc(s["unit"], 1)

                def maxima(b):
                    for j in range(2):
                        dve.wait_ge(s["logit_c"], at["logit_c"] + 2 * b + j + 1)
                        nc.vector.tensor_reduce(neg_c[:, bass.ds(b, 1), 2 * j:2 * j + 2], bank[2 + j][:].rearrange("p (k s) -> p k s", k=2),
                                                AX.X, ALU.max, negate=True).then_inc(s["max_c"], 1)
                    for j in range(2):
                        dve.wait_ge(s["logit_d"], at["logit_d"] + 2 * b + j + 1)
                        nc.vector.tensor_reduce(neg_d[:, bass.ds(b, 1), j:j + 1], bank[4 + j][:], AX.X, ALU.max, negate=True).then_inc(s["max_d"], 1)

                def keep(b, h):
                    dve.wait_ge(s["turn_c1"], at["turn_c1"] + b + 1)
                    nc.vector.tensor_copy(combT[:, 1, bass.ds(b, 1), :], bank[7][:]).then_inc(s["kept_c1"], 1)
                    dve.wait_ge(s["turn_d1"], at["turn_d1"] + b + 1)
                    nc.vector.tensor_copy(disp[:, h, 2:4, :].rearrange("p k s -> p (k s)"), bank[7][:]).then_inc(s["kept_d1"], 1)
                    nc.vector.reciprocal(inv_d[:, bass.ds(b, 1), :], sum_d[:, bass.ds(b, 1), :]).then_inc(s["weights"], 1)
                    dve.wait_ge(s["in_mm"], at["in_mm"] + b + 1)
                    dve.wait_ge(s["weights"], at["weights"] + b + 1)
                    for j in range(2):
                        last = nc.vector.tensor_scalar(slot_in[:, j, :], bank[1][:, j * D:j * D + D], inv_d[:, bass.ds(b, 1), j:j + 1], None, ALU.mult)
                        last.then_inc(s["in_kept"], 1)

                units(0, 0)
                units(1, 1)
                maxima(0)
                with dve.Fori(0, 3) as i:
                    dve.wait_ge(s["turned"], at["turned"] + 8 * i + 4)
                    units(2 * i + 2, 0)
                    maxima(2 * i + 1)
                    keep(2 * i, 0)
                    dve.wait_ge(s["turned"], at["turned"] + 8 * i + 8)
                    units(2 * i + 3, 1)
                    maxima(2 * i + 2)
                    keep(2 * i + 1, 1)
                maxima(7)
                keep(6, 0)
                keep(7, 1)
                chain(nc.vector.reciprocal(inv_c[:], sum_c[:]))
                chain(nc.vector.tensor_scalar(inv_c[:], inv_c[:], 0.5, None, ALU.mult))
                chains["m"] = chain.n
                for h in range(2):
                    for j in range(2):
                        dve.wait_ge(s["out_mm"], at["out_mm"] + 2 * h + j + 1)
                        nc.vector.tensor_tensor(slot_out[:, h, 4 * j:4 * j + 4, :], bank[2 + 2 * h + j][:].rearrange("p (b d) -> p b d", b=4),
                                                mb2[:, h, :].unsqueeze(1).to_broadcast([P, 4, D]), ALU.add).then_inc(s["out_kept"], 1)
                for b in range(B):
                    dve.wait_ge(s["y_mm"], at["y_mm"] + b + 1)
                    for k in range(TB):
                        t = TB * b + k
                        nc.vector.scalar_tensor_tensor(x[:, t, :], bank[Y_BANK[b % 4]][:, k * D:k * D + D], inv_c[:, t:t + 1], x[:, t, :],
                                                       ALU.mult, ALU.add).then_inc(x_done[n + 1], 1)

            Y_BANK = (6, 7, 0, 1)

            def gpsimd(pool):
                pool.wait_ge(mixw_in, MIXW)
                if n:
                    pool.wait_ge(x_done[n], T)
                pool.memset(hid_diag[:], 0.0).then_inc(s["cleared"], 1)
                with pool.Fori(0, B) as b:
                    pool.wait_ge(s["centered"], at["centered"] + TB * b + TB)
                    tiles = xn[:, bass.ds(TB * b, TB), :]
                    pool.tensor_tensor(tiles, tiles, gamma[:].unsqueeze(1).to_broadcast([P, TB, D]), ALU.mult).then_inc(s["scaled"], 1)

            def scalar(act):
                if n == stages.index("m"):
                    act.wait_ge(mix_set[1], 1)
                    nc.scalar.activation(mu_t[:, 1], bank[0][:, 0:SLOTS], ACT.Sqrt).then_inc(mix_set[2], 1)
                stats_scalar(act, s, at)
                act.wait_ge(s["var2"], at["var2"] + 1)
                nc.scalar.activation(st[:, 4, :], st[:, 3, :], ACT.Sqrt).then_inc(s["sqrt2"], 1)

                def squares(b):
                    act.wait_ge(s["xn"], at["xn"] + b + 1)
                    for k in range(TB):
                        t = bass.ds(TB * b + k, 1)
                        if later(TB * b + k):
                            act.wait_ge(s["squared"], at["squared"] + TB * b + k)
                        nc.scalar.activation(square[:], xn[:, t, :], ACT.Square, accum_out=st[:, 9, t]).then_inc(s["squared"], 1)

                peeled(act, 0, B, squares)
                act.wait_ge(s["squared"], at["squared"] + T)
                nc.scalar.activation(st[:, 2, :], st[:, 9, :], ACT.Sqrt).then_inc(s["norm_sqrt"], 1)

                def first(b, h):
                    act.wait_ge(s["turned"], at["turned"] + TB * b + TB)
                    nc.scalar.copy(xT[:, h, :], bank[0][:]).then_inc(s["xT_ready"], 1)
                    for k in range(TB):
                        t = bass.ds(TB * b + k, 1)
                        act.wait_ge(s["max_c"], at["max_c"] + 2 * b + k // 2 + 1)
                        nc.scalar.activation(comb[:, h, k, :], bank[2 + k // 2][:, SLOTS * (k % 2):SLOTS * (k % 2) + SLOTS], ACT.Exp,
                                             bias=neg_c[:, bass.ds(b, 1), k:k + 1], accum_out=sum_c[:, t]).then_inc(s["exp_c"], 1)
                    for j in range(2):
                        act.wait_ge(s["max_d"], at["max_d"] + 2 * b + j + 1)
                        nc.scalar.activation(disp_s[:, h, j, :], bank[4 + j][:], ACT.Exp, bias=neg_d[:, bass.ds(b, 1), j:j + 1],
                                             accum_out=sum_d[:, bass.ds(b, 1), j:j + 1]).then_inc(s["exp_d"], 1)

                def second(b, h):
                    act.wait_ge(s["turn_c0"], at["turn_c0"] + b + 1)
                    nc.scalar.copy(combT[:, 0, bass.ds(b, 1), :], bank[6][:]).then_inc(s["kept_c0"], 1)
                    act.wait_ge(s["turn_d0"], at["turn_d0"] + b + 1)
                    nc.scalar.copy(disp[:, h, 0:2, :].rearrange("p k s -> p (k s)"), bank[6][:]).then_inc(s["kept_d0"], 1)
                    act.wait_ge(s["in_turned"], at["in_turned"] + b + 1)
                    nc.scalar.copy(slotT[:, :, bass.ds(b, 1), :], bank[0][:, 0:SLOTS].rearrange("p (e s) -> p e s", e=ME)).then_inc(s["slotT"], 1)

                first(0, 0)
                with act.Fori(0, 3) as i:
                    first(2 * i + 1, 1)
                    second(2 * i, 0)
                    first(2 * i + 2, 0)
                    second(2 * i + 1, 1)
                first(7, 1)
                second(6, 0)
                second(7, 1)
                act.wait_ge(s["cleared"], at["cleared"] + 1)
                for g in range(MG):
                    act.wait_ge(s["h_mm"], at["h_mm"] + g + 1)
                    for q in range(MG):
                        r = slice(MH * q, MH * q + MH)
                        nc.scalar.activation(hid_diag[r, g, :, q, :], bank[g % 2][r, 0:P].rearrange("p (b s) -> p b s", b=B), ACT.Gelu,
                                             bias=mb1[r, g:g + 1]).then_inc(s["h_gelu"], 1)

            def tensor(pe):
                if n == stages.index("m"):
                    pe.wait_ge(mix_set[0], 1)
                    pe.matmul(bank[0][:, 0:SLOTS], cst[:, C_ONE:C_ONE + P], mu_t[:, 0], start=True, stop=True).then_inc(mix_set[1], 1)
                    pe.wait_ge(mix_set[3], 1)

                def first(b, h, slotT_before):
                    if later(slotT_before):
                        pe.wait_ge(s["slotT"], at["slotT"] + slotT_before)
                    for k in range(TB):
                        pe.wait_ge(s["unit"], at["unit"] + TB * b + k + 1)
                        pe.transpose(bank[0][:, k * P:k * P + P], xh[:, 4 * h + k, :], ident).then_inc(s["turned"], 1)
                    pe.wait_ge(s["xT_ready"], at["xT_ready"] + b + 1)
                    if later(b):
                        pe.wait_ge(s["exp_c"], at["exp_c"] + TB * b)
                    for k in range(TB):
                        last = pe.matmul(bank[2 + k // 2][:, SLOTS * (k % 2):SLOTS * (k % 2) + SLOTS], xT[:, h, k * P:k * P + P], mu[:],
                                         start=True, stop=True)
                        if k % 2:
                            last.then_inc(s["logit_c"], 1)
                    if later(b):
                        pe.wait_ge(s["exp_d"], at["exp_d"] + 2 * b)
                    for j in range(2):
                        pe.matmul(bank[4 + j][:], mu[:, j * P:j * P + P], xT[:, h, :], start=True, stop=True).then_inc(s["logit_d"], 1)

                def second(b, h):
                    pe.wait_ge(s["exp_c"], at["exp_c"] + TB * b + TB)
                    for j in range(2):
                        for k in range(TB):
                            last = pe.transpose(bank[6 + j][:, k * P:k * P + P], comb[:, h, k, j * P:j * P + P], ident)
                        last.then_inc(s[f"turn_c{j}"], 1)
                    pe.wait_ge(s["exp_d"], at["exp_d"] + 2 * b + 2)
                    for m in range(2):
                        pe.wait_ge(s[f"kept_c{m}"], at[f"kept_c{m}"] + b + 1)
                        for k in range(2):
                            for j in range(2):
                                c = SLOTS * k + P * j
                                last = pe.transpose(bank[6 + m][:, c:c + P], disp_s[:, h, j, (2 * m + k) * P:(2 * m + k + 1) * P], ident)
                        last.then_inc(s[f"turn_d{m}"], 1)
                    for m in range(2):
                        pe.wait_ge(s[f"kept_d{m}"], at[f"kept_d{m}"] + b + 1)
                    for j in range(2):
                        for k in range(TB):
                            last = pe.matmul(bank[1][:, j * D:j * D + D], disp[:, h, k, j * P:j * P + P], xn[:, bass.ds(TB * b + k, 1), :],
                                             start=(k == 0), stop=(k == TB - 1))
                    last.then_inc(s["in_mm"], 1)
                    pe.wait_ge(s["in_kept"], at["in_kept"] + 2 * b + 2)
                    for j in range(2):
                        last = pe.transpose(bank[0][:, j * P:j * P + P], slot_in[:, j, :], ident)
                    last.then_inc(s["in_turned"], 1)

                def pair(i):
                    first(2 * i + 1, 1, 2 * i)
                    second(2 * i, 0)
                    first(2 * i + 2, 0, 2 * i + 1)
                    second(2 * i + 1, 1)

                first(0, 0, 0)
                peeled(pe, 0, 3, pair)
                first(7, 1, 6)
                second(6, 0)
                second(7, 1)
                pe.wait_ge(s["slotT"], at["slotT"] + B)
                pe.wait_ge(mixw_in, MIXW)
                for g in range(MG):
                    if g >= 2:
                        pe.wait_ge(s["h_gelu"], at["h_gelu"] + MG * (g - 1))
                    for q in range(MG):
                        last = pe.matmul(bank[g % 2][MH * q:MH * q + MH, 0:P], mw1[:, MG * g + q, :],
                                         slotT[:, MG * g + q].rearrange("p b s -> p (b s)"), start=True, stop=True)
                    last.then_inc(s["h_mm"], 1)
                for h in range(2):
                    pe.wait_ge(s["h_gelu"], at["h_gelu"] + MG * (2 * h + 2))
                    for j in range(2):
                        for b in range(4 * j, 4 * j + 4):
                            for g in (2 * h, 2 * h + 1):
                                r = 64 * (g % 2)
                                last = pe.matmul(bank[2 + 2 * h + j][r:r + 64, (b % 4) * D:(b % 4) * D + D],
                                                 hid_diag[:, g, b].rearrange("p q s -> p (q s)"), mw2[:, g, :], start=True, stop=True)
                        last.then_inc(s["out_mm"], 1)
                pe.wait_ge(s["out_kept"], at["out_kept"] + 4)
                for b in range(B):
                    if b >= 4:
                        pe.wait_ge(x_done[n + 1], TB * (b - 3))
                    for k in range(TB):
                        for j in range(2):
                            last = pe.matmul(bank[Y_BANK[b % 4]][:, k * D:k * D + D], combT[:, j, b, k * P:k * P + P], slot_out[:, j, b, :],
                                             start=(j == 0), stop=(j == 1))
                    last.then_inc(s["y_mm"], 1)

            return dict(sync=lambda sp: None, vector=vector, scalar=scalar, tensor=tensor, gpsimd=gpsimd)


        def attention(n):
            s = {k: sem(f"a{n}_{k}") for k in (
                "stat var sqrt v normed misc_mm misc_read rope_v parts max_mm max_read exp_mm "
                "prob values sums_mm sums_read m_cut m_rows den set_ones rope_read tick".split())}
            stack_in = [sem(f"a{n}_stack_in{i}") for i in range(2)]
            m_in = [sem(f"a{n}_m_in{i}") for i in range(2)]
            at = dict.fromkeys(s, 0)
            HALF = H // 2

            STEPS = ((0, "xt"), (1, "m1"), (2, "p0"), (3, "p1"), (4, "p2"), (5, "p3"), (7, "n0"), (8, "n1"), (9, "m0"),
                     (10, "n2"), (11, "n3"), (12, "to"), (13, "wo"), (15, "v"))
            RANGE = {"x": (-1, B - 2), "p": (-1, B - 2), "m1": (1, B), "m0": (0, B - 1), "n": (2, B + 1), "t": (2, B + 1),
                     "w": (2, B + 1), "v": (0, B - 1)}

            def active(i, step):
                if not isinstance(i, int):
                    return True
                lo, hi = RANGE[step if step in RANGE else step[0]]
                return lo <= i <= hi

            before = {}
            count = 0
            for i in range(-1, B + 2):
                before[i] = count
                count += sum(active(i, step) for _, step in STEPS)

            def uses_before(i):
                return before[i] if isinstance(i, int) else before[2] + len(STEPS) * (i - 2)

            def odd_jobs(i, hh):
                base = uses_before(i)
                for k, (slot, step) in enumerate(st for st in STEPS if active(i, st[1])):
                    if slot == hh:
                        yield step, base + k

            def maxing(i):
                return not isinstance(i, int) or 0 <= i < B

            def exping(i):
                return not isinstance(i, int) or 1 <= i <= B

            def groups(i, hh):
                if hh % 4 == 1:
                    g = hh // 4 - 1
                    b = i - 1
                    if g < 0:
                        g, b = 3, i - 2
                    if not isinstance(i, int) or 0 <= b < B:
                        yield b, g, 4 * b + g

            UNITS = {}
            for hh in range(H):
                UNITS[hh] = [("a", hh, hh + hh // 2)]
                if hh % 2:
                    UNITS[hh].append(("b", hh, hh + hh // 2 + 1))
            N_UNITS = H + H // 2

            def turns(engine, body):
                for i in (-1, 0, 1):
                    body(i, i % 2)
                with engine.Fori(1, 3) as r:
                    for par in range(2):
                        body(2 * r + par, par)
                for i in range(6, B + 2):
                    body(i, i % 2)

            def tensor(pe):
                pe.wait_ge(att_w, 1)

                def step_(i, par, step, m):
                    nxt = 1 - par
                    to = bank[7]
                    if m is not None and not (isinstance(m, int) and m == 0):
                        pe.wait_ge(s["misc_read"], m)
                    if step == "xt":
                        for k in range(TB):
                            pe.wait_ge(s["normed"], TB * (i + 1) + k + 1)
                            last = pe.transpose(to[:, k * P:k * P + P], xh[:, 4 * nxt + k, :], ident)
                    elif step[0] == "p":
                        last = pe.matmul(to[:], wqk[:, int(step[1]), :], xT[:, nxt, :], start=True, stop=True)
                    elif step == "v":
                        for k in range(TB):
                            last = pe.matmul(to[:, k * P:k * P + P], xT[:, par, k * P:k * P + P], wqkv[:, 2 * D:], start=True, stop=True)
                    elif step[0] == "m":
                        half = int(step[1])
                        pe.wait_ge(s["m_cut"], 2 * i + 1 if half == 0 else 2 * i)
                        for k in range(TB):
                            last = pe.transpose(to[0:3 * HALF, :].bitcast(BF16)[:, k * P:k * P + P],
                                                m_cut[:, half, k].rearrange("p c h -> p (c h)"), ident_bf[:])
                    elif step[0] == "n":
                        pe.wait_ge(s["sums_read"], TB * (i - 1))
                        k = int(step[1])
                        for g in range(TB):
                            last = pe.transpose(to[:, g * P:g * P + P], o_t[par][:, g, k * P:k * P + P], ident)
                    elif step == "to":
                        for k in range(TB):
                            last = pe.transpose(to[:, k * P:k * P + P], o_tok[:, k, :], ident)
                    elif step == "wo":
                        for k in range(TB):
                            last = pe.matmul(to[:, k * P:k * P + P], o_hd[:, k * P:k * P + P], wout[:], start=True, stop=True)
                    last.then_inc(s["misc_mm"], 1)

                def maxima(i, par, hh):
                    half = hh // HALF
                    if hh % HALF == 0:
                        pe.wait_ge(stack_in[half], 16 * 2 * len(Q_PART) * (i + 1))
                    for unit, blocks in enumerate(((3,), (2, 0), (1,))):
                        number = 3 * (H * i + hh) + unit
                        to = bank[number % 2 if isinstance(i, int) else (3 * hh + unit) % 2]
                        if not (isinstance(i, int) and number < 2):
                            pe.wait_ge(s["max_read"], number - 1)
                        for col, k in zip((0, 3 * P), blocks):
                            n_keys = (k + 1) * P
                            pe.matmul(to[:, col:col + n_keys], q_stack[par][0:STACK, hh, k * P:k * P + P], k_stack[par][0:STACK, hh, 0:n_keys],
                                      start=True, stop=False)
                            last = pe.matmul(to[:, col + k * P:col + n_keys], ident_bf[:], mask_q[:], start=False, stop=True)
                        last.then_inc(s["max_mm"], 1)

                def exponents(i, par, hh):
                    prev = 1 - par
                    rows = STACK + 3
                    if hh % HALF == 0:
                        pe.wait_ge(m_in[hh // HALF], 16 * i)
                    for kind, h, u in UNITS[hh]:
                        number = N_UNITS * (i - 1) + u
                        b0 = 2 + 2 * (u % 2)
                        if not (isinstance(i, int) and number < 2):
                            pe.wait_ge(s["prob"], number - 1)
                        for head, k, to in (((h, 0, bank[b0][:]), (h, 1, bank[b0 + 1][:, 0:3 * P]), (h, 3, bank[b0 + 1][:, 3 * P:])) if kind == "a"
                                            else ((h - 1, 2, bank[b0][:, 0:2 * P]), (h, 2, bank[b0][:, 2 * P:]))):
                            pe.matmul(to, k_stack[prev][0:rows, head, k * P:k * P + P], q_stack[prev][0:rows, head, k * P:], start=True, stop=False)
                            last = pe.matmul(to[:, 0:P], ident_bf[:], mask_k[:], start=False, stop=True)
                        last.then_inc(s["exp_mm"], 1)

                def sums(b, g, number, vpar):
                    pe.wait_ge(s["prob"], N_UNITS * b + 6 * g + 6)
                    pe.wait_ge(s["values"], b + 1)
                    if later(number):
                        pe.wait_ge(s["sums_read"], number)
                    for k in range(TB):
                        for j in range(4):
                            last = pe.matmul(bank[6][32 * j:32 * j + 32, k * P:], v_aug[vpar][:, k, 4 * g + j, :],
                                             prob_e[g % 2][:, j, E_AT[k]:E_AT[k] + S - k * P], start=(k == 0), stop=(k == TB - 1))
                    last.then_inc(s["sums_mm"], 1)

                def body(i, par):
                    for hh in range(H):
                        if maxing(i):
                            maxima(i, par, hh)
                        if exping(i):
                            exponents(i, par, hh)
                        for b, g, number in groups(i, hh):
                            sums(b, g, number, par if g == 3 else 1 - par)
                        for step, m in odd_jobs(i, hh):
                            step_(i, par, step, m)

                turns(pe, body)

            def vector(dve):
                chain = Chain(dve, s["v"])
                if n == stages.index("a"):
                    dve.wait_ge(attw_in, 48)
                    nc.vector.tensor_copy(ident_bf[:], ident)
                    nc.vector.tensor_copy(mask_q[:], rot[:, R_MQ:R_MQ + P])
                    nc.vector.tensor_copy(mask_k[:], rot[:, R_MK:R_MK + P])
                    for m in range(2):
                        w = wqkv[:, m * D:m * D + D].rearrange("p (a h d) -> p a d h", a=2, d=DH)
                        to = [wqk[:, 2 * m + r, :].rearrange("p (a d h) -> p a d h", a=2, d=DH) for r in range(2)]
                        lo, hi = slice(0, DH // 2), slice(DH // 2, DH)
                        for half in range(2):
                            nc.vector.tensor_copy(to[0][:, half], w[:, half])
                            nc.vector.tensor_scalar(to[1][:, half, lo], w[:, half, hi], -1.0, None, ALU.mult)
                            last = nc.vector.tensor_copy(to[1][:, half, hi], w[:, half, lo])
                    last.then_inc(att_w, 1)
                stats_vector(dve, chain, n, s, at)

                def body(i, par):
                    nxt = 1 - par
                    for hh in range(H):
                        if hh == 0 and active(i, "xt"):
                            if not (isinstance(i, int) and i < 1):
                                dve.wait_ge(s["misc_mm"], uses_before(i) - 1)
                            for k in range(TB):
                                t = bass.ds(TB * (i + 1) + k, 1)
                                nc.vector.tensor_scalar(xh[:, 4 * nxt + k, :], x[:, t, :], mean[:, t], rstd[:, t],
                                                        ALU.subtract, ALU.mult).then_inc(s["normed"], 1)
                        if maxing(i):
                            for unit, blocks in enumerate(((3,), (2, 0), (1,))):
                                number = 3 * (H * i + hh) + unit
                                frm = bank[number % 2 if isinstance(i, int) else (3 * hh + unit) % 2]
                                dve.wait_ge(s["max_mm"], number + 1)
                                for col, k in zip((0, 3 * P), blocks):
                                    last = nc.vector.tensor_reduce(neg_m[:, par, k, hh:hh + 1], frm[:, col:col + (k + 1) * P], AX.X, ALU.max, negate=True)
                                last.then_inc(s["max_read"], 1)
                            if hh % HALF == HALF - 1:
                                half = hh // HALF
                                dve.wait_ge(s["max_read"], 3 * (H * i + hh) + 3)
                                v = neg_m[:, par, :, HALF * half:HALF * half + HALF]
                                c = [m_cut[:, half, :, r, :] for r in range(3)]
                                for op in ((c[0], v), (m_left[:], v, c[0]), (c[1], m_left[:]), (c[2], m_left[:], c[1])):
                                    if len(op) == 2:
                                        ins = nc.vector.tensor_copy(*op)
                                    else:
                                        ins = nc.vector.tensor_tensor(*op, ALU.subtract)
                                    last = ins.then_inc(s["den"], 1)
                                    den_count[0] += 1
                                    dve.wait_ge(s["den"], den_at(i))
                                dve.sem_inc(s["m_cut"], 1)
                        for step, m in odd_jobs(i, hh):
                            if step[0] == "m":
                                half = int(step[1])
                                dve.wait_ge(s["misc_mm"], m + 1)
                                prior = (i - 1 if half else i)
                                if not (isinstance(prior, int) and prior < 1):
                                    dve.wait_ge(m_in[half], 16 * prior)
                                nc.vector.tensor_copy(m_rows[:, half, :], bank[7][0:3 * HALF, :].bitcast(BF16)[:, 0:S]).then_inc(s["m_rows"], 1)
                                dve.wait_ge(s["m_rows"], rows_count(i, half))
                                dve.sem_inc(s["misc_read"], 1)
                            elif step[0] == "n":
                                k = int(step[1])
                                dve.wait_ge(s["misc_mm"], m + 1)
                                got = bank[7][:].rearrange("p (h c) -> p h c", c=32)
                                nc.vector.reciprocal(o_den[:], got[:, :, DH]).then_inc(s["den"], 1)
                                den_count[0] += 1
                                dve.wait_ge(s["den"], den_at(i))
                                nc.vector.tensor_tensor(o_tok[:, k, :].rearrange("p (h c) -> p h c", c=DH), got[:, :, 0:DH],
                                                        o_den[:].unsqueeze(2).to_broadcast([P, H, DH]), ALU.mult).then_inc(s["misc_read"], 1)
                            elif step == "wo":
                                dve.wait_ge(s["misc_mm"], m + 1)
                                tiles = x[:, bass.ds(TB * (i - 2), TB), :]
                                nc.vector.tensor_tensor(tiles, tiles, bank[7][:].rearrange("p (k d) -> p k d", k=TB), ALU.add).then_inc(x_done[n + 1], TB)
                                dve.wait_ge(x_done[n + 1], TB * (i - 1))
                                dve.sem_inc(s["misc_read"], 1)

                den_count = [0]
                den_base = {}

                def den_at(i):
                    if isinstance(i, int):
                        return den_count[0]
                    return den_count[0] + 24 * (i // 2 - 1) if False else den_loop(i)

                def den_loop(i):
                    return loop_den[0] + den_count[0] - loop_den[1]

                def rows_count(i, half):
                    return 2 * i if half else 2 * i + 1

                loop_den = [0, 0]

                def turns_v():
                    for i in (-1, 0, 1):
                        body(i, i % 2)
                    with dve.Fori(1, 3) as r:
                        loop_den[1] = den_count[0]
                        loop_den[0] = den_count[0] + 24 * (r - 1)
                        for par in range(2):
                            body(2 * r + par, par)
                        assert den_count[0] - loop_den[1] == 24
                    den_count[0] += 24
                    for i in range(6, B + 2):
                        body(i, i % 2)

                turns_v()

            def scalar(act):
                stats_scalar(act, s, at)

                def body(i, par):
                    nxt = 1 - par
                    for hh in range(H):
                        if exping(i):
                            for kind, h, u in UNITS[hh]:
                                number = N_UNITS * (i - 1) + u
                                b0 = 2 + 2 * (u % 2)
                                g = hh // 4
                                if hh % 4 == 0 and kind == "a" and not (isinstance(i, int) and 4 * (i - 1) + g - 1 < 1):
                                    act.wait_ge(s["sums_mm"], 4 * (i - 1) + g - 1)
                                act.wait_ge(s["exp_mm"], number + 1)
                                if kind == "a":
                                    frm = psum_pair[u % 2]
                                    to = prob_e[g % 2][:, h % 4, 0:2 * S]
                                else:
                                    frm = bank[b0][:].rearrange("p (h c) -> p h c", h=2)
                                    to = prob_e[g % 2][:, h % 4 - 1:h % 4 + 1, E_AT[2]:E_AT[2] + 2 * P]
                                nc.scalar.activation(to, frm, ACT.Exp, scale=DH ** -0.5).then_inc(s["prob"], 1)
                        for b, g, number in groups(i, hh):
                            vpar = par if g == 3 else 1 - par
                            act.wait_ge(s["sums_mm"], number + 1)
                            nc.scalar.copy(o_t[vpar][:, g, :], bank[6][:]).then_inc(s["sums_read"], 1)
                        for step, m in odd_jobs(i, hh):
                            if step == "xt":
                                act.wait_ge(s["misc_mm"], m + 1)
                                nc.scalar.copy(xT[:, nxt, :], bank[7][:]).then_inc(s["misc_read"], 1)
                            elif step[0] == "p":
                                r = int(step[1])
                                act.wait_ge(s["misc_mm"], m + 1)
                                if r >= 2 or not (isinstance(i, int) and i < 0):
                                    act.wait_ge(s["rope_read"], 2 * (i + 1) + r // 2)
                                nc.scalar.copy(raw[:, r % 2, :], bank[7][:]).then_inc(s["misc_read"], 1)
                            elif step == "v":
                                act.wait_ge(s["misc_mm"], m + 1)
                                act.wait_ge(s["set_ones"], 1)
                                nc.scalar.copy(v_aug[par][:, :, :, 0:DH], bank[7][:].rearrange("p (k h d) -> p k h d", k=TB, h=H)).then_inc(s["values"], 1)
                                act.wait_ge(s["values"], i + 1)
                                act.sem_inc(s["misc_read"], 1)
                            elif step == "to":
                                act.wait_ge(s["misc_mm"], m + 1)
                                nc.scalar.copy(o_hd[:], bank[7][:]).then_inc(s["misc_read"], 1)

                turns(act, body)

            def gpsimd(pool):
                if n:
                    pool.wait_ge(x_done[n], T)
                pool.wait_ge(zeroed, 2)
                setup = Chain(pool, s["rope_v"])
                for i in range(2):
                    setup(pool.memset(k_stack[i][32:64].rearrange("p h t -> p (h t)").bitcast(F32), ONE_ONE))
                    setup(pool.memset(v_aug[i][:], 0.0))
                    setup(pool.memset(v_aug[i][:, :, :, DH:DH + 1], 1.0))
                pool.sem_inc(s["set_ones"], 1)
                pool.wait_ge(attw_in, 48)
                t0, t1 = rope[:, 0, :], rope[:, 1, :]

                def rotate(b):
                    for m in range(2):
                        part = [cut[:, m, r, :] for r in range(3)]
                        done = 14 * b + 7 * m + 2
                        first = uses_before(b - 1)
                        off = [k for k, st in enumerate(x for x in STEPS if active(b - 1, x[1])) if st[1] == f"p{2 * m + 1}"][0]
                        pool.wait_ge(s["misc_read"], first + off + 1)
                        pool.tensor_tensor(t0, raw[:, 0, :], cos, ALU.mult).then_inc(s["rope_v"], 1)
                        pool.tensor_tensor(t1, raw[:, 1, :], sin, ALU.mult).then_inc(s["rope_v"], 1)
                        pool.wait_ge(s["rope_v"], setup.n + done)
                        pool.sem_inc(s["rope_read"], 1)
                        pool.tensor_tensor(t0, t0, t1, ALU.add).then_inc(s["rope_v"], 1)
                        pool.wait_ge(s["rope_v"], setup.n + done + 1)
                        if m == 0 and not (isinstance(b, int) and b < 1):
                            for half in range(2):
                                pool.wait_ge(stack_in[half], 16 * 2 * len(Q_PART) * b)
                        pool.sem_inc(s["tick"], 1)
                        pool.tensor_copy(part[0], t0).then_inc(s["rope_v"], 1)
                        pool.wait_ge(s["rope_v"], setup.n + done + 2)
                        pool.tensor_tensor(t1, t0, part[0], ALU.subtract).then_inc(s["rope_v"], 1)
                        pool.wait_ge(s["rope_v"], setup.n + done + 3)
                        pool.sem_inc(s["tick"], 1)
                        pool.tensor_copy(part[1], t1).then_inc(s["rope_v"], 1)
                        pool.wait_ge(s["rope_v"], setup.n + done + 4)
                        pool.tensor_tensor(part[2], t1, part[1], ALU.subtract).then_inc(s["rope_v"], 1)
                        pool.wait_ge(s["rope_v"], setup.n + done + 5)
                    pool.sem_inc(s["parts"], 1)

                for b in range(3):
                    rotate(b)
                with pool.Fori(3, 7) as b:
                    rotate(b)
                rotate(7)

            def sync(sp):
                sp.wait_ge(s["set_ones"], 1)

                def maximum(b, par, half):
                    sp.wait_ge(s["m_rows"], 2 * b + 1 + half)
                    sp.dma_start(q_stack[par][STACK:STACK + 3, HALF * half:HALF * half + HALF, :], m_rows[:, half, :]).then_inc(m_in[half], 16)

                def stack(b, par, half):
                    if half == 0:
                        sp.wait_ge(s["parts"], b + 1)
                    if not (isinstance(b, int) and b < 2):
                        sp.wait_ge(s["exp_mm"], N_UNITS * (b - 2) + N_UNITS // 2 * (half + 1))
                    for r in range(len(Q_PART)):
                        for m, to, part in ((0, q_stack, Q_PART), (1, k_stack, K_PART)):
                            sp.dma_start(to[par][DH * r:DH * r + DH, HALF * half:HALF * half + HALF, :],
                                         cut[64 * half:64 * half + 64, m, part[r], :]).then_inc(stack_in[half], 16)

                def body(i, par):
                    if not isinstance(i, int) or 1 <= i <= B:
                        maximum(i - 1, 1 - par, 1)
                    if maxing(i):
                        maximum(i, par, 0)
                    if active(i, "xt"):
                        for half in range(2):
                            stack(i + 1, 1 - par, half)

                turns(sp, body)

            return dict(sync=sync, vector=vector, scalar=scalar, tensor=tensor, gpsimd=gpsimd)

        kinds = {"f": ffn, "s": scan, "m": mix, "a": attention}
        parts = [kinds[k](n) for n, k in enumerate(stages)]
        block = ctx.enter_context(nc.Block())

        @block.sync
        def _(sp):
            load_sync(sp)
            for part in parts:
                part["sync"](sp)
            sp.wait_ge(x_done[len(stages)], T)
            sp.dma_start(out.rearrange("b (k p) d -> p (b k) d", p=P), x[:]).then_inc(stored_out, 16)
            sp.wait_ge(stored_out, 16)

        @block.scalar
        def _(act):
            load_scalar(act)
            for part in parts:
                part["scalar"](act)

        @block.vector
        def _(dve):
            setup_vector(dve, Chain(dve, sem("setup_v")))
            for part in parts:
                part["vector"](dve)

        @block.gpsimd
        def _(pool):
            setup_gpsimd(pool)
            for part in parts:
                part["gpsimd"](pool)

        @block.tensor
        def _(pe):
            setup_tensor(pe)
            for part in parts:
                part["tensor"](pe)


STAGES = "fsfmam"


def kernel(**inputs):
    import concourse.bacc as bacc
    from concourse.bass_utils import run_bass_kernel_spmd

    nc = bacc.Bacc("TRN2", target_bir_lowering=False, num_devices=1)
    arrays = {f"in_{k}": np.ascontiguousarray(v) for k, v in inputs.items()}
    arrays["in_consts"] = shape_constants()
    arrays["in_rotary"] = rotary_constants()
    ap = {k: nc.dram_tensor(k, v.shape, F32, kind="ExternalInput").ap() for k, v in arrays.items()}
    out = nc.dram_tensor("out", (B, S, D), F32, kind="ExternalOutput").ap()
    xhat_dram = nc.dram_tensor("xhat_rows", (B * S, D), F32).ap()
    yrow_dram = nc.dram_tensor("result_rows", (B * S, D), F32).ap()
    build(nc, {k[3:]: v for k, v in ap.items()}, ap["in_consts"], ap["in_rotary"], out, xhat_dram, yrow_dram, STAGES)
    return run_bass_kernel_spmd(nc, [arrays], core_ids=[0]).results[0]["out"]
```

```python
from contextlib import ExitStack

import concourse.bass as bass
import numpy as np
from concourse import mybir

F32 = mybir.dt.float32
BF16 = mybir.dt.bfloat16
I32 = mybir.dt.int32
ALU = mybir.AluOpType
ACT = mybir.ActivationFunctionType
AX = mybir.AxisListType

P = 128
B, S, D = 8, 512, 128
T = B * S // P
TB = S // P
N = 32
NJ = P // N
LEVELS = 9
E, F = 8, 512
FC = F // P
ROWS = T + E - 1
ME, MS, MH = 16, 16, 32
SLOTS = ME * MS
MG = P // MH
H, DH = 16, 8
Q_PART, K_PART = (0, 0, 1, 0, 2, 1), (0, 1, 0, 2, 0, 1)
STACK = DH * len(Q_PART)
E_AT = (0, 512, 1024, 896)
E_LEN = 1280
BIG = 1e30
ONE_ONE = float(np.array([0x3F803F80], np.uint32).view(np.float32)[0])
AHEAD = 6
NOWHERE = 8192
EPS = 1e-5

C_ID, C_EM, C_TILE, C_TCOL, C_P1, C_TRI, C_IOTA, C_ONE = 0, 128, 384, 423, 455, 456, 584, 712
C_ALL = C_ONE + 256
R_COS, R_SIN, R_MQ, R_MK, R_ALL = 0, S, 2 * S, 2 * S + P, 2 * S + 2 * P


def shape_constants():
    c = np.zeros((P, C_ALL), np.float32)
    p = np.arange(P)
    c[:, C_ID:C_ID + P] = np.eye(P)
    c[:, C_EM:C_EM + E * T] = np.repeat(np.arange(E) - E, T)
    c[:, C_TILE:C_TILE + ROWS] = np.arange(ROWS)
    c[:, C_TCOL:C_TCOL + T] = np.arange(T)
    c[:, C_P1] = p + 1
    c[:, C_TRI:C_TRI + P] = p[:, None] < p[None, :]
    c[:, C_IOTA:C_IOTA + P] = p
    c[:, C_ONE:C_ONE + 256] = 1.0
    return c


def rotary_constants():
    c = np.zeros((P, R_ALL), np.float32)
    inv_freq = (1.0 / np.float32(10000.0) ** (np.arange(0, DH, 2, dtype=np.float32) / DH)).astype(np.float32)
    freqs = np.arange(S, dtype=np.float32)[None, :] * inv_freq[:, None]
    dim = (np.arange(P) // (H // 2)) % DH % (DH // 2)
    c[:, R_COS:R_COS + S] = np.cos(freqs)[dim]
    c[:, R_SIN:R_SIN + S] = np.sin(freqs)[dim]
    p = np.arange(P)
    c[:, R_MQ:R_MQ + P] = np.where(p[None, :] > p[:, None], -BIG, 0)
    c[:, R_MK:R_MK + P] = np.where(p[:, None] > p[None, :], -BIG, 0)
    return c


def later(i):
    return not isinstance(i, int) or i > 0


def peeled(engine, start, stop, body):
    body(start)
    with engine.Fori(start + 1, stop) as i:
        body(i)


class Chain:

    def __init__(self, engine, sem, n=0):
        self.engine, self.sem, self.n = engine, sem, n

    def mark(self, instruction):
        instruction.then_inc(self.sem, 1)
        self.n += 1

    def sync(self):
        self.engine.wait_ge(self.sem, self.n)

    def __call__(self, instruction):
        self.mark(instruction)
        self.sync()


def build(nc, a, consts, rotary, out, xhat_dram, yrow_dram, stages="fsf"):
    ctx = ExitStack()
    with ctx:
        def sb(name, shape, dt=F32):
            return ctx.enter_context(nc.sbuf_tensor(name, shape, dt))

        def sem(name):
            return ctx.enter_context(nc.semaphore(name))

        psum = ctx.enter_context(nc.psum_tensor("psum", [P, 8 * 512], F32))
        bank = [psum[:, 512 * i:512 * i + 512] for i in range(8)]
        psum_pair = [psum[:, 1024 * i + 1024:1024 * i + 2048] for i in range(2)]

        x = sb("x", [P, T, D])
        cst = sb("cst", [P, C_ALL])
        ident = cst[:, C_ID:C_ID + P]
        tri = sb("tri", [P, P], BF16)
        ones_bf = sb("ones_bf", [P, P], BF16)
        iota_bf = sb("iota_bf", [P, P], BF16)
        half_stats = sb("half_stats", [P, T, 6])
        st = sb("st", [P, 10, T])
        mean, rstd, shift_by = st[:, 0, :], st[:, 1, :], st[:, 9, :]
        xh = sb("xh", [P, 8, D])
        xT = sb("xT", [P, 2, S])

        arena = sb("arena", [P, 2 * B * S])

        arena2 = sb("arena2", [P, 10752])
        arena3 = sb("arena3", [P, 2 * TB * E_LEN])
        arena4 = sb("arena4", [P, 8192])

        def carve(area, at, shape, dt=F32):
            n = int(np.prod(shape)) * (2 if dt == BF16 else 4) // 4
            v = area[:, at:at + n]
            if dt != F32:
                v = v.bitcast(dt)
            names = "abcde"[:len(shape)]
            return v.rearrange(f"p ({' '.join(names)}) -> p {' '.join(names)}", **dict(zip(names[1:], shape[1:]))) if len(shape) > 1 else v

        w1 = arena2[:, 0:4096].rearrange("p (e f) -> p e f", e=E)
        w2 = arena2[:, 4096:8192].rearrange("p (e c d) -> p e c d", e=E, c=FC)
        b1rows = arena2[:, 8192:10240].bitcast(BF16)
        b2rows = arena2[:, 10240:10752].bitcast(BF16)
        ones3 = sb("ones3", [P, P], BF16)
        bsplit = carve(arena4, 6100, (2, 2, 32))
        bparts = carve(arena4, 6228, (2, 3, 32), BF16)
        gateT = sb("gateT", [P, E])
        gate_rows = arena4[0:E, 6400:6400 + D]
        r_log = carve(arena4, 0, (E, T))
        r_exp = carve(arena4, 256, (E, T))
        r_eq = carve(arena4, 512, (E, T))
        r_one = carve(arena4, 768, (E, T))
        r_onebf = carve(arena4, 5840, (E, T), BF16)
        r_tot = carve(arena4, 1024, (E, T))
        r_scan = carve(arena4, 1280, (E, T))
        r_t = carve(arena4, 1536, (8, T))
        r_e = sb("r_e", [P, 8, E])
        r_ti = sb("r_ti", [P, 3, T], I32)
        r_ei = sb("r_ei", [P, 2, E], I32)
        expert_cmp = carve(arena4, 5248, (ROWS, E))[0:1]
        expert_f = sb("expert_f", [1, ROWS])
        expert_of = sb("expert_of", [1, ROWS], I32)
        lane_hot = arena[:, 4096:6144].bitcast(BF16).rearrange("p (t l) -> p t l", t=T)
        tile_hot = arena[:, 6144:6144 + 3 * T * ROWS // 2].bitcast(BF16).rearrange("p (m t r) -> p m t r", m=3, t=T)
        inv = arena4[:, 5600:5600 + 2 * ROWS]
        inv_v = carve(arena4, 5700, (3, ROWS))
        gather_row = sb("gather_row", [P, ROWS], I32)
        scatter_row = sb("scatter_row", [P, ROWS], I32)
        xg = carve(arena4, 1792, (AHEAD, D))
        xgT = carve(arena4, 2560, (2, P))
        hid = carve(arena4, 2816, (2, F))
        hidT = carve(arena4, 3840, (2, FC, P))
        yg = carve(arena4, 4864, (3, D))
        yback = arena[:, 0:T * D].rearrange("p (t d) -> p t d", t=T)

        win_rows = arena3[0:N, 9600:9728]
        win_z = carve(arena3, 8448, (NJ, P))
        bm_rows = carve(arena3, 9472, (NJ, N))[0:N]
        bm_diag = arena3[:, 9216:9344]
        c_rows = carve(arena3, 9344, (NJ, N))
        c_diag = carve(arena3, 7936, (NJ, D))
        b_in = sb("b_in", [P, 1])
        d_rep = arena3[:, 9728:9856]
        a_pow = carve(arena3, 6144, (LEVELS, 64 + P))
        a_powT = carve(arena3, 8960, (2, P))
        u1 = carve(arena, 0, (B, P))
        state = carve(arena, 1024, (B, P))

        mu = sb("mu", [P, SLOTS])
        mu_t = carve(arena, 0, (2, SLOTS))
        gamma = sb("gamma", [P, D])
        beta = sb("beta", [P, D])
        mscale = sb("mscale", [P, 1])
        mw1 = sb("mw1", [P, ME, MH])
        mw2 = sb("mw2", [P, MG, D])
        mb1 = sb("mb1", [P, MG])
        mb2 = sb("mb2", [P, 2, D])
        xn = carve(arena3, 0, (T, D))
        square = carve(arena4, 0, (8, D))
        comb = arena2[:, 0:2048].rearrange("p (h k s) -> p h k s", h=2, k=TB)
        disp_s = arena2[:, 2048:4096].rearrange("p (h j t) -> p h j t", h=2, j=2)
        combT = arena[:].rearrange("p (h b t) -> p h b t", h=2, b=B)
        disp = arena2[:, 4096:6144].rearrange("p (h k s) -> p h k s", h=2, k=TB)
        slot_in = carve(arena2, 10240, (2, D))
        slotT = arena2[:, 6144:8192].rearrange("p (e b s) -> p e b s", e=ME, b=B)
        hid_diag = carve(arena3, 4096, (MG, B, MG, MS))
        slot_out = arena2[:, 8192:10240].rearrange("p (h b d) -> p h b d", h=2, b=B)
        neg_c = sb("neg_c", [P, B, TB])
        neg_d = sb("neg_d", [P, B, 2])
        sum_c = sb("sum_c", [P, T])
        inv_c = sb("inv_c", [P, T])
        sum_d = sb("sum_d", [P, B, 2])
        inv_d = sb("inv_d", [P, B, 2])

        rot = sb("rot", [P, R_ALL])
        cos, sin = rot[:, R_COS:R_COS + S], rot[:, R_SIN:R_SIN + S]
        mask_q = sb("mask_q", [P, P], BF16)
        mask_k = sb("mask_k", [P, P], BF16)
        ident_bf = sb("ident_bf", [P, P], BF16)
        wqkv = sb("wqkv", [P, 3 * D])
        wqk = sb("wqk", [P, 4, P])
        wout = sb("wout", [P, D])
        q_stack = [carve(arena, 4096 * i, (H, S), BF16) for i in range(2)]
        k_stack = [carve(arena2, 4096 * i, (H, S), BF16) for i in range(2)]
        prob_e = [carve(arena3, TB * E_LEN * i, (TB, E_LEN)) for i in range(2)]
        v_aug = [carve(arena4, 2048 * i, (TB, H, 32)) for i in range(2)]
        o_t = [carve(arena4, 4096 + 2048 * i, (TB, S)) for i in range(2)]
        raw = sb("raw", [P, 2, S])
        rope = carve(arena2, 8192, (2, S))
        cut = sb("cut", [P, 2, 3, S], BF16)
        neg_m = sb("neg_m", [P, 2, TB, H])
        m_left = sb("m_left", [P, TB, DH])
        m_cut = sb("m_cut", [P, 2, TB, 3, H // 2], BF16)
        m_rows = carve(arena2, 10240, (2, S), BF16)[0:3 * H // 2]
        o_den = sb("o_den", [P, H])
        o_tok = carve(arena2, 9216, (TB, D))
        o_hd = arena2[:, 9728:9728 + S]
        attw_in, att_w = sem("attw_in"), sem("att_w")

        mixw_in, mix_set = sem("mixw_in"), [sem(f"mix_set{i}") for i in range(4)]
        x_in = [sem(f"x_in{i}") for i in range(4)]
        cst_in, w1_in, w2_in, bias_in, biasrow_in = (sem(n) for n in (
            "cst_in", "w1_in", "w2_in", "bias_in", "biasrow_in"))
        gate_in, scanw_in, a_in = sem("gate_in"), sem("scanw_in"), sem("a_in")
        bf_ready, zeroed, bias_cut, turned_w, placed_w = (sem(n) for n in (
            "bf_ready", "zeroed", "bias_cut", "turned_w", "placed_w"))
        pow_mm, pow_kept = sem("pow_mm"), sem("pow_kept")
        stored_out, rows_zeroed = sem("stored_out"), sem("rows_zeroed")
        x_done = [sem(f"x_done{i}") for i in range(len(stages) + 1)]

        def mix_loads(sp):
            if "a" in stages:
                sp.dma_start(rot[:], rotary).then_inc(attw_in, 16)
                sp.dma_start(wqkv[:], a["L1_attn_w_qkv"]).then_inc(attw_in, 16)
                sp.dma_start(wout[:], a["L1_attn_w_out"]).then_inc(attw_in, 16)
            if "m" in stages:
                sp.dma_start(mu[:], a["L1_ffn_mu"].rearrange("d e s -> d (e s)")).then_inc(mixw_in, 16)
                sp.dma_start(gamma[:], a["L1_ffn_ln_gamma"].partition_broadcast(P)).then_inc(mixw_in, 16)
                sp.dma_start(beta[:], a["L1_ffn_ln_beta"].partition_broadcast(P)).then_inc(mixw_in, 16)
                sp.dma_start(mscale[:], a["L1_ffn_scale"].partition_broadcast(P)).then_inc(mixw_in, 16)
                sp.dma_start(mw1[:], a["L1_ffn_w1"].rearrange("e d h -> d e h")).then_inc(mixw_in, 16)
                for q in range(MG):
                    sp.dma_start(mw2[MH * q:MH * q + MH], a["L1_ffn_w2"].rearrange("(g q) h d -> q h g d", q=MG)[q]).then_inc(mixw_in, 16)
                    sp.dma_start(mb1[MH * q:MH * q + MH], a["L1_ffn_b1"].rearrange("(g q) h -> q h g", q=MG)[q],
                                 allow_slow_non_contiguous=True).then_inc(mixw_in, 16)
                for e in range(ME):
                    h, r = e // 8, MS * (e % 8)
                    sp.dma_start(mb2[r:r + MS, h, :], a["L1_ffn_b2"][e].partition_broadcast(MS)).then_inc(mixw_in, 16)

        def load_sync(sp):
            xin = a["L0_attn_x"].rearrange("b (k p) d -> p (b k) d", p=P)
            sp.dma_start(cst[:], consts).then_inc(cst_in, 16)
            for i in range(4):
                sp.dma_start(x[:, 8 * i:8 * i + 8, :], xin[:, 8 * i:8 * i + 8, :]).then_inc(x_in[i], 16)
            if "f" not in stages:
                mix_loads(sp)
                return
            sp.dma_start(bsplit[:, 0, 0, :], a["L0_ffn_b1"].rearrange("e f -> (e f)").rearrange("(p i) -> p i", p=P)).then_inc(bias_in, 16)
            sp.dma_start(bsplit[:, 1, 0, 0:8], a["L0_ffn_b2"].rearrange("e f -> (e f)").rearrange("(p i) -> p i", p=P)).then_inc(bias_in, 16)
            mix_loads(sp)
            sp.dma_start(w1[:], a["L0_ffn_w1"].rearrange("e d f -> d e f")).then_inc(w1_in, 16)
            sp.wait_ge(bias_cut, 1)
            sp.wait_ge(rows_zeroed, 2)
            for r in range(3):
                sp.dma_start(b1rows[r:r + 1, :], bparts[:, 0, r, :]).then_inc(biasrow_in, 16)
                sp.dma_start(b2rows[r:r + 1, :], bparts[:, 1, r, 0:8]).then_inc(biasrow_in, 16)

        def load_scalar(act):
            act.dma_start(gate_rows[:], a["L0_ffn_gate_w"]).then_inc(gate_in, 16)
            if "s" in stages:
                act.dma_start(win_rows[:], a["L0_attn_W_in"]).then_inc(scanw_in, 16)
                for j in range(NJ):
                    act.dma_start(bm_rows[:, j, :], a["L0_attn_Bm"]).then_inc(scanw_in, 16)
                    act.dma_start(c_rows[:, j, :], a["L0_attn_C"]).then_inc(scanw_in, 16)
                    act.dma_start(b_in[N * j:N * j + N, :], a["L0_attn_b_in"].rearrange("(n o) -> n o", o=1)).then_inc(scanw_in, 16)
                act.dma_start(d_rep[:], a["L0_attn_D"].partition_broadcast(P)).then_inc(scanw_in, 16)
                act.wait_ge(zeroed, 1)
                for j in range(NJ):
                    act.dma_start(a_pow[N * j:N * j + N, 0, 64 + N * j:64 + N * j + N], a["L0_attn_A"]).then_inc(a_in, 16)
            if "f" in stages:
                act.dma_start(w2[:], a["L0_ffn_w2"].rearrange("e (c f) d -> f e c d", f=P)).then_inc(w2_in, 16)

        def setup_gpsimd(pool):
            if "f" in stages:
                pool.memset(b1rows[:], 0.0).then_inc(rows_zeroed, 1)
                pool.memset(b2rows[:], 0.0).then_inc(rows_zeroed, 1)
            pool.memset(a_pow[:], 0.0).then_inc(zeroed, 1)
            pool.memset(win_z[:], 0.0)
            pool.memset(bm_diag[:], 0.0)
            pool.memset(c_diag[:], 0.0).then_inc(zeroed, 1)

        def setup_vector(dve, chain):
            dve.wait_ge(cst_in, 16)
            nc.vector.tensor_copy(tri[:], cst[:, C_TRI:C_TRI + P])
            nc.vector.tensor_copy(iota_bf[:], cst[:, C_IOTA:C_IOTA + P])
            nc.vector.memset(ones_bf[:], 1.0)
            chain(nc.vector.memset(ones3[:], 0.0))
            nc.vector.memset(ones3[0:3, :], 1.0).then_inc(bf_ready, 1)
            if "f" in stages:
                dve.wait_ge(bias_in, 32)
            for w, n in ((0, 32), (1, 8)) if "f" in stages else ():
                v, left = bsplit[:, w, 0, 0:n], bsplit[:, w, 1, 0:n]
                part = [bparts[:, w, r, 0:n] for r in range(3)]
                chain(nc.vector.tensor_copy(part[0], v))
                chain(nc.vector.tensor_tensor(left, v, part[0], ALU.subtract))
                chain(nc.vector.tensor_copy(part[1], left))
                chain(nc.vector.tensor_tensor(part[2], left, part[1], ALU.subtract))
            dve.sem_inc(bias_cut, 1)
            dve.wait_ge(turned_w, 1)
            chain(nc.vector.tensor_copy(gateT[:], bank[0][:, 0:E]))
            dve.sem_inc(placed_w, 1)
            if "s" in stages:
                dve.wait_ge(zeroed, 2)
                dve.wait_ge(turned_w, 2)
                for j in range(NJ):
                    rows, cols = slice(N * j, N * j + N), slice(N * j, N * j + N)
                    chain(nc.vector.tensor_copy(win_z[:, j, cols], bank[1][:, 0:N]))
                    chain(nc.vector.tensor_copy(bm_diag[rows, cols], bank[1][rows, 128:128 + N]))
                    chain(nc.vector.tensor_copy(c_diag[rows, j, :], bank[1][rows, 256:256 + D]))
                chain(nc.vector.tensor_copy(a_powT[:, 0, :], bank[1][:, 384:512]))
                dve.sem_inc(placed_w, 1)
                for l in range(1, LEVELS):
                    dve.wait_ge(pow_mm, l)
                    chain(nc.vector.tensor_copy(a_pow[:, l, 64:], bank[2 + l % 2][:, 0:P]))
                    chain(nc.vector.tensor_copy(a_powT[:, l % 2, :], bank[2 + l % 2][:, P:2 * P]))
                    dve.sem_inc(pow_kept, 1)

        def setup_tensor(pe):
            pe.wait_ge(cst_in, 16)
            pe.wait_ge(gate_in, 16)
            pe.transpose(bank[0][:, 0:E], gate_rows[:], ident[0:E, 0:E]).then_inc(turned_w, 1)
            if "s" in stages:
                pe.wait_ge(scanw_in, 16 * (2 + 3 * NJ))
                pe.wait_ge(a_in, 16 * NJ)
                pe.transpose(bank[1][:, 0:N], win_rows[:], ident[0:N, 0:N])
                pe.transpose(bank[1][:, 128:128 + N], bm_rows[:].rearrange("m j n -> m (j n)"), ident[0:N, 0:N])
                pe.transpose(bank[1][:, 256:256 + D], c_rows[:].rearrange("m j n -> m (j n)"), ident)
                pe.transpose(bank[1][:, 384:512], a_pow[:, 0, 64:], ident).then_inc(turned_w, 1)
                pe.wait_ge(placed_w, 2)
                for l in range(1, LEVELS):
                    if l > 1:
                        pe.wait_ge(pow_kept, l - 1)
                    last, lastT = a_pow[:, l - 1, 64:], a_powT[:, (l - 1) % 2, :]
                    pe.matmul(bank[2 + l % 2][:, 0:P], lastT, last, start=True, stop=True)
                    pe.matmul(bank[2 + l % 2][:, P:2 * P], last, lastT, start=True, stop=True).then_inc(pow_mm, 1)

        GT = 8
        GROUPS = T // GT
        stat_sem, var_sem, root_sem, ready_sem = sem("stat"), sem("var"), sem("root"), sem("ready")
        stats_chain = Chain(None, sem("stats_v"))
        taken = set()

        def stats_take(dve, n, g):
            if n == len(stages) or ("take", n, g) in taken:
                return
            taken.add(("take", n, g))
            stats_chain.engine = dve
            if n == 0:
                dve.wait_ge(x_in[g], 16)
            else:
                dve.wait_ge(x_done[n], GT * g + GT)
            for t in range(GT * g, GT * g + GT):
                nc.vector.bn_stats(half_stats[:, t, :], x[:, t, :]).then_inc(stat_sem, 1)
            dve.wait_ge(stat_sem, T * n + GT * g + GT)
            c = slice(GT * g, GT * g + GT)
            me, m2e, mo, m2o = (half_stats[:, c, k] for k in (1, 2, 4, 5))
            nc.vector.tensor_tensor(st[:, 2, c], me, mo, ALU.add)
            nc.vector.tensor_tensor(st[:, 3, c], me, mo, ALU.subtract)
            stats_chain(nc.vector.tensor_tensor(st[:, 4, c], m2e, m2o, ALU.add))
            nc.vector.tensor_scalar(mean[:, c], st[:, 2, c], 0.5, None, ALU.mult)
            stats_chain(nc.vector.scalar_tensor_tensor(st[:, 5, c], st[:, 3, c], float(P // 4), st[:, 3, c], ALU.mult, ALU.mult))
            stats_chain(nc.vector.tensor_tensor(st[:, 6, c], st[:, 4, c], st[:, 5, c], ALU.add))
            scale, shift = ((1.0 + EPS) / P, EPS * EPS) if stages[n] == "m" else (1.0 / P, EPS)
            nc.vector.tensor_scalar(st[:, 7, c], st[:, 6, c], scale, shift, ALU.mult, ALU.add).then_inc(var_sem, 1)

        def stats_root(act, n, g):
            if n == len(stages) or ("root", n, g) in taken:
                return
            taken.add(("root", n, g))
            c = slice(GT * g, GT * g + GT)
            act.wait_ge(var_sem, GROUPS * n + g + 1)
            nc.scalar.activation(st[:, 8, c], st[:, 7, c], ACT.Sqrt).then_inc(root_sem, 1)

        def stats_finish(dve, n, g):
            if n == len(stages) or ("finish", n, g) in taken:
                return
            taken.add(("finish", n, g))
            c = slice(GT * g, GT * g + GT)
            dve.wait_ge(root_sem, GROUPS * n + g + 1)
            stats_chain(nc.vector.reciprocal(rstd[:, c], st[:, 8, c]))
            nc.vector.scalar_tensor_tensor(shift_by[:, c], mean[:, c], -1.0, rstd[:, c], ALU.mult, ALU.mult).then_inc(ready_sem, 1)

        def stats_after(dve, n, g):
            stats_take(dve, n, g)
            if g:
                stats_finish(dve, n, g - 1)
            if g == GROUPS - 1:
                stats_finish(dve, n, g)

        def normalise_scalar(act, n, s, at, copy_to, stored=None, stored_at=None):

            def tiles(g):
                act.wait_ge(ready_sem, GROUPS * n + g + 1)
                for r in range(GT):
                    if r % TB == 0 and g:
                        act.wait_ge(s["turned"], at["turned"] + GT * g - TB + r)
                        if stored is not None:
                            act.wait_ge(stored[r // TB], stored_at[r // TB] + 16 * g)
                    t = slice(GT * g + r, GT * g + r + 1)
                    nc.scalar.activation(xh[:, r, :], x[:, GT * g + r, :], ACT.Identity, bias=shift_by[:, t],
                                         scale=rstd[:, t]).then_inc(s["normed"], 1)
                for h in range(2):
                    act.wait_ge(s["turned"], at["turned"] + GT * g + TB * h + TB)
                    nc.scalar.copy(xT[:, h, :], bank[h][:]).then_inc(s["xT_ready"], 1)

            stats_root(act, n, 0)
            for g in range(1, GROUPS):
                stats_root(act, n, g)
                tiles(g - 1)
            tiles(GROUPS - 1)

        FFN_COUNTS = dict(v=0, normed=T, turned=T, xT_ready=B, gated=B, log_ready=1, exp_ready=1,
                          one_ready=1, ranked=1, hot_ready=1, inverted=1, rows_ready=1, expert_ready=1, g_turned=ROWS,
                          xgT=ROWS, h_mm=ROWS, h_relu=ROWS, h_turned=ROWS, hT_ready=ROWS, y_mm=ROWS, y_ready=ROWS)
        RING_COUNTS = dict(stored=[16 * 4] * 2, gathered=[16 * len(range(i, ROWS, AHEAD)) for i in range(AHEAD)],
                           scattered=[16 * len(range(i, ROWS, 3)) for i in range(3)], back=[16] * 4)
        ffn_sems = {k: sem(f"f_{k}") for k in FFN_COUNTS}
        ffn_rings = {k: [sem(f"f_{k}{i}") for i in range(len(v))] for k, v in RING_COUNTS.items()}
        chains = {"f": 0, "m": 0}

        def ffn(n):
            s, at = ffn_sems, {k: v * stages[:n].count("f") for k, v in FFN_COUNTS.items()}
            stored, gathered, scattered, back = (ffn_rings[k] for k in RING_COUNTS)
            for k, counts in RING_COUNTS.items():
                at[k] = [v * stages[:n].count("f") for v in counts]

            def sync(sp):
                rows = xhat_dram.rearrange("(t p) d -> p t d", p=P)
                with sp.Fori(0, 4) as i:
                    for h in range(2):
                        sp.wait_ge(s["normed"], at["normed"] + 8 * i + 4 * h + 4)
                        sp.dma_start(rows[:, bass.ds(8 * i + 4 * h, 4), :], xh[:, 4 * h:4 * h + 4, :]).then_inc(stored[h], 16)
                for q in range(3):
                    sp.wait_ge(scattered[q], at["scattered"][q] + 16 * (ROWS // 3))
                for q in range(4):
                    sp.dma_start(yback[:, 8 * q:8 * q + 8, :],
                                 yrow_dram.rearrange("(t p) d -> p t d", p=P)[:, 8 * q:8 * q + 8, :]).then_inc(back[q], 16)

            def vector(dve):
                chain = Chain(dve, s["v"], chains["f"])
                dve.wait_ge(s["gated"], at["gated"] + B)
                chain(nc.vector.tensor_copy(r_log[:], bank[2][:, 0:T * E].rearrange("p (t e) -> p e t", e=E)))
                by_token = lambda v: v.rearrange("p e t -> p t e")
                over_e = lambda v: v.unsqueeze(1).to_broadcast([P, E, T])
                over_t = lambda v: v.unsqueeze(2).to_broadcast([P, E, T])
                top, esum, prob, first, dest, lane, row = (r_t[:, k, :] for k in range(7))
                em = cst[:, C_EM:C_EM + E * T].rearrange("p (e t) -> p e t", e=E)
                chain(nc.vector.tensor_reduce(top, by_token(r_log[:]), AX.X, ALU.max))
                nc.vector.tensor_tensor(r_exp[:], r_log[:], over_e(top), ALU.subtract).then_inc(s["log_ready"], 1)
                chain(nc.vector.tensor_tensor(r_eq[:], r_log[:], over_e(top), ALU.is_equal))
                chain(nc.vector.tensor_tensor(r_scan[:], r_eq[:], em, ALU.mult))
                chain(nc.vector.tensor_reduce(first, by_token(r_scan[:]), AX.X, ALU.min))
                chain(nc.vector.tensor_tensor(r_one[:], em, over_e(first), ALU.is_equal))
                nc.vector.tensor_copy(r_onebf[:], r_one[:]).then_inc(s["one_ready"], 1)
                dve.wait_ge(s["exp_ready"], at["exp_ready"] + 1)
                chain(nc.vector.tensor_reduce(esum, by_token(r_log[:]), AX.X, ALU.add))
                chain(nc.vector.reciprocal(prob, esum))
                chain(nc.vector.tensor_scalar(prob, prob, 0.5, None, ALU.mult))
                dve.wait_ge(s["ranked"], at["ranked"] + 1)
                chain(nc.vector.tensor_copy(r_tot[:], bank[3][:, 256:512].rearrange("p (e t) -> p e t", e=E)))
                flat = lambda v: v.rearrange("p e t -> p (e t)")
                one = cst[:, C_ONE:C_ONE + 256]
                cnt, tiles, tiles_to, cnt_to, r_a, r_b, off = (r_e[:, k, :] for k in range(7))
                nc.vector.tensor_tensor_scan(flat(r_scan[:]), one, flat(r_tot[:]), 0.0, ALU.mult, ALU.add)
                chain(nc.vector.tensor_reduce(cnt, r_tot[:], AX.X, ALU.add))
                chain(nc.vector.tensor_scalar(r_ei[:, 0, :], cnt, float(P - 1), None, ALU.add))
                chain(nc.vector.tensor_scalar(r_ei[:, 1, :], r_ei[:, 0, :], 7, None, ALU.logical_shift_right))
                chain(nc.vector.tensor_copy(tiles, r_ei[:, 1, :]))
                nc.vector.tensor_tensor_scan(tiles_to, one[:, 0:E], tiles, 0.0, ALU.mult, ALU.add)
                chain(nc.vector.tensor_tensor_scan(cnt_to, one[:, 0:E], cnt, 0.0, ALU.mult, ALU.add))
                nc.vector.tensor_tensor(r_a, tiles_to, tiles, ALU.subtract)
                chain(nc.vector.tensor_tensor(r_b, cnt_to, cnt, ALU.subtract))
                chain(nc.vector.scalar_tensor_tensor(off, r_a, float(P), r_b, ALU.mult, ALU.subtract))
                chain(nc.vector.tensor_tensor(r_scan[:], r_scan[:], r_tot[:], ALU.subtract))
                chain(nc.vector.tensor_tensor(r_scan[:], r_scan[:], over_t(off), ALU.add))
                chain(nc.vector.tensor_tensor(flat(r_scan[:]), flat(r_scan[:]), bank[3][:, 0:256], ALU.add))
                chain(nc.vector.tensor_tensor(r_scan[:], r_scan[:], r_one[:], ALU.mult))
                chain(nc.vector.tensor_reduce(dest, by_token(r_scan[:]), AX.X, ALU.add))
                chain(nc.vector.tensor_copy(r_ti[:, 0, :], dest))
                nc.vector.tensor_scalar(r_ti[:, 1, :], r_ti[:, 0, :], P - 1, None, ALU.bitwise_and)
                chain(nc.vector.tensor_scalar(r_ti[:, 2, :], r_ti[:, 0, :], 7, None, ALU.logical_shift_right))
                nc.vector.tensor_copy(lane, r_ti[:, 1, :])
                chain(nc.vector.tensor_copy(row, r_ti[:, 2, :]))
                with dve.Fori(0, 4) as i:
                    for r in range(8):
                        t = bass.ds(8 * i + r, 1)
                        nc.vector.tensor_scalar(lane_hot[:, t, :], iota_bf[:], lane[:, t], None, ALU.is_equal)
                ramp = cst[:, C_TILE:C_TILE + ROWS].unsqueeze(1).to_broadcast([P, T, ROWS])
                tcol = cst[:, C_TCOL:C_TCOL + T].unsqueeze(2).to_broadcast([P, T, ROWS])
                chain(nc.vector.tensor_tensor(tile_hot[:, 2], ramp, row.unsqueeze(2).to_broadcast([P, T, ROWS]), ALU.is_equal))
                nc.vector.tensor_tensor(tile_hot[:, 0], tile_hot[:, 2], tcol, ALU.mult)
                nc.vector.tensor_scalar(tile_hot[:, 1], tile_hot[:, 2], cst[:, C_P1:C_P1 + 1], None, ALU.mult).then_inc(s["hot_ready"], 1)
                ends = r_e[0:1, 2, :].unsqueeze(1).to_broadcast([1, ROWS, E])
                tile_no = cst[0:1, C_TILE:C_TILE + ROWS].unsqueeze(2).to_broadcast([1, ROWS, E])
                chain(nc.vector.tensor_tensor(expert_cmp[:], ends, tile_no, ALU.is_le))
                chain(nc.vector.tensor_reduce(expert_f[:], expert_cmp[:], AX.X, ALU.add))
                nc.vector.tensor_scalar(expert_of[:], expert_f[:], float(E - 1), None, ALU.min).then_inc(s["expert_ready"], 1)
                dve.wait_ge(s["inverted"], at["inverted"] + 1)
                chain(nc.vector.tensor_copy(inv[:], bank[2][:, 0:2 * ROWS]))
                token, pad = inv_v[:, 0, :], inv_v[:, 1, :]
                chain(nc.vector.scalar_tensor_tensor(token, inv[:, 0:ROWS], float(P), inv[:, ROWS:], ALU.mult, ALU.add))
                chain(nc.vector.tensor_scalar(pad, token, 0.0, float(NOWHERE), ALU.is_equal, ALU.mult))
                nc.vector.tensor_scalar(gather_row[:], token, -1.0, 0.0, ALU.add, ALU.max)
                nc.vector.scalar_tensor_tensor(scatter_row[:], token, -1.0, pad, ALU.add, ALU.add).then_inc(s["rows_ready"], 1)

                chains["f"] = chain.n

                def hidden(j, k):
                    dve.wait_ge(s["h_turned"], at["h_turned"] + j + 1)
                    nc.vector.tensor_copy(hidT[:, k % 2].rearrange("p c m -> p (c m)"), bank[4 + k % 2][:]).then_inc(s["hT_ready"], 1)

                def result(j, k, used):
                    dve.wait_ge(s["y_mm"], at["y_mm"] + j + 1)
                    if later(used):
                        dve.wait_ge(scattered[k % 3], at["scattered"][k % 3] + used)
                    nc.vector.tensor_copy(yg[:, k % 3, :], bank[6 + k % 2][:, 0:D]).then_inc(s["y_ready"], 1)

                def six(i):
                    for k in range(6):
                        hidden(6 * i + k + 1, k + 1)
                        result(6 * i + k, k, 16 * (2 * i + k // 3))

                hidden(0, 0)
                peeled(dve, 0, 6, six)
                for j in range(36, ROWS):
                    if j + 1 < ROWS:
                        hidden(j + 1, j + 1)
                    result(j, j, 16 * (j // 3))
                for g in range(GROUPS):
                    dve.wait_ge(back[g], at["back"][g] + 16)
                    for t in range(GT * g, GT * g + GT):
                        nc.vector.scalar_tensor_tensor(x[:, t, :], yback[:, t, :], prob[:, t:t + 1], x[:, t, :],
                                                       ALU.mult, ALU.add).then_inc(x_done[n + 1], 1)
                    stats_after(dve, n + 1, g)

            def scalar(act):
                normalise_scalar(act, n, s, at, xT, stored, at["stored"])
                act.wait_ge(s["one_ready"], at["one_ready"] + 1)
                nc.scalar.activation(r_log[:], r_exp[:], ACT.Exp).then_inc(s["exp_ready"], 1)

                def tokens(j, k):
                    act.wait_ge(s["g_turned"], at["g_turned"] + j + 1)
                    nc.scalar.copy(xgT[:, k % 2, :], bank[k % 2][:, 0:P]).then_inc(s["xgT"], 1)

                def relu(j, k):
                    act.wait_ge(s["h_mm"], at["h_mm"] + j + 1)
                    nc.scalar.activation(hid[:, k % 2, :], bank[2 + k % 2][:], ACT.Relu).then_inc(s["h_relu"], 1)

                tokens(0, 0)
                with act.Fori(0, 6) as i:
                    for k in range(6):
                        tokens(6 * i + k + 1, k + 1)
                        relu(6 * i + k, k)
                for j in range(36, ROWS):
                    if j + 1 < ROWS:
                        tokens(j + 1, j + 1)
                    relu(j, j)

            def tensor(pe):
                if n == stages.index("f"):
                    pe.wait_ge(placed_w, 1)
                with pe.Fori(0, 4) as i:
                    for h in range(2):
                        for k in range(TB):
                            pe.wait_ge(s["normed"], at["normed"] + 8 * i + 4 * h + k + 1)
                            pe.transpose(bank[h][:, k * P:k * P + P], xh[:, 4 * h + k, :], ident).then_inc(s["turned"], 1)
                    for h in range(2):
                        pe.wait_ge(s["xT_ready"], at["xT_ready"] + 2 * i + h + 1)
                        for k in range(TB):
                            last = pe.matmul(bank[2][:, bass.ds((8 * i + 4 * h + k) * E, E)], xT[:, h, k * P:k * P + P],
                                             gateT[:], start=True, stop=True)
                        last.then_inc(s["gated"], 1)
                pe.wait_ge(bf_ready, 1)
                pe.wait_ge(s["one_ready"], at["one_ready"] + 1)
                one_hot = r_onebf[:].rearrange("p e t -> p (e t)")
                pe.matmul(bank[3][:, 0:256], tri[:], one_hot, start=True, stop=True)
                pe.matmul(bank[3][:, 256:512], ones_bf[:], one_hot, start=True, stop=True).then_inc(s["ranked"], 1)
                pe.wait_ge(s["hot_ready"], at["hot_ready"] + 1)
                for t in range(T):
                    last = pe.matmul(bank[2][:, 0:2 * ROWS], lane_hot[:, t, :], tile_hot[:, 0:2, t, :], start=(t == 0), stop=(t == T - 1))
                last.then_inc(s["inverted"], 1)

                pe.wait_ge(s["rows_ready"], at["rows_ready"] + 1)
                pe.wait_ge(s["expert_ready"], at["expert_ready"] + 1)
                pe.wait_ge(w1_in, 16)
                pe.wait_ge(w2_in, 16)
                pe.wait_ge(biasrow_in, 16 * 6)

                def turn_in(j, k, have):
                    pe.wait_ge(gathered[k % AHEAD], at["gathered"][k % AHEAD] + have)
                    pe.transpose(bank[k % 2][:, 0:P], xg[:, k % AHEAD, :], ident).then_inc(s["g_turned"], 1)

                def up(j, k):
                    e = pe.value_load(expert_of[0:1, bass.ds(j, 1)], min_val=0, max_val=E - 1)
                    pe.wait_ge(s["xgT"], at["xgT"] + j + 1)
                    pe.matmul(bank[2 + k % 2][:], ones3[:], b1rows[:, bass.ds(e * F, F)], start=True, stop=False)
                    pe.matmul(bank[2 + k % 2][:], xgT[:, k % 2, :], w1[:, bass.ds(e, 1), :], start=False, stop=True).then_inc(s["h_mm"], 1)

                def turn_hidden(j, k):
                    pe.wait_ge(s["h_relu"], at["h_relu"] + j + 1)
                    for c in range(FC):
                        last = pe.transpose(bank[4 + k % 2][:, c * P:c * P + P], hid[:, k % 2, c * P:c * P + P], ident)
                    last.then_inc(s["h_turned"], 1)

                def down(j, k):
                    e = pe.value_load(expert_of[0:1, bass.ds(j, 1)], min_val=0, max_val=E - 1)
                    pe.wait_ge(s["hT_ready"], at["hT_ready"] + j + 1)
                    if later(j):
                        pe.wait_ge(s["y_ready"], at["y_ready"] + j)
                    pe.matmul(bank[6 + k % 2][:, 0:D], ones3[:], b2rows[:, bass.ds(e * D, D)], start=True, stop=False)
                    for c in range(FC):
                        last = pe.matmul(bank[6 + k % 2][:, 0:D], hidT[:, k % 2, c, :], w2[:, bass.ds(e, 1), c, :],
                                         start=False, stop=(c == FC - 1))
                    last.then_inc(s["y_mm"], 1)

                for j in range(3):
                    turn_in(j, j, 16)
                    if j >= 1:
                        up(j - 1, j - 1)
                    if j >= 2:
                        turn_hidden(j - 2, j - 2)

                def six(i):
                    for k in range(6):
                        turn_in(6 * i + k + 3, k + 3, 16 * (i + (k + 3) // AHEAD + 1))
                        up(6 * i + k + 2, k + 2)
                        turn_hidden(6 * i + k + 1, k + 1)
                        down(6 * i + k, k)

                peeled(pe, 0, 6, six)
                for j in range(ROWS, ROWS + 3):
                    if j - 1 < ROWS:
                        up(j - 1, j - 1)
                    if j - 2 < ROWS:
                        turn_hidden(j - 2, j - 2)
                    down(j - 3, j - 3)

            def gpsimd(pool):
                pool.wait_ge(s["rows_ready"], at["rows_ready"] + 1)
                for h in range(2):
                    pool.wait_ge(stored[h], at["stored"][h] + 16 * 4)

                def gather(j):
                    if j >= AHEAD:
                        pool.wait_ge(s["g_turned"], at["g_turned"] + j - AHEAD + 1)
                    pool.indirect_dma_start(xg[:, j % AHEAD, :], None, xhat_dram, bass.IndirectOffsetOnAxis(gather_row[:, j:j + 1], 0)).then_inc(gathered[j % AHEAD], 16)

                for j in range(AHEAD):
                    gather(j)
                for j in range(ROWS):
                    pool.wait_ge(s["y_ready"], at["y_ready"] + j + 1)
                    pool.indirect_dma_start(yrow_dram, bass.IndirectOffsetOnAxis(scatter_row[:, j:j + 1], 0), yg[:, j % 3, :], None,
                                            bounds_check=T * P - 1, oob_is_err=False).then_inc(scattered[j % 3], 16)
                    if j + AHEAD < ROWS:
                        gather(j + AHEAD)

            return dict(sync=sync, vector=vector, scalar=scalar, tensor=tensor, gpsimd=gpsimd)

        def scan(n):
            s = {k: sem(f"s{n}_{k}") for k in (
                "v normed turned xT_ready u_mm u_kept ub_mm level_mm level_done d_added y_mm").split()}
            at = dict.fromkeys(s, 0)

            def vector(dve):
                chain = Chain(dve, s["v"])
                for g in range(2):
                    dve.wait_ge(s["ub_mm"], g + 1)
                    nc.vector.tensor_copy(half(state, g), bank[4 + g][:]).then_inc(s["level_done"], 1)
                for l in range(LEVELS):
                    for g in range(2):
                        dve.wait_ge(s["level_mm"], 2 * l + g + 1)
                        dve.wait_ge(s["level_done"], 2 * l + g + 1)
                        nc.vector.tensor_tensor(half(state, g), half(state, g), bank[6 + g][:], ALU.add).then_inc(s["level_done"], 1)
                for b in range(B):
                    dve.wait_ge(s["y_mm"], b + 1)
                    dve.wait_ge(s["d_added"], b + 1)
                    tiles = x[:, TB * b:TB * b + TB, :].rearrange("p t d -> p (t d)")
                    nc.vector.tensor_tensor(tiles, tiles, bank[4 + b % 4][:], ALU.add).then_inc(x_done[n + 1], TB)
                    if b % 2:
                        stats_after(dve, n + 1, b // 2)

            def half(v, g):
                return v[:, 4 * g:4 * g + 4, :].rearrange("p b c -> p (b c)")

            def gpsimd(pool):
                pool.wait_ge(scanw_in, 16 * (2 + 3 * NJ))
                with pool.Fori(0, B) as b:
                    pool.wait_ge(s["normed"], TB * b + TB)
                    tiles = x[:, bass.ds(TB * b, TB), :]
                    pool.tensor_tensor(tiles, tiles, d_rep[:].unsqueeze(1).to_broadcast([P, TB, D]), ALU.add).then_inc(s["d_added"], 1)

            def scalar(act):
                normalise_scalar(act, n, s, at, xT)
                act.wait_ge(scanw_in, 16 * (2 + 3 * NJ))
                for g in range(2):
                    act.wait_ge(s["u_mm"], 4 * g + 4)
                    nc.scalar.activation(half(u1, g), bank[2 + g][:], ACT.Identity, bias=b_in[:, 0:1]).then_inc(s["u_kept"], 1)

            def tensor(pe):
                for g in range(2):
                    with pe.Fori(0, 2) as i:
                        for h in range(2):
                            for k in range(TB):
                                pe.wait_ge(s["normed"], 16 * g + 8 * i + 4 * h + k + 1)
                                pe.transpose(bank[h][:, k * P:k * P + P], xh[:, 4 * h + k, :], ident).then_inc(s["turned"], 1)
                        for h in range(2):
                            pe.wait_ge(s["xT_ready"], 4 * g + 2 * i + h + 1)
                            for k in range(TB):
                                last = pe.matmul(bank[2 + g][:, bass.ds((2 * i + h) * P, P)], win_z[:, k, :],
                                                 xT[:, h, k * P:k * P + P], start=(k == 0), stop=(k == TB - 1))
                            last.then_inc(s["u_mm"], 1)
                for g in range(2):
                    pe.wait_ge(s["u_kept"], g + 1)
                    pe.matmul(bank[4 + g][:], bm_diag[:], half(u1, g), start=True, stop=True).then_inc(s["ub_mm"], 1)
                for l in range(LEVELS):
                    step = 1 << l
                    for g in range(2):
                        pe.wait_ge(s["level_done"], 2 * l + g + 1)
                        to = bank[6 + g][:].rearrange("p (b c) -> p b c", b=4)
                        h = state[:, 4 * g:4 * g + 4, :]
                        if step < P:
                            pe.matmul(to[:, :, step:], a_pow[:, l, 64:], h[:, :, 0:P - step], start=True, stop=True)
                            last = pe.matmul(to[:, :, 0:step], a_pow[:, l, 32:160], h[:, :, P - step:], start=True, stop=True)
                        else:
                            shift = N * step // P
                            last = pe.matmul(to, a_pow[:, l, 64 - shift:192 - shift], h, start=True, stop=True)
                        last.then_inc(s["level_mm"], 1)
                for b in range(B):
                    if b == 0:
                        pe.wait_ge(s["level_done"], 2 * LEVELS + 1)
                    if b == 3:
                        pe.wait_ge(s["level_done"], 2 * LEVELS + 2)
                    if b >= 4:
                        pe.wait_ge(x_done[n + 1], TB * (b - 3))
                    pe.matmul(bank[4 + b % 4][:], state[:, b, :], c_diag[:].rearrange("p j d -> p (j d)"), start=True, stop=True).then_inc(s["y_mm"], 1)

            return dict(sync=lambda sp: None, vector=vector, scalar=scalar, tensor=tensor, gpsimd=gpsimd)


        MIX_COUNTS = dict(v=0, centered=T, xn=T, squared=T, norm_sqrt=GROUPS, unit_ready=GROUPS, unit=B, turned=T,
                          xT_ready=B, logit_c=2 * B, logit_d=2 * B, max_c=2 * B, max_d=2 * B, exp_c=T, exp_d=2 * B,
                          turn_c0=B, turn_c1=B, turn_d0=B, turn_d1=B, kept_c0=B, kept_c1=B, kept_d0=B, kept_d1=B,
                          in_mm=B, in_kept=2 * B, in_turned=B, slotT=B, h_mm=MG, h_gelu=MG * MG, out_mm=4, out_kept=4,
                          y_mm=B, weights=B, cleared=1)
        mix_sems = {k: sem(f"m_{k}") for k in MIX_COUNTS}
        MIXW = 16 * (5 + 2 * MG + ME)

        def mix_setup_vector(dve, chain):
            dve.wait_ge(mixw_in, MIXW)
            nc.vector.tensor_tensor(mu_t[:, 0], mu[:], mu[:], ALU.mult).then_inc(mix_set[0], 1)
            dve.wait_ge(mix_set[2], 1)
            chain(nc.vector.tensor_scalar(mu_t[:, 0], mu_t[:, 1], 1e-12, None, ALU.max))
            chain(nc.vector.reciprocal(mu_t[:, 1], mu_t[:, 0]))
            nc.vector.tensor_tensor(mu[:], mu[:], mu_t[:, 1], ALU.mult).then_inc(mix_set[3], 1)

        def mix(n):
            s, at = mix_sems, {k: v * stages[:n].count("m") for k, v in MIX_COUNTS.items()}

            def vector(dve):
                chain = Chain(dve, s["v"], chains["m"])
                if n == stages.index("m"):
                    if n:
                        dve.wait_ge(x_done[n], T)
                    mix_setup_vector(dve, chain)
                norm, unit = st[:, 3, :], st[:, 4, :]

                def unit_of(g):
                    c = slice(GT * g, GT * g + GT)
                    dve.wait_ge(s["norm_sqrt"], at["norm_sqrt"] + g + 1)
                    chain(nc.vector.tensor_scalar(norm[:, c], st[:, 2, c], 1e-12, None, ALU.max))
                    chain(nc.vector.reciprocal(unit[:, c], norm[:, c]))
                    nc.vector.tensor_scalar(unit[:, c], unit[:, c], mscale[:, 0:1], None, ALU.mult).then_inc(s["unit_ready"], 1)

                for g in range(GROUPS):
                    dve.wait_ge(ready_sem, GROUPS * n + g + 1)
                    for t in range(GT * g, GT * g + GT):
                        nc.vector.scalar_tensor_tensor(xn[:, t, :], x[:, t, :], mean[:, t:t + 1], gamma[:], ALU.subtract,
                                                       ALU.mult).then_inc(s["centered"], 1)
                    dve.wait_ge(s["centered"], at["centered"] + GT * g + GT)
                    for t in range(GT * g, GT * g + GT):
                        nc.vector.scalar_tensor_tensor(xn[:, t, :], xn[:, t, :], rstd[:, t:t + 1], beta[:], ALU.mult,
                                                       ALU.add).then_inc(s["xn"], 1)
                    if g:
                        unit_of(g - 1)
                unit_of(GROUPS - 1)

                def max_c(b):
                    for j in range(2):
                        dve.wait_ge(s["logit_c"], at["logit_c"] + 2 * b + j + 1)
                        nc.vector.tensor_reduce(neg_c[:, bass.ds(b, 1), 2 * j:2 * j + 2], bank[2 + j][:].rearrange("p (k s) -> p k s", k=2),
                                                AX.X, ALU.max, negate=True).then_inc(s["max_c"], 1)

                def max_d(b):
                    for j in range(2):
                        dve.wait_ge(s["logit_d"], at["logit_d"] + 2 * b + j + 1)
                        nc.vector.tensor_reduce(neg_d[:, bass.ds(b, 1), j:j + 1], bank[4 + j][:], AX.X, ALU.max, negate=True).then_inc(s["max_d"], 1)

                def keep_c(b):
                    dve.wait_ge(s["turn_c1"], at["turn_c1"] + b + 1)
                    nc.vector.tensor_copy(combT[:, 1, bass.ds(b, 1), :], bank[7][:]).then_inc(s["kept_c1"], 1)

                def keep_d(b, h):
                    dve.wait_ge(s["turn_d1"], at["turn_d1"] + b + 1)
                    nc.vector.tensor_copy(disp[:, h, 2:4, :].rearrange("p k s -> p (k s)"), bank[7][:]).then_inc(s["kept_d1"], 1)
                    nc.vector.reciprocal(inv_d[:, bass.ds(b, 1), :], sum_d[:, bass.ds(b, 1), :]).then_inc(s["weights"], 1)

                def keep_in(b):
                    dve.wait_ge(s["in_mm"], at["in_mm"] + b + 1)
                    dve.wait_ge(s["weights"], at["weights"] + b + 1)
                    for j in range(2):
                        nc.vector.tensor_scalar(slot_in[:, j, :], bank[1][:, j * D:j * D + D], inv_d[:, bass.ds(b, 1), j:j + 1], None,
                                                ALU.mult).then_inc(s["in_kept"], 1)

                def step(b, h):
                    keep_c(b)
                    max_c(b + 1)
                    keep_d(b, h)
                    max_d(b + 1)
                    keep_in(b)

                max_c(0)
                max_d(0)
                step(0, 0)
                with dve.Fori(0, 3) as i:
                    step(2 * i + 1, 1)
                    step(2 * i + 2, 0)
                keep_c(7)
                keep_d(7, 1)
                keep_in(7)
                chain(nc.vector.reciprocal(inv_c[:], sum_c[:]))
                chain(nc.vector.tensor_scalar(inv_c[:], inv_c[:], 0.5, None, ALU.mult))
                chains["m"] = chain.n
                for h in range(2):
                    for j in range(2):
                        dve.wait_ge(s["out_mm"], at["out_mm"] + 2 * h + j + 1)
                        nc.vector.tensor_tensor(slot_out[:, h, 4 * j:4 * j + 4, :], bank[2 + 2 * h + j][:].rearrange("p (b d) -> p b d", b=4),
                                                mb2[:, h, :].unsqueeze(1).to_broadcast([P, 4, D]), ALU.add).then_inc(s["out_kept"], 1)
                for b in range(B):
                    dve.wait_ge(s["y_mm"], at["y_mm"] + b + 1)
                    for k in range(TB):
                        t = TB * b + k
                        nc.vector.scalar_tensor_tensor(x[:, t, :], bank[Y_BANK[b % 4]][:, k * D:k * D + D], inv_c[:, t:t + 1], x[:, t, :],
                                                       ALU.mult, ALU.add).then_inc(x_done[n + 1], 1)
                    if b % 2:
                        stats_after(dve, n + 1, b // 2)

            Y_BANK = (6, 0, 1, 4)

            def gpsimd(pool):

                def units(b):
                    if not isinstance(b, int) or b % 2 == 0:
                        pool.wait_ge(s["unit_ready"], at["unit_ready"] + b // 2 + 1)
                    h = b % 2
                    tiles = slice(TB * b, TB * b + TB)
                    if b >= 2:
                        pool.wait_ge(s["turned"], at["turned"] + TB * (b - 1))
                    pool.tensor_tensor(xh[:, TB * h:TB * h + TB, :], xn[:, tiles, :], st[:, 4, tiles].unsqueeze(2).to_broadcast([P, TB, D]),
                                       ALU.mult).then_inc(s["unit"], 1)

                for b in range(B):
                    units(b)
                pool.memset(hid_diag[:], 0.0).then_inc(s["cleared"], 1)

            def scalar(act):
                def squares(g):
                    for r in range(GT):
                        t = GT * g + r
                        act.wait_ge(s["xn"], at["xn"] + t + 1)
                        nc.scalar.activation(square[:, r, :], xn[:, t, :], ACT.Square, accum_out=st[:, 5, t:t + 1]).then_inc(s["squared"], 1)
                    act.wait_ge(s["squared"], at["squared"] + GT * g + GT)
                    c = slice(GT * g, GT * g + GT)
                    nc.scalar.activation(st[:, 2, c], st[:, 5, c], ACT.Sqrt).then_inc(s["norm_sqrt"], 1)

                def copy_xT(b, h):
                    act.wait_ge(s["turned"], at["turned"] + TB * b + TB)
                    nc.scalar.copy(xT[:, h, :], bank[0][:]).then_inc(s["xT_ready"], 1)

                def exp_c(b, h):
                    for k in range(TB):
                        t = bass.ds(TB * b + k, 1)
                        act.wait_ge(s["max_c"], at["max_c"] + 2 * b + k // 2 + 1)
                        nc.scalar.activation(comb[:, h, k, :], bank[2 + k // 2][:, SLOTS * (k % 2):SLOTS * (k % 2) + SLOTS], ACT.Exp,
                                             bias=neg_c[:, bass.ds(b, 1), k:k + 1], accum_out=sum_c[:, t]).then_inc(s["exp_c"], 1)

                def exp_d(b, h):
                    for j in range(2):
                        act.wait_ge(s["max_d"], at["max_d"] + 2 * b + j + 1)
                        nc.scalar.activation(disp_s[:, h, j, :], bank[4 + j][:], ACT.Exp, bias=neg_d[:, bass.ds(b, 1), j:j + 1],
                                             accum_out=sum_d[:, bass.ds(b, 1), j:j + 1]).then_inc(s["exp_d"], 1)

                def keep_c(b):
                    act.wait_ge(s["turn_c0"], at["turn_c0"] + b + 1)
                    nc.scalar.copy(combT[:, 0, bass.ds(b, 1), :], bank[6][:]).then_inc(s["kept_c0"], 1)

                def keep_d(b, h):
                    act.wait_ge(s["turn_d0"], at["turn_d0"] + b + 1)
                    nc.scalar.copy(disp[:, h, 0:2, :].rearrange("p k s -> p (k s)"), bank[6][:]).then_inc(s["kept_d0"], 1)

                def keep_slots(b):
                    act.wait_ge(s["in_turned"], at["in_turned"] + b + 1)
                    nc.scalar.copy(slotT[:, :, bass.ds(b, 1), :], bank[1][:, SLOTS:].rearrange("p (e s) -> p e s", e=ME)).then_inc(s["slotT"], 1)

                def step(b, h):
                    copy_xT(b + 1, 1 - h)
                    if later(b):
                        keep_slots(b - 1)
                    keep_c(b)
                    exp_c(b + 1, 1 - h)
                    keep_d(b, h)
                    exp_d(b + 1, 1 - h)

                for g in range(GROUPS):
                    stats_root(act, n, g)
                if n == stages.index("m"):
                    act.wait_ge(mix_set[1], 1)
                    nc.scalar.activation(mu_t[:, 1], bank[0][:, 0:SLOTS], ACT.Sqrt).then_inc(mix_set[2], 1)
                for g in range(GROUPS):
                    squares(g)
                copy_xT(0, 0)
                exp_c(0, 0)
                exp_d(0, 0)
                step(0, 0)
                with act.Fori(0, 3) as i:
                    step(2 * i + 1, 1)
                    step(2 * i + 2, 0)
                keep_slots(6)
                keep_c(7)
                keep_d(7, 1)
                keep_slots(7)
                act.wait_ge(s["cleared"], at["cleared"] + 1)
                for g in range(MG):
                    act.wait_ge(s["h_mm"], at["h_mm"] + g + 1)
                    for q in range(MG):
                        r = slice(MH * q, MH * q + MH)
                        nc.scalar.activation(hid_diag[r, g, :, q, :], bank[g % 2][r, 0:P].rearrange("p (b s) -> p b s", b=B), ACT.Gelu,
                                             bias=mb1[r, g:g + 1]).then_inc(s["h_gelu"], 1)

            def tensor(pe):
                if n == stages.index("m"):
                    pe.wait_ge(mix_set[0], 1)
                    pe.matmul(bank[0][:, 0:SLOTS], cst[:, C_ONE:C_ONE + P], mu_t[:, 0], start=True, stop=True).then_inc(mix_set[1], 1)
                    pe.wait_ge(mix_set[3], 1)

                def turn_tokens(b, h):
                    if later(b):
                        pe.wait_ge(s["xT_ready"], at["xT_ready"] + b)
                    pe.wait_ge(s["unit"], at["unit"] + b + 1)
                    for k in range(TB):
                        pe.transpose(bank[0][:, k * P:k * P + P], xh[:, TB * h + k, :], ident).then_inc(s["turned"], 1)

                def logits_c(b, h):
                    pe.wait_ge(s["xT_ready"], at["xT_ready"] + b + 1)
                    if later(b):
                        pe.wait_ge(s["exp_c"], at["exp_c"] + TB * b)
                    for k in range(TB):
                        last = pe.matmul(bank[2 + k // 2][:, SLOTS * (k % 2):SLOTS * (k % 2) + SLOTS], xT[:, h, k * P:k * P + P], mu[:],
                                         start=True, stop=True)
                        if k % 2:
                            last.then_inc(s["logit_c"], 1)

                def logits_d(b, h):
                    if later(b):
                        pe.wait_ge(s["exp_d"], at["exp_d"] + 2 * b)
                    for j in range(2):
                        pe.matmul(bank[4 + j][:], mu[:, j * P:j * P + P], xT[:, h, :], start=True, stop=True).then_inc(s["logit_d"], 1)

                def turn_c(b, h):
                    pe.wait_ge(s["exp_c"], at["exp_c"] + TB * b + TB)
                    for j in range(2):
                        if later(b):
                            pe.wait_ge(s[f"kept_d{j}"], at[f"kept_d{j}"] + b)
                        for k in range(TB):
                            last = pe.transpose(bank[6 + j][:, k * P:k * P + P], comb[:, h, k, j * P:j * P + P], ident)
                        last.then_inc(s[f"turn_c{j}"], 1)

                def turn_d(b, h):
                    pe.wait_ge(s["exp_d"], at["exp_d"] + 2 * b + 2)
                    for m in range(2):
                        pe.wait_ge(s[f"kept_c{m}"], at[f"kept_c{m}"] + b + 1)
                        for k in range(2):
                            for j in range(2):
                                c = SLOTS * k + P * j
                                last = pe.transpose(bank[6 + m][:, c:c + P], disp_s[:, h, j, (2 * m + k) * P:(2 * m + k + 1) * P], ident)
                        last.then_inc(s[f"turn_d{m}"], 1)

                def slots_in(b, h):
                    for m in range(2):
                        pe.wait_ge(s[f"kept_d{m}"], at[f"kept_d{m}"] + b + 1)
                    for j in range(2):
                        for k in range(TB):
                            last = pe.matmul(bank[1][:, j * D:j * D + D], disp[:, h, k, j * P:j * P + P], xn[:, bass.ds(TB * b + k, 1), :],
                                             start=(k == 0), stop=(k == TB - 1))
                    last.then_inc(s["in_mm"], 1)

                def turn_slots(b):
                    pe.wait_ge(s["in_kept"], at["in_kept"] + 2 * b + 2)
                    if later(b):
                        pe.wait_ge(s["slotT"], at["slotT"] + b)
                    for j in range(2):
                        last = pe.transpose(bank[1][:, SLOTS + j * P:SLOTS + j * P + P], slot_in[:, j, :], ident)
                    last.then_inc(s["in_turned"], 1)

                def step(b, h):
                    turn_tokens(b + 1, 1 - h)
                    if later(b):
                        turn_slots(b - 1)
                    turn_c(b, h)
                    logits_c(b + 1, 1 - h)
                    turn_d(b, h)
                    logits_d(b + 1, 1 - h)
                    slots_in(b, h)

                turn_tokens(0, 0)
                logits_c(0, 0)
                logits_d(0, 0)
                step(0, 0)
                step(1, 1)
                step(2, 0)
                with pe.Fori(1, 3) as i:
                    step(2 * i + 1, 1)
                    step(2 * i + 2, 0)
                turn_slots(6)
                turn_c(7, 1)
                turn_d(7, 1)
                slots_in(7, 1)
                turn_slots(7)
                pe.wait_ge(s["slotT"], at["slotT"] + B)
                pe.wait_ge(mixw_in, MIXW)
                for g in range(MG):
                    if g >= 2:
                        pe.wait_ge(s["h_gelu"], at["h_gelu"] + MG * (g - 1))
                    for q in range(MG):
                        last = pe.matmul(bank[g % 2][MH * q:MH * q + MH, 0:P], mw1[:, MG * g + q, :],
                                         slotT[:, MG * g + q].rearrange("p b s -> p (b s)"), start=True, stop=True)
                    last.then_inc(s["h_mm"], 1)
                for h in range(2):
                    pe.wait_ge(s["h_gelu"], at["h_gelu"] + MG * (2 * h + 2))
                    for j in range(2):
                        for b in range(4 * j, 4 * j + 4):
                            for g in (2 * h, 2 * h + 1):
                                r = 64 * (g % 2)
                                last = pe.matmul(bank[2 + 2 * h + j][r:r + 64, (b % 4) * D:(b % 4) * D + D],
                                                 hid_diag[:, g, b].rearrange("p q s -> p (q s)"), mw2[:, g, :], start=True, stop=True)
                        last.then_inc(s["out_mm"], 1)
                pe.wait_ge(s["out_kept"], at["out_kept"] + 4)
                for b in range(B):
                    if b >= 4:
                        pe.wait_ge(x_done[n + 1], TB * (b - 3))
                    for k in range(TB):
                        for j in range(2):
                            last = pe.matmul(bank[Y_BANK[b % 4]][:, k * D:k * D + D], combT[:, j, b, k * P:k * P + P], slot_out[:, j, b, :],
                                             start=(j == 0), stop=(j == 1))
                    last.then_inc(s["y_mm"], 1)

            return dict(sync=lambda sp: None, vector=vector, scalar=scalar, tensor=tensor, gpsimd=gpsimd)


        def attention(n):
            s = {k: sem(f"a{n}_{k}") for k in (
                "v normed misc_mm misc_read rope_v parts max_mm max_read exp_mm "
                "prob values sums_mm sums_read m_cut m_rows den set_ones rope_read tick".split())}
            stack_in = [sem(f"a{n}_stack_in{i}") for i in range(2)]
            m_in = [sem(f"a{n}_m_in{i}") for i in range(2)]
            at = dict.fromkeys(s, 0)
            HALF = H // 2

            STEPS = ((0, "xt"), (1, "m1"), (2, "p0"), (3, "p1"), (4, "p2"), (5, "p3"), (7, "n0"), (8, "n1"), (9, "m0"),
                     (10, "n2"), (11, "n3"), (12, "to"), (13, "wo"), (15, "v"))
            RANGE = {"x": (-1, B - 2), "p": (-1, B - 2), "m1": (1, B), "m0": (0, B - 1), "n": (2, B + 1), "t": (2, B + 1),
                     "w": (2, B + 1), "v": (0, B - 1)}

            def active(i, step):
                if not isinstance(i, int):
                    return True
                lo, hi = RANGE[step if step in RANGE else step[0]]
                return lo <= i <= hi

            before = {}
            count = 0
            for i in range(-1, B + 2):
                before[i] = count
                count += sum(active(i, step) for _, step in STEPS)

            def uses_before(i):
                return before[i] if isinstance(i, int) else before[2] + len(STEPS) * (i - 2)

            def odd_jobs(i, hh):
                base = uses_before(i)
                for k, (slot, step) in enumerate(st for st in STEPS if active(i, st[1])):
                    if slot == hh:
                        yield step, base + k

            def maxing(i):
                return not isinstance(i, int) or 0 <= i < B

            def exping(i):
                return not isinstance(i, int) or 1 <= i <= B

            def groups(i, hh):
                if hh % 4 == 1:
                    g = hh // 4 - 1
                    b = i - 1
                    if g < 0:
                        g, b = 3, i - 2
                    if not isinstance(i, int) or 0 <= b < B:
                        yield b, g, 4 * b + g

            UNITS = {}
            for hh in range(H):
                UNITS[hh] = [("a", hh, hh + hh // 2)]
                if hh % 2:
                    UNITS[hh].append(("b", hh, hh + hh // 2 + 1))
            N_UNITS = H + H // 2

            def turns(engine, body):
                for i in (-1, 0, 1):
                    body(i, i % 2)
                with engine.Fori(1, 3) as r:
                    for par in range(2):
                        body(2 * r + par, par)
                for i in range(6, B + 2):
                    body(i, i % 2)

            def tensor(pe):
                pe.wait_ge(att_w, 1)

                def step_(i, par, step, m):
                    nxt = 1 - par
                    to = bank[7]
                    if m is not None and not (isinstance(m, int) and m == 0):
                        pe.wait_ge(s["misc_read"], m)
                    if step == "xt":
                        for k in range(TB):
                            pe.wait_ge(s["normed"], TB * (i + 1) + k + 1)
                            last = pe.transpose(to[:, k * P:k * P + P], xh[:, 4 * nxt + k, :], ident)
                    elif step[0] == "p":
                        last = pe.matmul(to[:], wqk[:, int(step[1]), :], xT[:, nxt, :], start=True, stop=True)
                    elif step == "v":
                        for k in range(TB):
                            last = pe.matmul(to[:, k * P:k * P + P], xT[:, par, k * P:k * P + P], wqkv[:, 2 * D:], start=True, stop=True)
                    elif step[0] == "m":
                        half = int(step[1])
                        pe.wait_ge(s["m_cut"], 2 * i + 1 if half == 0 else 2 * i)
                        for k in range(TB):
                            last = pe.transpose(to[0:3 * HALF, :].bitcast(BF16)[:, k * P:k * P + P],
                                                m_cut[:, half, k].rearrange("p c h -> p (c h)"), ident_bf[:])
                    elif step[0] == "n":
                        pe.wait_ge(s["sums_read"], TB * (i - 1))
                        k = int(step[1])
                        for g in range(TB):
                            last = pe.transpose(to[:, g * P:g * P + P], o_t[par][:, g, k * P:k * P + P], ident)
                    elif step == "to":
                        for k in range(TB):
                            last = pe.transpose(to[:, k * P:k * P + P], o_tok[:, k, :], ident)
                    elif step == "wo":
                        for k in range(TB):
                            last = pe.matmul(to[:, k * P:k * P + P], o_hd[:, k * P:k * P + P], wout[:], start=True, stop=True)
                    last.then_inc(s["misc_mm"], 1)

                def maxima(i, par, hh):
                    half = hh // HALF
                    if hh % HALF == 0:
                        pe.wait_ge(stack_in[half], 16 * 2 * len(Q_PART) * (i + 1))
                    for unit, blocks in enumerate(((3,), (2, 0), (1,))):
                        number = 3 * (H * i + hh) + unit
                        to = bank[number % 2 if isinstance(i, int) else (3 * hh + unit) % 2]
                        if not (isinstance(i, int) and number < 2):
                            pe.wait_ge(s["max_read"], number - 1)
                        for col, k in zip((0, 3 * P), blocks):
                            n_keys = (k + 1) * P
                            pe.matmul(to[:, col:col + n_keys], q_stack[par][0:STACK, hh, k * P:k * P + P], k_stack[par][0:STACK, hh, 0:n_keys],
                                      start=True, stop=False)
                            last = pe.matmul(to[:, col + k * P:col + n_keys], ident_bf[:], mask_q[:], start=False, stop=True)
                        last.then_inc(s["max_mm"], 1)

                def exponents(i, par, hh):
                    prev = 1 - par
                    rows = STACK + 3
                    if hh % HALF == 0:
                        pe.wait_ge(m_in[hh // HALF], 16 * i)
                    for kind, h, u in UNITS[hh]:
                        number = N_UNITS * (i - 1) + u
                        b0 = 2 + 2 * (u % 2)
                        if not (isinstance(i, int) and number < 2):
                            pe.wait_ge(s["prob"], number - 1)
                        for head, k, to in (((h, 0, bank[b0][:]), (h, 1, bank[b0 + 1][:, 0:3 * P]), (h, 3, bank[b0 + 1][:, 3 * P:])) if kind == "a"
                                            else ((h - 1, 2, bank[b0][:, 0:2 * P]), (h, 2, bank[b0][:, 2 * P:]))):
                            pe.matmul(to, k_stack[prev][0:rows, head, k * P:k * P + P], q_stack[prev][0:rows, head, k * P:], start=True, stop=False)
                            last = pe.matmul(to[:, 0:P], ident_bf[:], mask_k[:], start=False, stop=True)
                        last.then_inc(s["exp_mm"], 1)

                def sums(b, g, number, vpar):
                    pe.wait_ge(s["prob"], N_UNITS * b + 6 * g + 6)
                    pe.wait_ge(s["values"], b + 1)
                    if later(number):
                        pe.wait_ge(s["sums_read"], number)
                    for k in range(TB):
                        for j in range(4):
                            last = pe.matmul(bank[6][32 * j:32 * j + 32, k * P:], v_aug[vpar][:, k, 4 * g + j, :],
                                             prob_e[g % 2][:, j, E_AT[k]:E_AT[k] + S - k * P], start=(k == 0), stop=(k == TB - 1))
                    last.then_inc(s["sums_mm"], 1)

                def body(i, par):
                    for hh in range(H):
                        if maxing(i):
                            maxima(i, par, hh)
                        if exping(i):
                            exponents(i, par, hh)
                        for b, g, number in groups(i, hh):
                            sums(b, g, number, par if g == 3 else 1 - par)
                        for step, m in odd_jobs(i, hh):
                            step_(i, par, step, m)

                turns(pe, body)

            def vector(dve):
                chain = Chain(dve, s["v"])
                if n == stages.index("a"):
                    dve.wait_ge(attw_in, 48)
                    nc.vector.tensor_copy(ident_bf[:], ident)
                    nc.vector.tensor_copy(mask_q[:], rot[:, R_MQ:R_MQ + P])
                    nc.vector.tensor_copy(mask_k[:], rot[:, R_MK:R_MK + P])
                    for m in range(2):
                        w = wqkv[:, m * D:m * D + D].rearrange("p (a h d) -> p a d h", a=2, d=DH)
                        to = [wqk[:, 2 * m + r, :].rearrange("p (a d h) -> p a d h", a=2, d=DH) for r in range(2)]
                        lo, hi = slice(0, DH // 2), slice(DH // 2, DH)
                        for half in range(2):
                            nc.vector.tensor_copy(to[0][:, half], w[:, half])
                            nc.vector.tensor_scalar(to[1][:, half, lo], w[:, half, hi], -1.0, None, ALU.mult)
                            last = nc.vector.tensor_copy(to[1][:, half, hi], w[:, half, lo])
                    last.then_inc(att_w, 1)

                def body(i, par):
                    for hh in range(H):
                        if maxing(i):
                            for unit, blocks in enumerate(((3,), (2, 0), (1,))):
                                number = 3 * (H * i + hh) + unit
                                frm = bank[number % 2 if isinstance(i, int) else (3 * hh + unit) % 2]
                                dve.wait_ge(s["max_mm"], number + 1)
                                for col, k in zip((0, 3 * P), blocks):
                                    last = nc.vector.tensor_reduce(neg_m[:, par, k, hh:hh + 1], frm[:, col:col + (k + 1) * P], AX.X, ALU.max, negate=True)
                                last.then_inc(s["max_read"], 1)
                            if hh % HALF == HALF - 1:
                                half = hh // HALF
                                dve.wait_ge(s["max_read"], 3 * (H * i + hh) + 3)
                                v = neg_m[:, par, :, HALF * half:HALF * half + HALF]
                                c = [m_cut[:, half, :, r, :] for r in range(3)]
                                for op in ((c[0], v), (m_left[:], v, c[0]), (c[1], m_left[:]), (c[2], m_left[:], c[1])):
                                    if len(op) == 2:
                                        ins = nc.vector.tensor_copy(*op)
                                    else:
                                        ins = nc.vector.tensor_tensor(*op, ALU.subtract)
                                    last = ins.then_inc(s["den"], 1)
                                    den_count[0] += 1
                                    dve.wait_ge(s["den"], den_at(i))
                                dve.sem_inc(s["m_cut"], 1)
                        for step, m in odd_jobs(i, hh):
                            if step[0] == "m":
                                half = int(step[1])
                                dve.wait_ge(s["misc_mm"], m + 1)
                                prior = (i - 1 if half else i)
                                if not (isinstance(prior, int) and prior < 1):
                                    dve.wait_ge(m_in[half], 16 * prior)
                                nc.vector.tensor_copy(m_rows[:, half, :], bank[7][0:3 * HALF, :].bitcast(BF16)[:, 0:S]).then_inc(s["m_rows"], 1)
                                dve.wait_ge(s["m_rows"], rows_count(i, half))
                                dve.sem_inc(s["misc_read"], 1)
                            elif step[0] == "n":
                                k = int(step[1])
                                dve.wait_ge(s["misc_mm"], m + 1)
                                got = bank[7][:].rearrange("p (h c) -> p h c", c=32)
                                nc.vector.reciprocal(o_den[:], got[:, :, DH]).then_inc(s["den"], 1)
                                den_count[0] += 1
                                dve.wait_ge(s["den"], den_at(i))
                                nc.vector.tensor_tensor(o_tok[:, k, :].rearrange("p (h c) -> p h c", c=DH), got[:, :, 0:DH],
                                                        o_den[:].unsqueeze(2).to_broadcast([P, H, DH]), ALU.mult).then_inc(s["misc_read"], 1)
                            elif step == "wo":
                                dve.wait_ge(s["misc_mm"], m + 1)
                                tiles = x[:, bass.ds(TB * (i - 2), TB), :]
                                nc.vector.tensor_tensor(tiles, tiles, bank[7][:].rearrange("p (k d) -> p k d", k=TB), ALU.add).then_inc(x_done[n + 1], TB)
                                dve.wait_ge(x_done[n + 1], TB * (i - 1))
                                dve.sem_inc(s["misc_read"], 1)

                den_count = [0]
                den_base = {}

                def den_at(i):
                    if isinstance(i, int):
                        return den_count[0]
                    return den_count[0] + 24 * (i // 2 - 1) if False else den_loop(i)

                def den_loop(i):
                    return loop_den[0] + den_count[0] - loop_den[1]

                def rows_count(i, half):
                    return 2 * i if half else 2 * i + 1

                loop_den = [0, 0]

                def turns_v():
                    for i in (-1, 0, 1):
                        body(i, i % 2)
                    with dve.Fori(1, 3) as r:
                        loop_den[1] = den_count[0]
                        loop_den[0] = den_count[0] + 24 * (r - 1)
                        for par in range(2):
                            body(2 * r + par, par)
                        assert den_count[0] - loop_den[1] == 24
                    den_count[0] += 24
                    for i in range(6, B + 2):
                        if i == B + 1:
                            for g in range(GROUPS - 1):
                                stats_after(dve, n + 1, g)
                        body(i, i % 2)
                    stats_after(dve, n + 1, GROUPS - 1)

                turns_v()

            def scalar(act):
                for g in range(GROUPS):
                    stats_root(act, n, g)
                act.wait_ge(ready_sem, GROUPS * n + GROUPS)

                def body(i, par):
                    if i == B + 1 if isinstance(i, int) else False:
                        for g in range(GROUPS - 1):
                            stats_root(act, n + 1, g)
                    nxt = 1 - par
                    for hh in range(H):
                        if hh == 0 and active(i, "xt"):
                            if not (isinstance(i, int) and i < 1):
                                act.wait_ge(s["misc_mm"], uses_before(i) - 1)
                            for k in range(TB):
                                t = bass.ds(TB * (i + 1) + k, 1)
                                nc.scalar.activation(xh[:, 4 * nxt + k, :], x[:, t, :], ACT.Identity, bias=shift_by[:, t],
                                                     scale=rstd[:, t]).then_inc(s["normed"], 1)
                        if exping(i):
                            for kind, h, u in UNITS[hh]:
                                number = N_UNITS * (i - 1) + u
                                b0 = 2 + 2 * (u % 2)
                                g = hh // 4
                                if hh % 4 == 0 and kind == "a" and not (isinstance(i, int) and 4 * (i - 1) + g - 1 < 1):
                                    act.wait_ge(s["sums_mm"], 4 * (i - 1) + g - 1)
                                act.wait_ge(s["exp_mm"], number + 1)
                                if kind == "a":
                                    frm = psum_pair[u % 2]
                                    to = prob_e[g % 2][:, h % 4, 0:2 * S]
                                else:
                                    frm = bank[b0][:].rearrange("p (h c) -> p h c", h=2)
                                    to = prob_e[g % 2][:, h % 4 - 1:h % 4 + 1, E_AT[2]:E_AT[2] + 2 * P]
                                nc.scalar.activation(to, frm, ACT.Exp, scale=DH ** -0.5).then_inc(s["prob"], 1)
                        for b, g, number in groups(i, hh):
                            vpar = par if g == 3 else 1 - par
                            act.wait_ge(s["sums_mm"], number + 1)
                            nc.scalar.copy(o_t[vpar][:, g, :], bank[6][:]).then_inc(s["sums_read"], 1)
                        for step, m in odd_jobs(i, hh):
                            if step == "xt":
                                act.wait_ge(s["misc_mm"], m + 1)
                                nc.scalar.copy(xT[:, nxt, :], bank[7][:]).then_inc(s["misc_read"], 1)
                            elif step[0] == "p":
                                r = int(step[1])
                                act.wait_ge(s["misc_mm"], m + 1)
                                if r >= 2 or not (isinstance(i, int) and i < 0):
                                    act.wait_ge(s["rope_read"], 2 * (i + 1) + r // 2)
                                nc.scalar.copy(raw[:, r % 2, :], bank[7][:]).then_inc(s["misc_read"], 1)
                            elif step == "v":
                                act.wait_ge(s["misc_mm"], m + 1)
                                act.wait_ge(s["set_ones"], 1)
                                nc.scalar.copy(v_aug[par][:, :, :, 0:DH], bank[7][:].rearrange("p (k h d) -> p k h d", k=TB, h=H)).then_inc(s["values"], 1)
                                act.wait_ge(s["values"], i + 1)
                                act.sem_inc(s["misc_read"], 1)
                            elif step == "to":
                                act.wait_ge(s["misc_mm"], m + 1)
                                nc.scalar.copy(o_hd[:], bank[7][:]).then_inc(s["misc_read"], 1)

                turns(act, body)

            def gpsimd(pool):
                if n:
                    pool.wait_ge(x_done[n], T)
                pool.wait_ge(zeroed, 2)
                setup = Chain(pool, s["rope_v"])
                for i in range(2):
                    setup(pool.memset(k_stack[i][32:64].rearrange("p h t -> p (h t)").bitcast(F32), ONE_ONE))
                    setup(pool.memset(v_aug[i][:], 0.0))
                    setup(pool.memset(v_aug[i][:, :, :, DH:DH + 1], 1.0))
                pool.sem_inc(s["set_ones"], 1)
                pool.wait_ge(attw_in, 48)
                t0, t1 = rope[:, 0, :], rope[:, 1, :]

                def rotate(b):
                    for m in range(2):
                        part = [cut[:, m, r, :] for r in range(3)]
                        done = 14 * b + 7 * m + 2
                        first = uses_before(b - 1)
                        off = [k for k, st in enumerate(x for x in STEPS if active(b - 1, x[1])) if st[1] == f"p{2 * m + 1}"][0]
                        pool.wait_ge(s["misc_read"], first + off + 1)
                        pool.tensor_tensor(t0, raw[:, 0, :], cos, ALU.mult).then_inc(s["rope_v"], 1)
                        pool.tensor_tensor(t1, raw[:, 1, :], sin, ALU.mult).then_inc(s["rope_v"], 1)
                        pool.wait_ge(s["rope_v"], setup.n + done)
                        pool.sem_inc(s["rope_read"], 1)
                        pool.tensor_tensor(t0, t0, t1, ALU.add).then_inc(s["rope_v"], 1)
                        pool.wait_ge(s["rope_v"], setup.n + done + 1)
                        if m == 0 and not (isinstance(b, int) and b < 1):
                            for half in range(2):
                                pool.wait_ge(stack_in[half], 16 * 2 * len(Q_PART) * b)
                        pool.sem_inc(s["tick"], 1)
                        pool.tensor_copy(part[0], t0).then_inc(s["rope_v"], 1)
                        pool.wait_ge(s["rope_v"], setup.n + done + 2)
                        pool.tensor_tensor(t1, t0, part[0], ALU.subtract).then_inc(s["rope_v"], 1)
                        pool.wait_ge(s["rope_v"], setup.n + done + 3)
                        pool.sem_inc(s["tick"], 1)
                        pool.tensor_copy(part[1], t1).then_inc(s["rope_v"], 1)
                        pool.wait_ge(s["rope_v"], setup.n + done + 4)
                        pool.tensor_tensor(part[2], t1, part[1], ALU.subtract).then_inc(s["rope_v"], 1)
                        pool.wait_ge(s["rope_v"], setup.n + done + 5)
                    pool.sem_inc(s["parts"], 1)

                for b in range(3):
                    rotate(b)
                with pool.Fori(3, 7) as b:
                    rotate(b)
                rotate(7)

            def sync(sp):
                sp.wait_ge(s["set_ones"], 1)

                def maximum(b, par, half):
                    sp.wait_ge(s["m_rows"], 2 * b + 1 + half)
                    sp.dma_start(q_stack[par][STACK:STACK + 3, HALF * half:HALF * half + HALF, :], m_rows[:, half, :]).then_inc(m_in[half], 16)

                def stack(b, par, half):
                    if half == 0:
                        sp.wait_ge(s["parts"], b + 1)
                    if not (isinstance(b, int) and b < 2):
                        sp.wait_ge(s["exp_mm"], N_UNITS * (b - 2) + N_UNITS // 2 * (half + 1))
                    for r in range(len(Q_PART)):
                        for m, to, part in ((0, q_stack, Q_PART), (1, k_stack, K_PART)):
                            sp.dma_start(to[par][DH * r:DH * r + DH, HALF * half:HALF * half + HALF, :],
                                         cut[64 * half:64 * half + 64, m, part[r], :]).then_inc(stack_in[half], 16)

                def body(i, par):
                    if not isinstance(i, int) or 1 <= i <= B:
                        maximum(i - 1, 1 - par, 1)
                    if maxing(i):
                        maximum(i, par, 0)
                    if active(i, "xt"):
                        for half in range(2):
                            stack(i + 1, 1 - par, half)

                turns(sp, body)

            return dict(sync=sync, vector=vector, scalar=scalar, tensor=tensor, gpsimd=gpsimd)

        kinds = {"f": ffn, "s": scan, "m": mix, "a": attention}
        parts = [kinds[k](n) for n, k in enumerate(stages)]
        block = ctx.enter_context(nc.Block())

        @block.sync
        def _(sp):
            load_sync(sp)
            for part in parts:
                part["sync"](sp)
            to = out.rearrange("b (k p) d -> p (b k) d", p=P)
            for g in range(GROUPS):
                sp.wait_ge(x_done[len(stages)], GT * g + GT)
                sp.dma_start(to[:, GT * g:GT * g + GT, :], x[:, GT * g:GT * g + GT, :]).then_inc(stored_out, 16)
            sp.wait_ge(stored_out, 16 * GROUPS)

        @block.scalar
        def _(act):
            load_scalar(act)
            for part in parts:
                part["scalar"](act)

        @block.vector
        def _(dve):
            setup_vector(dve, Chain(dve, sem("setup_v")))
            for g in range(GROUPS):
                stats_after(dve, 0, g)
            for part in parts:
                part["vector"](dve)

        @block.gpsimd
        def _(pool):
            setup_gpsimd(pool)
            for part in parts:
                part["gpsimd"](pool)

        @block.tensor
        def _(pe):
            setup_tensor(pe)
            for part in parts:
                part["tensor"](pe)


STAGES = "fsfmam"


def kernel(**inputs):
    import concourse.bacc as bacc
    from concourse.bass_utils import run_bass_kernel_spmd

    nc = bacc.Bacc("TRN2", target_bir_lowering=False, num_devices=1)
    arrays = {f"in_{k}": np.ascontiguousarray(v) for k, v in inputs.items()}
    arrays["in_consts"] = shape_constants()
    arrays["in_rotary"] = rotary_constants()
    ap = {k: nc.dram_tensor(k, v.shape, F32, kind="ExternalInput").ap() for k, v in arrays.items()}
    out = nc.dram_tensor("out", (B, S, D), F32, kind="ExternalOutput").ap()
    xhat_dram = nc.dram_tensor("xhat_rows", (B * S, D), F32).ap()
    yrow_dram = nc.dram_tensor("result_rows", (B * S, D), F32).ap()
    build(nc, {k[3:]: v for k, v in ap.items()}, ap["in_consts"], ap["in_rotary"], out, xhat_dram, yrow_dram, STAGES)
    return run_bass_kernel_spmd(nc, [arrays], core_ids=[0]).results[0]["out"]
```

```python
from contextlib import ExitStack

import concourse.bass as bass
import numpy as np
from concourse import mybir

F32 = mybir.dt.float32
BF16 = mybir.dt.bfloat16
I32 = mybir.dt.int32
ALU = mybir.AluOpType
ACT = mybir.ActivationFunctionType
AX = mybir.AxisListType

P = 128
B, S, D = 8, 512, 128
T = B * S // P
TB = S // P
N = 32
NJ = P // N
LEVELS = 9
E, F = 8, 512
FC = F // P
ROWS = T + E - 1
ME, MS, MH = 16, 16, 32
SLOTS = ME * MS
MG = P // MH
H, DH = 16, 8
Q_PART, K_PART = (0, 0, 1, 0, 2, 1), (0, 1, 0, 2, 0, 1)
STACK = DH * len(Q_PART)
E_AT = (0, 512, 1024, 896)
E_LEN = 1280
BIG = 1e30
ONE_ONE = float(np.array([0x3F803F80], np.uint32).view(np.float32)[0])
AHEAD = 6
ROUND = AHEAD
ROUNDS = (ROWS - 3) // ROUND
NOWHERE = 8192
EPS = 1e-5

C_ID, C_EM, C_TILE, C_TCOL, C_P1, C_TRI, C_IOTA, C_ONE = 0, 128, 384, 423, 455, 456, 584, 712
C_ALL = C_ONE + 256
R_COS, R_SIN, R_MQ, R_MK, R_ALL = 0, S, 2 * S, 2 * S + P, 2 * S + 2 * P


def shape_constants():
    c = np.zeros((P, C_ALL), np.float32)
    p = np.arange(P)
    c[:, C_ID:C_ID + P] = np.eye(P)
    c[:, C_EM:C_EM + E * T] = np.repeat(np.arange(E) - E, T)
    c[:, C_TILE:C_TILE + ROWS] = np.arange(ROWS)
    c[:, C_TCOL:C_TCOL + T] = np.arange(T)
    c[:, C_P1] = p + 1
    c[:, C_TRI:C_TRI + P] = p[:, None] < p[None, :]
    c[:, C_IOTA:C_IOTA + P] = p
    c[:, C_ONE:C_ONE + 256] = 1.0
    return c


def rotary_constants():
    c = np.zeros((P, R_ALL), np.float32)
    inv_freq = (1.0 / np.float32(10000.0) ** (np.arange(0, DH, 2, dtype=np.float32) / DH)).astype(np.float32)
    freqs = np.arange(S, dtype=np.float32)[None, :] * inv_freq[:, None]
    dim = (np.arange(P) // (H // 2)) % DH % (DH // 2)
    c[:, R_COS:R_COS + S] = np.cos(freqs)[dim]
    upper = (np.arange(P) // (H // 2)) % DH >= DH // 2
    c[:, R_SIN:R_SIN + S] = np.sin(freqs)[dim] * np.where(upper, 1, -1)[:, None]
    p = np.arange(P)
    c[:, R_MQ:R_MQ + P] = np.where(p[None, :] > p[:, None], -BIG, 0)
    c[:, R_MK:R_MK + P] = np.where(p[:, None] > p[None, :], -BIG, 0)
    return c


def later(i):
    return not isinstance(i, int) or i > 0


def peeled(engine, start, stop, body):
    body(start)
    with engine.Fori(start + 1, stop) as i:
        body(i)


class Chain:

    def __init__(self, engine, sem, n=0):
        self.engine, self.sem, self.n = engine, sem, n
        self.shift = 0

    def mark(self, instruction):
        instruction.then_inc(self.sem, 1)
        self.n += 1

    def sync(self):
        self.engine.wait_ge(self.sem, self.n + self.shift)

    def __call__(self, instruction):
        self.mark(instruction)
        self.sync()


def build(nc, a, consts, rotary, out, xhat_dram, yrow_dram, stages):
    ctx = ExitStack()
    with ctx:
        def sb(name, shape, dt=F32):
            return ctx.enter_context(nc.sbuf_tensor(name, shape, dt))

        def sem(name):
            return ctx.enter_context(nc.semaphore(name))

        psum = ctx.enter_context(nc.psum_tensor("psum", [P, 8 * 512], F32))
        bank = [psum[:, 512 * i:512 * i + 512] for i in range(8)]
        psum_pair = [psum[:, 1024 * i + 1024:1024 * i + 2048] for i in range(2)]

        x = sb("x", [P, T, D])
        cst = sb("cst", [P, C_ALL])
        ident = cst[:, C_ID:C_ID + P]
        tri = sb("tri", [P, P], BF16)
        ones_bf = sb("ones_bf", [P, P], BF16)
        iota_bf = sb("iota_bf", [P, P], BF16)
        half_stats = sb("half_stats", [P, T, 6])
        st = sb("st", [P, 10, T])
        mean, rstd, shift_by = st[:, 0, :], st[:, 1, :], st[:, 9, :]
        xh = sb("xh", [P, 8, D])
        xT = sb("xT", [P, 2, S])

        arena = sb("arena", [P, 2 * B * S])
        arena2 = sb("arena2", [P, 10752])
        arena3 = sb("arena3", [P, 2 * TB * E_LEN])
        arena4 = sb("arena4", [P, 8192])

        def carve(area, at, shape, dt=F32):
            n = int(np.prod(shape)) * (2 if dt == BF16 else 4) // 4
            v = area[:, at:at + n]
            if dt != F32:
                v = v.bitcast(dt)
            names = "abcde"[:len(shape)]
            return v.rearrange(f"p ({' '.join(names)}) -> p {' '.join(names)}", **dict(zip(names[1:], shape[1:]))) if len(shape) > 1 else v

        w1 = arena2[:, 0:4096].rearrange("p (e f) -> p e f", e=E)
        w2 = arena2[:, 4096:8192].rearrange("p (e c d) -> p e c d", e=E, c=FC)
        b2rows = arena2[:, 10240:10752].bitcast(BF16)
        ones3 = sb("ones3", [P, P], BF16)
        BN = E * D // P
        bsplit = carve(arena4, 6100, (2, BN))
        bparts = carve(arena4, 6228, (3, BN), BF16)
        gate_b1T = sb("gate_b1T", [P, E + E * FC])
        gateT, b1T = gate_b1T[:, 0:E], gate_b1T[:, E:]
        b1_quarters = arena4[0:E * FC, 6528:6528 + P]
        gate_rows = arena4[0:E, 6400:6400 + D]
        r_log = carve(arena4, 0, (E, T))
        r_exp = carve(arena4, 256, (E, T))
        r_eq = carve(arena4, 512, (E, T))
        r_one = carve(arena4, 768, (E, T))
        r_onebf = carve(arena4, 5840, (E, T), BF16)
        r_tot = carve(arena4, 1024, (E, T))
        r_scan = carve(arena4, 1280, (E, T))
        r_t = carve(arena4, 1536, (8, T))
        r_e = sb("r_e", [P, 8, E])
        r_ti = sb("r_ti", [P, 3, T], I32)
        r_ei = sb("r_ei", [P, 2, E], I32)
        expert_cmp = carve(arena4, 5248, (ROWS, E))[0:1]
        expert_f = sb("expert_f", [1, ROWS])
        expert_of = sb("expert_of", [1, ROWS], I32)
        lane_hot = arena[:, 4096:6144].bitcast(BF16).rearrange("p (t l) -> p t l", t=T)
        tile_hot = arena[:, 6144:6144 + 3 * T * ROWS // 2].bitcast(BF16).rearrange("p (m t r) -> p m t r", m=3, t=T)
        inv = arena4[:, 5600:5600 + 2 * ROWS]
        inv_v = carve(arena4, 5700, (3, ROWS))
        gather_row = sb("gather_row", [P, ROWS], I32)
        scatter_row = sb("scatter_row", [P, ROWS], I32)
        xg = carve(arena4, 1792, (AHEAD, D))
        xgT = carve(arena4, 2560, (2, P))
        hid = carve(arena4, 2816, (2, F))
        hidT = carve(arena4, 3840, (2, FC, P))
        yg = carve(arena4, 4864, (3, D))
        yback = arena[:, 0:T * D].rearrange("p (t d) -> p t d", t=T)

        win_rows = arena3[0:N, 9600:9728]
        win_z = carve(arena3, 8448, (NJ, P))
        bm_rows = carve(arena3, 9472, (NJ, N))[0:N]
        bm_diag = arena3[:, 9216:9344]
        c_rows = carve(arena3, 9344, (NJ, N))
        c_diag = carve(arena3, 7936, (NJ, D))
        b_in = sb("b_in", [P, 1])
        d_rep = arena3[:, 9728:9856]
        a_pow = carve(arena3, 6144, (LEVELS, 64 + P))
        a_powT = carve(arena3, 8960, (2, P))
        u1 = carve(arena, 0, (B, P))
        state = carve(arena, 1024, (B, P))

        mu = sb("mu", [P, SLOTS])
        mu_t = carve(arena, 0, (2, SLOTS))
        gamma = sb("gamma", [P, D])
        beta = sb("beta", [P, D])
        mscale = sb("mscale", [P, 1])
        mw1 = sb("mw1", [P, ME, MH])
        mw2 = sb("mw2", [P, MG, D])
        mb1 = sb("mb1", [P, MG])
        mb2 = sb("mb2", [P, 2, D])
        xn = carve(arena3, 0, (T, D))
        square = carve(arena4, 0, (8, D))
        comb = arena2[:, 0:2048].rearrange("p (h k s) -> p h k s", h=2, k=TB)
        disp_s = arena2[:, 2048:4096].rearrange("p (h j t) -> p h j t", h=2, j=2)
        combT = arena[:].rearrange("p (h b t) -> p h b t", h=2, b=B)
        disp = arena2[:, 4096:6144].rearrange("p (h k s) -> p h k s", h=2, k=TB)
        slot_in = carve(arena2, 10240, (2, D))
        slotT = arena2[:, 6144:8192].rearrange("p (e b s) -> p e b s", e=ME, b=B)
        hid_diag = carve(arena3, 4096, (MG, B, MG, MS))
        slot_out = arena2[:, 8192:10240].rearrange("p (h b d) -> p h b d", h=2, b=B)
        neg_c = sb("neg_c", [P, B, TB])
        neg_d = sb("neg_d", [P, B, 2])
        sum_c = sb("sum_c", [P, T])
        inv_c = sb("inv_c", [P, T])
        sum_d = sb("sum_d", [P, B, 2])
        inv_d = sb("inv_d", [P, B, 2])

        rot = sb("rot", [P, R_ALL])
        cos, sin = rot[:, R_COS:R_COS + S], rot[:, R_SIN:R_SIN + S]
        mask_q = sb("mask_q", [P, P], BF16)
        mask_k = sb("mask_k", [P, P], BF16)
        ident_bf = sb("ident_bf", [P, P], BF16)
        wqkv = sb("wqkv", [P, 3 * D])
        wqk = sb("wqk", [P, 2, P])
        wout = sb("wout", [P, D])
        q_stack = [carve(arena, 4096 * i, (H, S), BF16) for i in range(2)]
        k_stack = [carve(arena2, 4096 * i, (H, S), BF16) for i in range(2)]
        prob_e = [carve(arena3, TB * E_LEN * i, (TB, E_LEN)) for i in range(2)]
        v_aug = [carve(arena4, 2048 * i, (TB, H, 32)) for i in range(2)]
        o_t = [carve(arena4, 4096 + 2048 * i, (TB, S)) for i in range(2)]
        raw = sb("raw", [P, 2, S])
        swapped = carve(arena2, 8192, (2, S))
        cut = sb("cut", [P, 2, 3, S], BF16)
        neg_m = sb("neg_m", [P, 2, TB, H])
        m_left = sb("m_left", [P, TB, DH])
        m_cut = sb("m_cut", [P, 2, TB, 3, H // 2], BF16)
        m_rows = carve(arena2, 10240, (2, S), BF16)[0:3 * H // 2]
        o_den = sb("o_den", [P, H])
        o_tok = carve(arena2, 9216, (TB, D))
        o_hd = arena2[:, 9728:9728 + S]
        attw_in, att_w = sem("attw_in"), sem("att_w")

        mixw_in, mix_set = sem("mixw_in"), [sem(f"mix_set{i}") for i in range(4)]
        x_in = [sem(f"x_in{i}") for i in range(4)]
        cst_in, w1_in, w2_in, bias_in, biasrow_in = (sem(n) for n in (
            "cst_in", "w1_in", "w2_in", "bias_in", "biasrow_in"))
        gate_in, scanw_in, a_in = sem("gate_in"), sem("scanw_in"), sem("a_in")
        bf_ready, zeroed, bias_cut, turned_w, placed_w = (sem(n) for n in (
            "bf_ready", "zeroed", "bias_cut", "turned_w", "placed_w"))
        pow_mm, pow_kept, scan_kept = sem("pow_mm"), sem("pow_kept"), sem("scan_kept")
        stored_out, rows_zeroed = sem("stored_out"), sem("rows_zeroed")
        x_done = [sem(f"x_done{i}") for i in range(len(stages) + 1)]

        def loads_for_later(sp):
            sp.dma_start(rot[:], rotary).then_inc(attw_in, 16)
            sp.dma_start(wqkv[:], a["L1_attn_w_qkv"]).then_inc(attw_in, 16)
            sp.dma_start(wout[:], a["L1_attn_w_out"]).then_inc(attw_in, 16)
            sp.dma_start(mu[:], a["L1_ffn_mu"].rearrange("d e s -> d (e s)")).then_inc(mixw_in, 16)
            sp.dma_start(gamma[:], a["L1_ffn_ln_gamma"].partition_broadcast(P)).then_inc(mixw_in, 16)
            sp.dma_start(beta[:], a["L1_ffn_ln_beta"].partition_broadcast(P)).then_inc(mixw_in, 16)
            sp.dma_start(mscale[:], a["L1_ffn_scale"].partition_broadcast(P)).then_inc(mixw_in, 16)
            sp.dma_start(mw1[:], a["L1_ffn_w1"].rearrange("e d h -> d e h")).then_inc(mixw_in, 16)
            for q in range(MG):
                sp.dma_start(mw2[MH * q:MH * q + MH], a["L1_ffn_w2"].rearrange("(g q) h d -> q h g d", q=MG)[q]).then_inc(mixw_in, 16)
                sp.dma_start(mb1[MH * q:MH * q + MH], a["L1_ffn_b1"].rearrange("(g q) h -> q h g", q=MG)[q],
                             allow_slow_non_contiguous=True).then_inc(mixw_in, 16)
            for e in range(ME):
                h, r = e // 8, MS * (e % 8)
                sp.dma_start(mb2[r:r + MS, h, :], a["L1_ffn_b2"][e].partition_broadcast(MS)).then_inc(mixw_in, 16)

        def load_sync(sp):
            xin = a["L0_attn_x"].rearrange("b (k p) d -> p (b k) d", p=P)
            for i in range(4):
                sp.dma_start(x[:, 8 * i:8 * i + 8, :], xin[:, 8 * i:8 * i + 8, :]).then_inc(x_in[i], 16)
            sp.dma_start(bsplit[:, 0, :], a["L0_ffn_b2"].rearrange("e f -> (e f)").rearrange("(p i) -> p i", p=P)).then_inc(bias_in, 16)

        def late_loads(sp):
            sp.dma_start(w1[:], a["L0_ffn_w1"].rearrange("e d f -> d e f")).then_inc(w1_in, 16)
            sp.dma_start(w2[:], a["L0_ffn_w2"].rearrange("e (c f) d -> f e c d", f=P)).then_inc(w2_in, 16)
            sp.wait_ge(bias_cut, 1)
            sp.wait_ge(rows_zeroed, 1)
            for r in range(3):
                sp.dma_start(b2rows[r:r + 1, :], bparts[:, r, :]).then_inc(biasrow_in, 16)
            loads_for_later(sp)

        def load_scalar(act):
            act.dma_start(cst[:], consts).then_inc(cst_in, 16)
            act.dma_start(gate_rows[:], a["L0_ffn_gate_w"]).then_inc(gate_in, 16)
            act.dma_start(b1_quarters[:], a["L0_ffn_b1"].rearrange("e (c f) -> (e c) f", f=P)).then_inc(gate_in, 16)
            act.dma_start(win_rows[:], a["L0_attn_W_in"]).then_inc(scanw_in, 16)
            for j in range(NJ):
                act.dma_start(bm_rows[:, j, :], a["L0_attn_Bm"]).then_inc(scanw_in, 16)
                act.dma_start(c_rows[:, j, :], a["L0_attn_C"]).then_inc(scanw_in, 16)
                act.dma_start(b_in[N * j:N * j + N, :], a["L0_attn_b_in"].rearrange("(n o) -> n o", o=1)).then_inc(scanw_in, 16)
            act.dma_start(d_rep[:], a["L0_attn_D"].partition_broadcast(P)).then_inc(scanw_in, 16)
            act.wait_ge(zeroed, 1)
            for j in range(NJ):
                act.dma_start(a_pow[N * j:N * j + N, 0, 64 + N * j:64 + N * j + N], a["L0_attn_A"]).then_inc(a_in, 16)
            act.wait_ge(turned_w, 1)
            nc.scalar.copy(gate_b1T[:], bank[0][:, 0:E + E * FC]).then_inc(placed_w, 1)

        def setup_gpsimd(pool):
            pool.memset(a_pow[:], 0.0).then_inc(zeroed, 1)
            pool.memset(win_z[:], 0.0)
            pool.memset(bm_diag[:], 0.0)
            pool.memset(c_diag[:], 0.0).then_inc(zeroed, 1)
            pool.memset(b2rows[:], 0.0).then_inc(rows_zeroed, 1)

        def setup_vector(dve, chain):
            dve.wait_ge(cst_in, 16)
            nc.vector.tensor_copy(tri[:], cst[:, C_TRI:C_TRI + P])
            nc.vector.tensor_copy(iota_bf[:], cst[:, C_IOTA:C_IOTA + P])
            nc.vector.memset(ones_bf[:], 1.0)
            chain(nc.vector.memset(ones3[:], 0.0))
            nc.vector.memset(ones3[0:3, :], 1.0).then_inc(bf_ready, 1)
            dve.wait_ge(bias_in, 16)
            v, left = bsplit[:, 0, :], bsplit[:, 1, :]
            part = [bparts[:, r, :] for r in range(3)]
            chain(nc.vector.tensor_copy(part[0], v))
            chain(nc.vector.tensor_tensor(left, v, part[0], ALU.subtract))
            chain(nc.vector.tensor_copy(part[1], left))
            chain(nc.vector.tensor_tensor(part[2], left, part[1], ALU.subtract))
            dve.sem_inc(bias_cut, 1)

        def scan_setup_scalar(act):
            keep = Chain(act, scan_kept)
            act.wait_ge(zeroed, 2)
            act.wait_ge(turned_w, 2)
            for j in range(NJ):
                rows = cols = slice(N * j, N * j + N)
                keep.mark(nc.scalar.copy(win_z[:, j, cols], bank[4][:, 0:N]))
                keep.mark(nc.scalar.copy(bm_diag[rows, cols], bank[4][rows, 128:128 + N]))
                keep.mark(nc.scalar.copy(c_diag[rows, j, :], bank[4][rows, 256:256 + D]))
            keep(nc.scalar.copy(a_powT[:, 0, :], bank[4][:, 384:512]))
            act.sem_inc(placed_w, 1)
            for l in range(1, LEVELS):
                act.wait_ge(pow_mm, l)
                keep.mark(nc.scalar.copy(a_pow[:, l, 64:], bank[5 + l % 2][:, 0:P]))
                keep(nc.scalar.copy(a_powT[:, l % 2, :], bank[5 + l % 2][:, P:2 * P]))
                act.sem_inc(pow_kept, 1)

        def setup_tensor(pe):
            pe.wait_ge(cst_in, 16)
            pe.wait_ge(gate_in, 32)
            pe.transpose(bank[0][:, 0:E], gate_rows[:], ident[0:E, 0:E])
            pe.transpose(bank[0][:, E:E + E * FC], b1_quarters[:], ident[0:E * FC, 0:E * FC]).then_inc(turned_w, 1)

        def scan_setup_tensor(pe):
            pe.wait_ge(scanw_in, 16 * (2 + 3 * NJ))
            pe.wait_ge(a_in, 16 * NJ)
            pe.transpose(bank[4][:, 0:N], win_rows[:], ident[0:N, 0:N])
            pe.transpose(bank[4][:, 128:128 + N], bm_rows[:].rearrange("m j n -> m (j n)"), ident[0:N, 0:N])
            pe.transpose(bank[4][:, 256:256 + D], c_rows[:].rearrange("m j n -> m (j n)"), ident)
            pe.transpose(bank[4][:, 384:512], a_pow[:, 0, 64:], ident).then_inc(turned_w, 1)
            pe.wait_ge(placed_w, 2)

        def powers_tensor(pe, levels):
            for l in levels:
                if l > 1:
                    pe.wait_ge(pow_kept, l - 1)
                last, lastT = a_pow[:, l - 1, 64:], a_powT[:, (l - 1) % 2, :]
                pe.matmul(bank[5 + l % 2][:, 0:P], lastT, last, start=True, stop=True)
                pe.matmul(bank[5 + l % 2][:, P:2 * P], last, lastT, start=True, stop=True).then_inc(pow_mm, 1)
            if l == LEVELS - 1:
                pe.wait_ge(pow_kept, l)

        MIXW = 16 * (5 + 2 * MG + ME)

        def slots_unit_first(dve):
            dve.wait_ge(mixw_in, MIXW)
            nc.vector.tensor_tensor(mu_t[:, 0], mu[:], mu[:], ALU.mult).then_inc(mix_set[0], 1)

        def slots_unit_tensor(pe):
            pe.wait_ge(mix_set[0], 1)
            pe.matmul(bank[7][:, 0:SLOTS], cst[:, C_ONE:C_ONE + P], mu_t[:, 0], start=True, stop=True).then_inc(mix_set[1], 1)
            pe.wait_ge(mix_set[2], 1)

        def slots_unit_scalar(act):
            act.wait_ge(mix_set[1], 1)
            nc.scalar.activation(mu_t[:, 1], bank[7][:, 0:SLOTS], ACT.Sqrt).then_inc(mix_set[2], 1)

        def slots_unit_last(dve, chain):
            dve.wait_ge(mix_set[2], 1)
            chain(nc.vector.tensor_scalar(mu_t[:, 0], mu_t[:, 1], 1e-12, None, ALU.max))
            chain(nc.vector.reciprocal(mu_t[:, 1], mu_t[:, 0]))
            nc.vector.tensor_tensor(mu[:], mu[:], mu_t[:, 1], ALU.mult).then_inc(mix_set[3], 1)

        early = stages.index("fm")

        GT = 8
        GROUPS = T // GT
        stat_sem, var_sem, root_sem, ready_sem = sem("stat"), sem("var"), sem("root"), sem("ready")
        stats_chain = Chain(None, sem("stats_v"))
        after_finish = {}
        taken = set()

        def stats_take(dve, n, g):
            if n == len(stages) or ("take", n, g) in taken:
                return
            taken.add(("take", n, g))
            stats_chain.engine = dve
            if n == 0:
                dve.wait_ge(x_in[g], 16)
            else:
                dve.wait_ge(x_done[n], GT * g + GT)
            for t in range(GT * g, GT * g + GT):
                nc.vector.bn_stats(half_stats[:, t, :], x[:, t, :]).then_inc(stat_sem, 1)
            dve.wait_ge(stat_sem, T * n + GT * g + GT)
            c = slice(GT * g, GT * g + GT)
            me, m2e, mo, m2o = (half_stats[:, c, k] for k in (1, 2, 4, 5))
            nc.vector.tensor_tensor(st[:, 2, c], me, mo, ALU.add)
            nc.vector.tensor_tensor(st[:, 3, c], me, mo, ALU.subtract)
            stats_chain(nc.vector.tensor_tensor(st[:, 4, c], m2e, m2o, ALU.add))
            nc.vector.tensor_scalar(mean[:, c], st[:, 2, c], 0.5, None, ALU.mult)
            stats_chain(nc.vector.scalar_tensor_tensor(st[:, 5, c], st[:, 3, c], float(P // 4), st[:, 3, c], ALU.mult, ALU.mult))
            stats_chain(nc.vector.tensor_tensor(st[:, 6, c], st[:, 4, c], st[:, 5, c], ALU.add))
            scale, shift = ((1.0 + EPS) / P, EPS * EPS) if stages[n] == "m" else (1.0 / P, EPS)
            nc.vector.tensor_scalar(st[:, 7, c], st[:, 6, c], scale, shift, ALU.mult, ALU.add).then_inc(var_sem, 1)

        def stats_root(act, n, g):
            if n == len(stages) or ("root", n, g) in taken:
                return
            taken.add(("root", n, g))
            c = slice(GT * g, GT * g + GT)
            act.wait_ge(var_sem, GROUPS * n + g + 1)
            nc.scalar.activation(st[:, 8, c], st[:, 7, c], ACT.Sqrt).then_inc(root_sem, 1)

        def stats_finish(dve, n, g):
            if n == len(stages) or ("finish", n, g) in taken:
                return
            taken.add(("finish", n, g))
            c = slice(GT * g, GT * g + GT)
            dve.wait_ge(root_sem, GROUPS * n + g + 1)
            stats_chain(nc.vector.reciprocal(rstd[:, c], st[:, 8, c]))
            nc.vector.scalar_tensor_tensor(shift_by[:, c], mean[:, c], -1.0, rstd[:, c], ALU.mult, ALU.mult).then_inc(ready_sem, 1)
            if n in after_finish:
                after_finish[n](dve, g)

        def stats_after(dve, n, g):
            stats_take(dve, n, g)
            if g:
                stats_finish(dve, n, g - 1)
            if g == GROUPS - 1:
                stats_finish(dve, n, g)

        SHARED = GROUPS // 2
        BY_SCALAR, BY_VECTOR = T - TB * (GROUPS - SHARED), TB * (GROUPS - SHARED)

        def wait_normed(engine, s, at, t):
            g, r = t // GT, t % GT
            if g < SHARED:
                engine.wait_ge(s["normed"], at["normed"] + t + 1)
            elif r < TB:
                engine.wait_ge(s["normed"], at["normed"] + GT * SHARED + TB * (g - SHARED) + r + 1)
            else:
                engine.wait_ge(s["normed_v"], at["normed_v"] + TB * (g - SHARED) + r - TB + 1)

        def normalise_vector(dve, n, s, at, g, stored=None, stored_at=None):
            if g < SHARED:
                return
            dve.wait_ge(ready_sem, GROUPS * n + g + 1)
            dve.wait_ge(s["turned"], at["turned"] + GT * g)
            if stored is not None:
                dve.wait_ge(stored[1], stored_at[1] + 16 * g)
            for r in range(TB, GT):
                t = GT * g + r
                nc.vector.tensor_scalar(xh[:, r, :], x[:, t, :], mean[:, t:t + 1], rstd[:, t:t + 1],
                                        ALU.subtract, ALU.mult).then_inc(s["normed_v"], 1)

        def normalise_scalar(act, n, s, at, stored=None, stored_at=None):

            def tiles(g):
                act.wait_ge(ready_sem, GROUPS * n + g + 1)
                for r in range(GT if g < SHARED else TB):
                    if r % TB == 0 and g:
                        act.wait_ge(s["turned"], at["turned"] + GT * g - TB + r)
                        if stored is not None:
                            act.wait_ge(stored[r // TB], stored_at[r // TB] + 16 * g)
                    t = slice(GT * g + r, GT * g + r + 1)
                    nc.scalar.activation(xh[:, r, :], x[:, GT * g + r, :], ACT.Identity, bias=shift_by[:, t],
                                         scale=rstd[:, t]).then_inc(s["normed"], 1)
                for h in range(2):
                    act.wait_ge(s["turned"], at["turned"] + GT * g + TB * h + TB)
                    nc.scalar.copy(xT[:, h, :], bank[h][:]).then_inc(s["xT_ready"], 1)

            stats_root(act, n, 0)
            for g in range(1, GROUPS):
                stats_root(act, n, g)
                tiles(g - 1)
            tiles(GROUPS - 1)

        FFN_COUNTS = dict(v=0, normed=BY_SCALAR, normed_v=BY_VECTOR, turned=T, xT_ready=B, gated=B, log_ready=1, exp_ready=1,
                          one_ready=1, ranked=1, hot_ready=T, tile_ready=1, inverted=1, rows_ready=1, expert_ready=1, g_turned=ROWS,
                          xgT=ROWS, h_mm=ROWS, h_out=ROWS, h_turned=ROWS, hT_ready=ROWS, y_mm=ROWS, y_ready=ROWS)
        RING_COUNTS = dict(stored=[16 * 4] * 2, gathered=[16 * len(range(i, ROWS, AHEAD)) for i in range(AHEAD)],
                           scattered=[16 * len(range(i, ROWS, 3)) for i in range(3)], back=[16] * 4)
        ffn_sems = {k: sem(f"f_{k}") for k in FFN_COUNTS}
        ffn_rings = {k: [sem(f"f_{k}{i}") for i in range(len(v))] for k, v in RING_COUNTS.items()}
        chains = {"f": 0, "m": 0}

        def ffn(n):
            s, at = ffn_sems, {k: v * stages[:n].count("f") for k, v in FFN_COUNTS.items()}
            stored, gathered, scattered, back = (ffn_rings[k] for k in RING_COUNTS)
            after_finish[n] = lambda dve, g: normalise_vector(dve, n, s, at, g, stored, at["stored"])
            for k, counts in RING_COUNTS.items():
                at[k] = [v * stages[:n].count("f") for v in counts]

            def sync(sp):
                rows = xhat_dram.rearrange("(t p) d -> p t d", p=P)
                for i in range(GROUPS):
                    for h in range(2):
                        wait_normed(sp, s, at, GT * i + TB * h + TB - 1)
                        sp.dma_start(rows[:, GT * i + TB * h:GT * i + TB * h + TB, :], xh[:, 4 * h:4 * h + 4, :]).then_inc(stored[h], 16)
                if n == stages.index("f"):
                    late_loads(sp)
                for q in range(3):
                    sp.wait_ge(scattered[q], at["scattered"][q] + 16 * (ROWS // 3))
                for q in range(4):
                    sp.dma_start(yback[:, 8 * q:8 * q + 8, :],
                                 yrow_dram.rearrange("(t p) d -> p t d", p=P)[:, 8 * q:8 * q + 8, :]).then_inc(back[q], 16)

            def vector(dve):
                chain = Chain(dve, s["v"], chains["f"])
                if n == early:
                    slots_unit_first(dve)
                dve.wait_ge(s["gated"], at["gated"] + B)
                chain(nc.vector.tensor_copy(r_log[:], bank[2][:, 0:T * E].rearrange("p (t e) -> p e t", e=E)))
                by_token = lambda v: v.rearrange("p e t -> p t e")
                over_e = lambda v: v.unsqueeze(1).to_broadcast([P, E, T])
                over_t = lambda v: v.unsqueeze(2).to_broadcast([P, E, T])
                top, esum, prob, first, dest, lane, row = (r_t[:, k, :] for k in range(7))
                em = cst[:, C_EM:C_EM + E * T].rearrange("p (e t) -> p e t", e=E)
                chain(nc.vector.tensor_reduce(top, by_token(r_log[:]), AX.X, ALU.max))
                nc.vector.tensor_tensor(r_exp[:], r_log[:], over_e(top), ALU.subtract).then_inc(s["log_ready"], 1)
                chain(nc.vector.tensor_tensor(r_eq[:], r_log[:], over_e(top), ALU.is_equal))
                chain(nc.vector.tensor_tensor(r_scan[:], r_eq[:], em, ALU.mult))
                chain(nc.vector.tensor_reduce(first, by_token(r_scan[:]), AX.X, ALU.min))
                chain(nc.vector.tensor_tensor(r_one[:], em, over_e(first), ALU.is_equal))
                nc.vector.tensor_copy(r_onebf[:], r_one[:]).then_inc(s["one_ready"], 1)
                dve.wait_ge(s["exp_ready"], at["exp_ready"] + 1)
                chain(nc.vector.tensor_reduce(esum, by_token(r_log[:]), AX.X, ALU.add))
                chain(nc.vector.reciprocal(prob, esum))
                chain(nc.vector.tensor_scalar(prob, prob, 0.5, None, ALU.mult))
                dve.wait_ge(s["ranked"], at["ranked"] + 1)
                chain(nc.vector.tensor_copy(r_tot[:], bank[3][:, 256:512].rearrange("p (e t) -> p e t", e=E)))
                flat = lambda v: v.rearrange("p e t -> p (e t)")
                one = cst[:, C_ONE:C_ONE + 256]
                cnt, tiles, tiles_to, cnt_to, r_a, r_b, off = (r_e[:, k, :] for k in range(7))
                nc.vector.tensor_tensor_scan(flat(r_scan[:]), one, flat(r_tot[:]), 0.0, ALU.mult, ALU.add)
                chain(nc.vector.tensor_reduce(cnt, r_tot[:], AX.X, ALU.add))
                chain(nc.vector.tensor_scalar(r_ei[:, 0, :], cnt, float(P - 1), None, ALU.add))
                chain(nc.vector.tensor_scalar(r_ei[:, 1, :], r_ei[:, 0, :], 7, None, ALU.logical_shift_right))
                chain(nc.vector.tensor_copy(tiles, r_ei[:, 1, :]))
                nc.vector.tensor_tensor_scan(tiles_to, one[:, 0:E], tiles, 0.0, ALU.mult, ALU.add)
                chain(nc.vector.tensor_tensor_scan(cnt_to, one[:, 0:E], cnt, 0.0, ALU.mult, ALU.add))
                nc.vector.tensor_tensor(r_a, tiles_to, tiles, ALU.subtract)
                chain(nc.vector.tensor_tensor(r_b, cnt_to, cnt, ALU.subtract))
                chain(nc.vector.scalar_tensor_tensor(off, r_a, float(P), r_b, ALU.mult, ALU.subtract))
                chain(nc.vector.tensor_tensor(r_scan[:], r_scan[:], r_tot[:], ALU.subtract))
                chain(nc.vector.tensor_tensor(r_scan[:], r_scan[:], over_t(off), ALU.add))
                chain(nc.vector.tensor_tensor(flat(r_scan[:]), flat(r_scan[:]), bank[3][:, 0:256], ALU.add))
                chain(nc.vector.tensor_tensor(r_scan[:], r_scan[:], r_one[:], ALU.mult))
                chain(nc.vector.tensor_reduce(dest, by_token(r_scan[:]), AX.X, ALU.add))
                chain(nc.vector.tensor_copy(r_ti[:, 0, :], dest))
                nc.vector.tensor_scalar(r_ti[:, 1, :], r_ti[:, 0, :], P - 1, None, ALU.bitwise_and)
                chain(nc.vector.tensor_scalar(r_ti[:, 2, :], r_ti[:, 0, :], 7, None, ALU.logical_shift_right))
                nc.vector.tensor_copy(lane, r_ti[:, 1, :])
                chain(nc.vector.tensor_copy(row, r_ti[:, 2, :]))
                ramp = cst[:, C_TILE:C_TILE + ROWS].unsqueeze(1).to_broadcast([P, T, ROWS])
                tcol = cst[:, C_TCOL:C_TCOL + T].unsqueeze(2).to_broadcast([P, T, ROWS])
                chain(nc.vector.tensor_tensor(tile_hot[:, 2], ramp, row.unsqueeze(2).to_broadcast([P, T, ROWS]), ALU.is_equal))
                nc.vector.tensor_tensor(tile_hot[:, 0], tile_hot[:, 2], tcol, ALU.mult)
                nc.vector.tensor_scalar(tile_hot[:, 1], tile_hot[:, 2], cst[:, C_P1:C_P1 + 1], None, ALU.mult).then_inc(s["tile_ready"], 1)
                for t in range(T):
                    nc.vector.tensor_scalar(lane_hot[:, t, :], iota_bf[:], lane[:, t:t + 1], None, ALU.is_equal).then_inc(s["hot_ready"], 1)
                ends = r_e[0:1, 2, :].unsqueeze(1).to_broadcast([1, ROWS, E])
                tile_no = cst[0:1, C_TILE:C_TILE + ROWS].unsqueeze(2).to_broadcast([1, ROWS, E])
                chain(nc.vector.tensor_tensor(expert_cmp[:], ends, tile_no, ALU.is_le))
                chain(nc.vector.tensor_reduce(expert_f[:], expert_cmp[:], AX.X, ALU.add))
                nc.vector.tensor_scalar(expert_of[:], expert_f[:], float(E - 1), None, ALU.min).then_inc(s["expert_ready"], 1)
                dve.wait_ge(s["inverted"], at["inverted"] + 1)
                chain(nc.vector.tensor_copy(inv[:], bank[2][:, 0:2 * ROWS]))
                token, pad = inv_v[:, 0, :], inv_v[:, 1, :]
                chain(nc.vector.scalar_tensor_tensor(token, inv[:, 0:ROWS], float(P), inv[:, ROWS:], ALU.mult, ALU.add))
                chain(nc.vector.tensor_scalar(pad, token, 0.0, float(NOWHERE), ALU.is_equal, ALU.mult))
                nc.vector.tensor_scalar(gather_row[:], token, -1.0, 0.0, ALU.add, ALU.max)
                nc.vector.scalar_tensor_tensor(scatter_row[:], token, -1.0, pad, ALU.add, ALU.add).then_inc(s["rows_ready"], 1)
                if n == early:
                    slots_unit_last(dve, chain)

                chains["f"] = chain.n

                dve.wait_ge(s["expert_ready"], at["expert_ready"] + 1)
                def hidden(j, k):
                    e = dve.value_load(expert_of[0:1, bass.ds(j, 1)], min_val=0, max_val=E - 1)
                    dve.wait_ge(s["h_turned"], at["h_turned"] + j + 1)
                    for c in range(FC):
                        last = nc.vector.tensor_scalar(hidT[:, k % 2, c, :], bank[4 + k % 2][:, c * P:c * P + P],
                                                       b1T[:, bass.ds(e * FC + c, 1)], 0.0, ALU.add, ALU.max)
                    last.then_inc(s["hT_ready"], 1)

                def result(j, k, used):
                    dve.wait_ge(s["y_mm"], at["y_mm"] + j + 1)
                    if later(used):
                        dve.wait_ge(scattered[k % 3], at["scattered"][k % 3] + used)
                    nc.vector.tensor_copy(yg[:, k % 3, :], bank[6 + k % 2][:, 0:D]).then_inc(s["y_ready"], 1)

                def round_of(i):
                    for k in range(ROUND):
                        hidden(ROUND * i + k + 1, k + 1)
                        result(ROUND * i + k, k, 16 * (ROUND // 3 * i + k // 3))

                hidden(0, 0)
                peeled(dve, 0, ROUNDS, round_of)
                for j in range(ROUND * ROUNDS, ROWS):
                    if j + 1 < ROWS:
                        hidden(j + 1, j + 1)
                    result(j, j, 16 * (j // 3))
                for g in range(GROUPS):
                    dve.wait_ge(back[g], at["back"][g] + 16)
                    for t in range(GT * g, GT * g + GT):
                        nc.vector.scalar_tensor_tensor(x[:, t, :], yback[:, t, :], prob[:, t:t + 1], x[:, t, :],
                                                       ALU.mult, ALU.add).then_inc(x_done[n + 1], 1)
                    stats_after(dve, n + 1, g)

            def scalar(act):
                normalise_scalar(act, n, s, at, stored, at["stored"])
                act.wait_ge(s["one_ready"], at["one_ready"] + 1)
                nc.scalar.activation(r_log[:], r_exp[:], ACT.Exp).then_inc(s["exp_ready"], 1)
                if n == 0:
                    scan_setup_scalar(act)
                if n == early:
                    slots_unit_scalar(act)

                def tokens(j, k):
                    act.wait_ge(s["g_turned"], at["g_turned"] + j + 1)
                    nc.scalar.copy(xgT[:, k % 2, :], bank[k % 2][:, 0:P]).then_inc(s["xgT"], 1)

                def hidden(j, k):
                    act.wait_ge(s["h_mm"], at["h_mm"] + j + 1)
                    nc.scalar.copy(hid[:, k % 2, :], bank[2 + k % 2][:]).then_inc(s["h_out"], 1)

                tokens(0, 0)
                with act.Fori(0, ROUNDS) as i:
                    for k in range(ROUND):
                        tokens(ROUND * i + k + 1, k + 1)
                        hidden(ROUND * i + k, k)
                for j in range(ROUND * ROUNDS, ROWS):
                    if j + 1 < ROWS:
                        tokens(j + 1, j + 1)
                    hidden(j, j)

            def tensor(pe):
                if n == stages.index("f"):
                    pe.wait_ge(placed_w, 1)
                for i in range(GROUPS):
                    for h in range(2):
                        for k in range(TB):
                            wait_normed(pe, s, at, GT * i + TB * h + k)
                            pe.transpose(bank[h][:, k * P:k * P + P], xh[:, 4 * h + k, :], ident).then_inc(s["turned"], 1)
                    for h in range(2):
                        pe.wait_ge(s["xT_ready"], at["xT_ready"] + 2 * i + h + 1)
                        for k in range(TB):
                            last = pe.matmul(bank[2][:, (8 * i + 4 * h + k) * E:(8 * i + 4 * h + k + 1) * E], xT[:, h, k * P:k * P + P],
                                             gateT[:], start=True, stop=True)
                        last.then_inc(s["gated"], 1)
                pe.wait_ge(bf_ready, 1)
                pe.wait_ge(s["one_ready"], at["one_ready"] + 1)
                one_hot = r_onebf[:].rearrange("p e t -> p (e t)")
                pe.matmul(bank[3][:, 0:256], tri[:], one_hot, start=True, stop=True)
                pe.matmul(bank[3][:, 256:512], ones_bf[:], one_hot, start=True, stop=True).then_inc(s["ranked"], 1)
                if n == 0:
                    scan_setup_tensor(pe)
                    powers_tensor(pe, range(1, LEVELS - 2))
                if n == early:
                    slots_unit_tensor(pe)
                pe.wait_ge(s["tile_ready"], at["tile_ready"] + 1)
                for t in range(T):
                    pe.wait_ge(s["hot_ready"], at["hot_ready"] + t + 1)
                    last = pe.matmul(bank[2][:, 0:2 * ROWS], lane_hot[:, t, :], tile_hot[:, 0:2, t, :], start=(t == 0), stop=(t == T - 1))
                last.then_inc(s["inverted"], 1)
                if n == 0:
                    powers_tensor(pe, range(LEVELS - 2, LEVELS))

                pe.wait_ge(s["rows_ready"], at["rows_ready"] + 1)
                pe.wait_ge(s["expert_ready"], at["expert_ready"] + 1)
                pe.wait_ge(w1_in, 16)
                pe.wait_ge(w2_in, 16)
                pe.wait_ge(biasrow_in, 16 * 3)

                def turn_in(j, k, have):
                    pe.wait_ge(gathered[k % AHEAD], at["gathered"][k % AHEAD] + have)
                    pe.transpose(bank[k % 2][:, 0:P], xg[:, k % AHEAD, :], ident).then_inc(s["g_turned"], 1)

                def expert(j):
                    return pe.value_load(expert_of[0:1, bass.ds(j, 1)], min_val=0, max_val=E - 1)

                def up(j, k, e):
                    pe.wait_ge(s["xgT"], at["xgT"] + j + 1)
                    pe.matmul(bank[2 + k % 2][:], xgT[:, k % 2, :], w1[:, bass.ds(e, 1), :], start=True, stop=True).then_inc(s["h_mm"], 1)

                def turn_hidden(j, k):
                    pe.wait_ge(s["h_out"], at["h_out"] + j + 1)
                    for c in range(FC):
                        last = pe.transpose(bank[4 + k % 2][:, c * P:c * P + P], hid[:, k % 2, c * P:c * P + P], ident)
                    last.then_inc(s["h_turned"], 1)

                def down(j, k, e):
                    pe.wait_ge(s["hT_ready"], at["hT_ready"] + j + 1)
                    if later(j):
                        pe.wait_ge(s["y_ready"], at["y_ready"] + j)
                    pe.matmul(bank[6 + k % 2][:, 0:D], ones3[:], b2rows[:, bass.ds(e * D, D)], start=True, stop=False)
                    for c in range(FC):
                        last = pe.matmul(bank[6 + k % 2][:, 0:D], hidT[:, k % 2, c, :], w2[:, bass.ds(e, 1), c, :],
                                         start=False, stop=(c == FC - 1))
                    last.then_inc(s["y_mm"], 1)

                for j in range(3):
                    turn_in(j, j, 16)
                    if j >= 1:
                        up(j - 1, j - 1, expert(j - 1))
                    if j >= 2:
                        turn_hidden(j - 2, j - 2)

                def round_of(i):
                    e = {}
                    for k in range(ROUND):
                        turn_in(ROUND * i + k + 3, k + 3, 16 * (i + (k + 3) // AHEAD + 1))
                        e[k + 2] = expert(ROUND * i + k + 2)
                        up(ROUND * i + k + 2, k + 2, e[k + 2])
                        turn_hidden(ROUND * i + k + 1, k + 1)
                        down(ROUND * i + k, k, e[k] if k in e else expert(ROUND * i + k))

                peeled(pe, 0, ROUNDS, round_of)
                for j in range(ROWS, ROWS + 3):
                    if j - 1 < ROWS:
                        up(j - 1, j - 1, expert(j - 1))
                    if j - 2 < ROWS:
                        turn_hidden(j - 2, j - 2)
                    down(j - 3, j - 3, expert(j - 3))

            def gpsimd(pool):
                pool.wait_ge(s["rows_ready"], at["rows_ready"] + 1)
                for h in range(2):
                    pool.wait_ge(stored[h], at["stored"][h] + 16 * 4)

                def gather(j):
                    if j >= AHEAD:
                        pool.wait_ge(s["g_turned"], at["g_turned"] + j - AHEAD + 1)
                    pool.indirect_dma_start(xg[:, j % AHEAD, :], None, xhat_dram, bass.IndirectOffsetOnAxis(gather_row[:, j:j + 1], 0)).then_inc(gathered[j % AHEAD], 16)

                for j in range(AHEAD):
                    gather(j)
                for j in range(ROWS):
                    pool.wait_ge(s["y_ready"], at["y_ready"] + j + 1)
                    pool.indirect_dma_start(yrow_dram, bass.IndirectOffsetOnAxis(scatter_row[:, j:j + 1], 0), yg[:, j % 3, :], None,
                                            bounds_check=T * P - 1, oob_is_err=False).then_inc(scattered[j % 3], 16)
                    if j + AHEAD < ROWS:
                        gather(j + AHEAD)

            return dict(sync=sync, vector=vector, scalar=scalar, tensor=tensor, gpsimd=gpsimd)

        def scan(n):
            s = {k: sem(f"s{n}_{k}") for k in (
                "normed normed_v turned xT_ready u_mm u_kept ub_mm level_mm level_done d_added y_mm").split()}
            at = dict.fromkeys(s, 0)
            after_finish[n] = lambda dve, g: normalise_vector(dve, n, s, at, g)

            def vector(dve):
                for g in range(2):
                    dve.wait_ge(s["ub_mm"], g + 1)
                    nc.vector.tensor_copy(half(state, g), bank[4 + g][:]).then_inc(s["level_done"], 1)
                for l in range(LEVELS):
                    for g in range(2):
                        dve.wait_ge(s["level_mm"], 2 * l + g + 1)
                        dve.wait_ge(s["level_done"], 2 * l + g + 1)
                        nc.vector.tensor_tensor(half(state, g), half(state, g), bank[6 + g][:], ALU.add).then_inc(s["level_done"], 1)
                for b in range(B):
                    dve.wait_ge(s["y_mm"], b + 1)
                    dve.wait_ge(s["d_added"], b + 1)
                    tiles = x[:, TB * b:TB * b + TB, :].rearrange("p t d -> p (t d)")
                    nc.vector.tensor_tensor(tiles, tiles, bank[4 + b % 4][:], ALU.add).then_inc(x_done[n + 1], TB)
                    if b % 2:
                        stats_after(dve, n + 1, b // 2)

            def half(v, g):
                return v[:, 4 * g:4 * g + 4, :].rearrange("p b c -> p (b c)")

            def gpsimd(pool):
                pool.wait_ge(scanw_in, 16 * (2 + 3 * NJ))
                for b in range(B):
                    wait_normed(pool, s, at, TB * b + TB - 1)
                    tiles = x[:, TB * b:TB * b + TB, :]
                    pool.tensor_tensor(tiles, tiles, d_rep[:].unsqueeze(1).to_broadcast([P, TB, D]), ALU.add).then_inc(s["d_added"], 1)

            def scalar(act):
                normalise_scalar(act, n, s, at)
                act.wait_ge(scanw_in, 16 * (2 + 3 * NJ))
                for g in range(2):
                    act.wait_ge(s["u_mm"], 4 * g + 4)
                    nc.scalar.activation(half(u1, g), bank[2 + g][:], ACT.Identity, bias=b_in[:, 0:1]).then_inc(s["u_kept"], 1)

            def tensor(pe):
                for g in range(2):
                    for i in range(2):
                        for h in range(2):
                            for k in range(TB):
                                wait_normed(pe, s, at, 16 * g + 8 * i + 4 * h + k)
                                pe.transpose(bank[h][:, k * P:k * P + P], xh[:, 4 * h + k, :], ident).then_inc(s["turned"], 1)
                        for h in range(2):
                            pe.wait_ge(s["xT_ready"], 4 * g + 2 * i + h + 1)
                            for k in range(TB):
                                last = pe.matmul(bank[2 + g][:, (2 * i + h) * P:(2 * i + h + 1) * P], win_z[:, k, :],
                                                 xT[:, h, k * P:k * P + P], start=(k == 0), stop=(k == TB - 1))
                            last.then_inc(s["u_mm"], 1)
                for g in range(2):
                    pe.wait_ge(s["u_kept"], g + 1)
                    pe.matmul(bank[4 + g][:], bm_diag[:], half(u1, g), start=True, stop=True).then_inc(s["ub_mm"], 1)
                for l in range(LEVELS):
                    step = 1 << l
                    for g in range(2):
                        pe.wait_ge(s["level_done"], 2 * l + g + 1)
                        to = bank[6 + g][:].rearrange("p (b c) -> p b c", b=4)
                        h = state[:, 4 * g:4 * g + 4, :]
                        if step < P:
                            pe.matmul(to[:, :, step:], a_pow[:, l, 64:], h[:, :, 0:P - step], start=True, stop=True)
                            last = pe.matmul(to[:, :, 0:step], a_pow[:, l, 32:160], h[:, :, P - step:], start=True, stop=True)
                        else:
                            shift = N * step // P
                            last = pe.matmul(to, a_pow[:, l, 64 - shift:192 - shift], h, start=True, stop=True)
                        last.then_inc(s["level_mm"], 1)
                for b in range(B):
                    if b == 0:
                        pe.wait_ge(s["level_done"], 2 * LEVELS + 1)
                    if b == 3:
                        pe.wait_ge(s["level_done"], 2 * LEVELS + 2)
                    if b >= 4:
                        pe.wait_ge(x_done[n + 1], TB * (b - 3))
                    pe.matmul(bank[4 + b % 4][:], state[:, b, :], c_diag[:].rearrange("p j d -> p (j d)"), start=True, stop=True).then_inc(s["y_mm"], 1)

            return dict(sync=lambda sp: None, vector=vector, scalar=scalar, tensor=tensor, gpsimd=gpsimd)


        BY_ACT = 6
        MIX_COUNTS = dict(v=0, centered=GROUPS * BY_ACT, centered_v=GROUPS * (GT - BY_ACT), scaled=B, xn=B, squared=T, norm_sqrt=2, unit_ready=2, unit=B, turned=T,
                          xT_ready=B, logit_c=2 * B, logit_d=2 * B, max_c=2 * B, max_d=2 * B, exp_c=T, exp_d=2 * B,
                          turn_c0=B, turn_c1=B, turn_d0=B, turn_d1=B, kept_c0=B, kept_c1=B, kept_d0=B, kept_d1=B,
                          in_mm=B, in_kept=2 * B, in_turned=B, slotT=B, h_mm=MG, h_gelu=MG * MG, out_mm=4, out_kept=4,
                          y_mm=B, weights=B, cleared=1)
        mix_sems = {k: sem(f"m_{k}") for k in MIX_COUNTS}
        def mix(n):
            s, at = mix_sems, {k: v * stages[:n].count("m") for k, v in MIX_COUNTS.items()}

            def centre_vector(dve, g):
                dve.wait_ge(ready_sem, GROUPS * n + g + 1)
                for t in range(GT * g + BY_ACT, GT * g + GT):
                    nc.vector.tensor_scalar(xn[:, t, :], x[:, t, :], mean[:, t:t + 1], rstd[:, t:t + 1],
                                            ALU.subtract, ALU.mult).then_inc(s["centered_v"], 1)

            after_finish[n] = centre_vector

            def vector(dve):
                chain = Chain(dve, s["v"], chains["m"])
                for b in range(B):
                    dve.wait_ge(s["scaled"], at["scaled"] + b + 1)
                    tiles = xn[:, TB * b:TB * b + TB, :]
                    nc.vector.tensor_tensor(tiles, tiles, beta[:].unsqueeze(1).to_broadcast([P, TB, D]), ALU.add).then_inc(s["xn"], 1)
                norm, unit = st[:, 3, :], st[:, 4, :]
                for half in range(2):
                    c = slice(T // 2 * half, T // 2 * half + T // 2)
                    dve.wait_ge(s["norm_sqrt"], at["norm_sqrt"] + half + 1)
                    chain(nc.vector.tensor_scalar(norm[:, c], st[:, 2, c], 1e-12, None, ALU.max))
                    chain(nc.vector.reciprocal(unit[:, c], norm[:, c]))
                    nc.vector.tensor_scalar(unit[:, c], unit[:, c], mscale[:, 0:1], None, ALU.mult).then_inc(s["unit_ready"], 1)

                def max_c(b):
                    for j in range(2):
                        dve.wait_ge(s["logit_c"], at["logit_c"] + 2 * b + j + 1)
                        nc.vector.tensor_reduce(neg_c[:, bass.ds(b, 1), 2 * j:2 * j + 2], bank[2 + j][:].rearrange("p (k s) -> p k s", k=2),
                                                AX.X, ALU.max, negate=True).then_inc(s["max_c"], 1)

                def max_d(b):
                    for j in range(2):
                        dve.wait_ge(s["logit_d"], at["logit_d"] + 2 * b + j + 1)
                        nc.vector.tensor_reduce(neg_d[:, bass.ds(b, 1), j:j + 1], bank[4 + j][:], AX.X, ALU.max, negate=True).then_inc(s["max_d"], 1)

                def keep_c(b):
                    dve.wait_ge(s["turn_c1"], at["turn_c1"] + b + 1)
                    nc.vector.tensor_copy(combT[:, 1, bass.ds(b, 1), :], bank[7][:]).then_inc(s["kept_c1"], 1)

                def keep_d(b, h):
                    dve.wait_ge(s["turn_d1"], at["turn_d1"] + b + 1)
                    nc.vector.tensor_copy(disp[:, h, 2:4, :].rearrange("p k s -> p (k s)"), bank[7][:]).then_inc(s["kept_d1"], 1)
                    nc.vector.reciprocal(inv_d[:, bass.ds(b, 1), :], sum_d[:, bass.ds(b, 1), :]).then_inc(s["weights"], 1)

                def keep_in(b):
                    dve.wait_ge(s["in_mm"], at["in_mm"] + b + 1)
                    dve.wait_ge(s["weights"], at["weights"] + b + 1)
                    for j in range(2):
                        nc.vector.tensor_scalar(slot_in[:, j, :], bank[1][:, j * D:j * D + D], inv_d[:, bass.ds(b, 1), j:j + 1], None,
                                                ALU.mult).then_inc(s["in_kept"], 1)

                def step(b, h):
                    keep_c(b)
                    max_c(b + 1)
                    keep_d(b, h)
                    max_d(b + 1)
                    keep_in(b)

                max_c(0)
                max_d(0)
                step(0, 0)
                with dve.Fori(0, 3) as i:
                    step(2 * i + 1, 1)
                    step(2 * i + 2, 0)
                keep_c(7)
                keep_d(7, 1)
                keep_in(7)
                chain(nc.vector.reciprocal(inv_c[:], sum_c[:]))
                chain(nc.vector.tensor_scalar(inv_c[:], inv_c[:], 0.5, None, ALU.mult))
                chains["m"] = chain.n
                for h in range(2):
                    for j in range(2):
                        dve.wait_ge(s["out_mm"], at["out_mm"] + 2 * h + j + 1)
                        nc.vector.tensor_tensor(slot_out[:, h, 4 * j:4 * j + 4, :], bank[2 + 2 * h + j][:].rearrange("p (b d) -> p b d", b=4),
                                                mb2[:, h, :].unsqueeze(1).to_broadcast([P, 4, D]), ALU.add).then_inc(s["out_kept"], 1)
                for b in range(B):
                    dve.wait_ge(s["y_mm"], at["y_mm"] + b + 1)
                    for k in range(TB):
                        t = TB * b + k
                        nc.vector.scalar_tensor_tensor(x[:, t, :], bank[Y_BANK[b % 4]][:, k * D:k * D + D], inv_c[:, t:t + 1], x[:, t, :],
                                                       ALU.mult, ALU.add).then_inc(x_done[n + 1], 1)
                    if b % 2:
                        stats_after(dve, n + 1, b // 2)

            Y_BANK = (6, 0, 1, 4)

            def gpsimd(pool):
                pool.wait_ge(mixw_in, MIXW)
                for b in range(B):
                    if b % 2 == 0:
                        pool.wait_ge(s["centered"], at["centered"] + BY_ACT * (b // 2) + TB)
                    else:
                        pool.wait_ge(s["centered"], at["centered"] + BY_ACT * (b // 2 + 1))
                        pool.wait_ge(s["centered_v"], at["centered_v"] + (GT - BY_ACT) * (b // 2 + 1))
                    tiles = xn[:, TB * b:TB * b + TB, :]
                    pool.tensor_tensor(tiles, tiles, gamma[:].unsqueeze(1).to_broadcast([P, TB, D]), ALU.mult).then_inc(s["scaled"], 1)

                def units(b):
                    pool.wait_ge(s["unit_ready"], at["unit_ready"] + b // (B // 2) + 1)
                    h = b % 2
                    tiles = slice(TB * b, TB * b + TB)
                    if b >= 2:
                        pool.wait_ge(s["turned"], at["turned"] + TB * (b - 1))
                    pool.tensor_tensor(xh[:, TB * h:TB * h + TB, :], xn[:, tiles, :], st[:, 4, tiles].unsqueeze(2).to_broadcast([P, TB, D]),
                                       ALU.mult).then_inc(s["unit"], 1)

                for b in range(B):
                    units(b)
                pool.memset(hid_diag[:], 0.0).then_inc(s["cleared"], 1)

            def scalar(act):
                def centre(g):
                    act.wait_ge(ready_sem, GROUPS * n + g + 1)
                    for t in range(GT * g, GT * g + BY_ACT):
                        nc.scalar.activation(xn[:, t, :], x[:, t, :], ACT.Identity, bias=shift_by[:, t:t + 1],
                                             scale=rstd[:, t:t + 1]).then_inc(s["centered"], 1)

                def squares(half):
                    for t in range(T // 2 * half, T // 2 * half + T // 2):
                        if t % TB == 0:
                            act.wait_ge(s["xn"], at["xn"] + t // TB + 1)
                        if t >= GT:
                            act.wait_ge(s["squared"], at["squared"] + t - GT + 1)
                        nc.scalar.activation(square[:, t % GT, :], xn[:, t, :], ACT.Square, accum_out=st[:, 5, t:t + 1]).then_inc(s["squared"], 1)
                    act.wait_ge(s["squared"], at["squared"] + T // 2 * half + T // 2)
                    c = slice(T // 2 * half, T // 2 * half + T // 2)
                    nc.scalar.activation(st[:, 2, c], st[:, 5, c], ACT.Sqrt).then_inc(s["norm_sqrt"], 1)

                def copy_xT(b, h):
                    act.wait_ge(s["turned"], at["turned"] + TB * b + TB)
                    nc.scalar.copy(xT[:, h, :], bank[0][:]).then_inc(s["xT_ready"], 1)

                def exp_c(b, h):
                    for k in range(TB):
                        t = bass.ds(TB * b + k, 1)
                        act.wait_ge(s["max_c"], at["max_c"] + 2 * b + k // 2 + 1)
                        nc.scalar.activation(comb[:, h, k, :], bank[2 + k // 2][:, SLOTS * (k % 2):SLOTS * (k % 2) + SLOTS], ACT.Exp,
                                             bias=neg_c[:, bass.ds(b, 1), k:k + 1], accum_out=sum_c[:, t]).then_inc(s["exp_c"], 1)

                def exp_d(b, h):
                    for j in range(2):
                        act.wait_ge(s["max_d"], at["max_d"] + 2 * b + j + 1)
                        nc.scalar.activation(disp_s[:, h, j, :], bank[4 + j][:], ACT.Exp, bias=neg_d[:, bass.ds(b, 1), j:j + 1],
                                             accum_out=sum_d[:, bass.ds(b, 1), j:j + 1]).then_inc(s["exp_d"], 1)

                def keep_c(b):
                    act.wait_ge(s["turn_c0"], at["turn_c0"] + b + 1)
                    nc.scalar.copy(combT[:, 0, bass.ds(b, 1), :], bank[6][:]).then_inc(s["kept_c0"], 1)

                def keep_d(b, h):
                    act.wait_ge(s["turn_d0"], at["turn_d0"] + b + 1)
                    nc.scalar.copy(disp[:, h, 0:2, :].rearrange("p k s -> p (k s)"), bank[6][:]).then_inc(s["kept_d0"], 1)

                def keep_slots(b):
                    act.wait_ge(s["in_turned"], at["in_turned"] + b + 1)
                    nc.scalar.copy(slotT[:, :, bass.ds(b, 1), :], bank[1][:, SLOTS:].rearrange("p (e s) -> p e s", e=ME)).then_inc(s["slotT"], 1)

                def step(b, h):
                    copy_xT(b + 1, 1 - h)
                    if later(b):
                        keep_slots(b - 1)
                    keep_c(b)
                    exp_c(b + 1, 1 - h)
                    keep_d(b, h)
                    exp_d(b + 1, 1 - h)

                stats_root(act, n, 0)
                for g in range(1, GROUPS):
                    stats_root(act, n, g)
                    centre(g - 1)
                centre(GROUPS - 1)
                squares(0)
                copy_xT(0, 0)
                squares(1)
                exp_c(0, 0)
                exp_d(0, 0)
                step(0, 0)
                with act.Fori(0, 3) as i:
                    step(2 * i + 1, 1)
                    step(2 * i + 2, 0)
                keep_slots(6)
                keep_c(7)
                keep_d(7, 1)
                keep_slots(7)
                act.wait_ge(s["cleared"], at["cleared"] + 1)
                for g in range(MG):
                    act.wait_ge(s["h_mm"], at["h_mm"] + g + 1)
                    for q in range(MG):
                        r = slice(MH * q, MH * q + MH)
                        nc.scalar.activation(hid_diag[r, g, :, q, :], bank[g % 2][r, 0:P].rearrange("p (b s) -> p b s", b=B), ACT.Gelu,
                                             bias=mb1[r, g:g + 1]).then_inc(s["h_gelu"], 1)

            def tensor(pe):
                if n == stages.index("m"):
                    pe.wait_ge(mix_set[3], 1)

                def turn_tokens(b, h):
                    if later(b):
                        pe.wait_ge(s["xT_ready"], at["xT_ready"] + b)
                    pe.wait_ge(s["unit"], at["unit"] + b + 1)
                    for k in range(TB):
                        pe.transpose(bank[0][:, k * P:k * P + P], xh[:, TB * h + k, :], ident).then_inc(s["turned"], 1)

                def logits_c(b, h):
                    pe.wait_ge(s["xT_ready"], at["xT_ready"] + b + 1)
                    if later(b):
                        pe.wait_ge(s["exp_c"], at["exp_c"] + TB * b)
                    for k in range(TB):
                        last = pe.matmul(bank[2 + k // 2][:, SLOTS * (k % 2):SLOTS * (k % 2) + SLOTS], xT[:, h, k * P:k * P + P], mu[:],
                                         start=True, stop=True)
                        if k % 2:
                            last.then_inc(s["logit_c"], 1)

                def logits_d(b, h):
                    if later(b):
                        pe.wait_ge(s["exp_d"], at["exp_d"] + 2 * b)
                    for j in range(2):
                        pe.matmul(bank[4 + j][:], mu[:, j * P:j * P + P], xT[:, h, :], start=True, stop=True).then_inc(s["logit_d"], 1)

                def turn_c(b, h):
                    pe.wait_ge(s["exp_c"], at["exp_c"] + TB * b + TB)
                    for j in range(2):
                        if later(b):
                            pe.wait_ge(s[f"kept_d{j}"], at[f"kept_d{j}"] + b)
                        for k in range(TB):
                            last = pe.transpose(bank[6 + j][:, k * P:k * P + P], comb[:, h, k, j * P:j * P + P], ident)
                        last.then_inc(s[f"turn_c{j}"], 1)

                def turn_d(b, h):
                    pe.wait_ge(s["exp_d"], at["exp_d"] + 2 * b + 2)
                    for m in range(2):
                        pe.wait_ge(s[f"kept_c{m}"], at[f"kept_c{m}"] + b + 1)
                        for k in range(2):
                            for j in range(2):
                                c = SLOTS * k + P * j
                                last = pe.transpose(bank[6 + m][:, c:c + P], disp_s[:, h, j, (2 * m + k) * P:(2 * m + k + 1) * P], ident)
                        last.then_inc(s[f"turn_d{m}"], 1)

                def slots_in(b, h):
                    for m in range(2):
                        pe.wait_ge(s[f"kept_d{m}"], at[f"kept_d{m}"] + b + 1)
                    for j in range(2):
                        for k in range(TB):
                            last = pe.matmul(bank[1][:, j * D:j * D + D], disp[:, h, k, j * P:j * P + P], xn[:, bass.ds(TB * b + k, 1), :],
                                             start=(k == 0), stop=(k == TB - 1))
                    last.then_inc(s["in_mm"], 1)

                def turn_slots(b):
                    pe.wait_ge(s["in_kept"], at["in_kept"] + 2 * b + 2)
                    if later(b):
                        pe.wait_ge(s["slotT"], at["slotT"] + b)
                    for j in range(2):
                        last = pe.transpose(bank[1][:, SLOTS + j * P:SLOTS + j * P + P], slot_in[:, j, :], ident)
                    last.then_inc(s["in_turned"], 1)

                def step(b, h):
                    turn_tokens(b + 1, 1 - h)
                    if later(b):
                        turn_slots(b - 1)
                    turn_c(b, h)
                    logits_c(b + 1, 1 - h)
                    turn_d(b, h)
                    logits_d(b + 1, 1 - h)
                    slots_in(b, h)

                turn_tokens(0, 0)
                logits_c(0, 0)
                logits_d(0, 0)
                step(0, 0)
                step(1, 1)
                step(2, 0)
                with pe.Fori(1, 3) as i:
                    step(2 * i + 1, 1)
                    step(2 * i + 2, 0)
                turn_slots(6)
                turn_c(7, 1)
                turn_d(7, 1)
                slots_in(7, 1)
                turn_slots(7)
                pe.wait_ge(s["slotT"], at["slotT"] + B)
                pe.wait_ge(mixw_in, MIXW)
                for g in range(MG):
                    if g >= 2:
                        pe.wait_ge(s["h_gelu"], at["h_gelu"] + MG * (g - 1))
                    for q in range(MG):
                        last = pe.matmul(bank[g % 2][MH * q:MH * q + MH, 0:P], mw1[:, MG * g + q, :],
                                         slotT[:, MG * g + q].rearrange("p b s -> p (b s)"), start=True, stop=True)
                    last.then_inc(s["h_mm"], 1)
                for h in range(2):
                    pe.wait_ge(s["h_gelu"], at["h_gelu"] + MG * (2 * h + 2))
                    for j in range(2):
                        for b in range(4 * j, 4 * j + 4):
                            for g in (2 * h, 2 * h + 1):
                                r = 64 * (g % 2)
                                last = pe.matmul(bank[2 + 2 * h + j][r:r + 64, (b % 4) * D:(b % 4) * D + D],
                                                 hid_diag[:, g, b].rearrange("p q s -> p (q s)"), mw2[:, g, :], start=True, stop=True)
                        last.then_inc(s["out_mm"], 1)
                pe.wait_ge(s["out_kept"], at["out_kept"] + 4)
                for b in range(B):
                    if b >= 4:
                        pe.wait_ge(x_done[n + 1], TB * (b - 3))
                    for k in range(TB):
                        for j in range(2):
                            last = pe.matmul(bank[Y_BANK[b % 4]][:, k * D:k * D + D], combT[:, j, b, k * P:k * P + P], slot_out[:, j, b, :],
                                             start=(j == 0), stop=(j == 1))
                    last.then_inc(s["y_mm"], 1)

            return dict(sync=lambda sp: None, vector=vector, scalar=scalar, tensor=tensor, gpsimd=gpsimd)


        def attention(n):
            s = {k: sem(f"a{n}_{k}") for k in (
                "normed misc_mm misc_read rope_v parts max_mm max_read exp_mm "
                "prob values sums_mm sums_read m_cut m_rows steps set_up rope_read sines".split())}
            stack_in = [sem(f"a{n}_stack_in{i}") for i in range(2)]
            m_in = [sem(f"a{n}_m_in{i}") for i in range(2)]
            swap_in = sem(f"a{n}_swap_in")
            at = dict.fromkeys(s, 0)
            HALF = H // 2

            STEPS = ((0, "xt"), (1, "p0"), (2, "p1"), (3, "m1"), (7, "n0"), (8, "n1"), (9, "m0"),
                     (10, "n2"), (11, "n3"), (12, "to"), (13, "wo"), (15, "v"))
            RANGE = {"x": (-1, B - 2), "p": (-1, B - 2), "m1": (1, B), "m0": (0, B - 1), "n": (2, B + 1), "t": (2, B + 1),
                     "w": (2, B + 1), "v": (0, B - 1)}

            def active(i, step):
                if not isinstance(i, int):
                    return True
                lo, hi = RANGE[step if step in RANGE else step[0]]
                return lo <= i <= hi

            before = {}
            count = 0
            for i in range(-1, B + 2):
                before[i] = count
                count += sum(active(i, step) for _, step in STEPS)

            def uses_before(i):
                return before[i] if isinstance(i, int) else before[2] + len(STEPS) * (i - 2)

            def odd_jobs(i, hh):
                base = uses_before(i)
                for k, (slot, step) in enumerate(st for st in STEPS if active(i, st[1])):
                    if slot == hh:
                        yield step, base + k

            def maxing(i):
                return not isinstance(i, int) or 0 <= i < B

            def exping(i):
                return not isinstance(i, int) or 1 <= i <= B

            SUM_BLOCKS = {1: (0,), 2: (1,), 3: (2, 3)}

            def groups(i, hh):
                if hh % 4:
                    g = hh // 4 - 1
                    b = i - 1
                    if g < 0:
                        g, b = 3, i - 2
                    if not isinstance(i, int) or 0 <= b < B:
                        yield b, g, 4 * b + g

            MAX_UNITS = ((0, (1,)), (1, (3,)), (2, (2, 0)))
            UNITS = {}
            for hh in range(H):
                UNITS[hh] = [("a", hh, hh + hh // 2)]
                if hh % 2:
                    UNITS[hh].append(("b", hh, hh + hh // 2 + 1))
            N_UNITS = H + H // 2

            def turns(engine, body):
                for i in (-1, 0, 1):
                    body(i, i % 2)
                with engine.Fori(1, 3) as r:
                    for par in range(2):
                        body(2 * r + par, par)
                for i in range(6, B + 2):
                    body(i, i % 2)

            def tensor(pe):
                pe.wait_ge(att_w, 1)

                def step_(i, par, step, m):
                    nxt = 1 - par
                    to = bank[7]
                    if m is not None and not (isinstance(m, int) and m == 0):
                        pe.wait_ge(s["misc_read"], m)
                    if step == "xt":
                        for k in range(TB):
                            pe.wait_ge(s["normed"], TB * (i + 1) + k + 1)
                            last = pe.transpose(to[:, k * P:k * P + P], xh[:, 4 * nxt + k, :], ident)
                    elif step[0] == "p":
                        last = pe.matmul(to[:], wqk[:, int(step[1]), :], xT[:, nxt, :], start=True, stop=True)
                    elif step == "v":
                        for k in range(TB):
                            last = pe.matmul(to[:, k * P:k * P + P], xT[:, par, k * P:k * P + P], wqkv[:, 2 * D:], start=True, stop=True)
                    elif step[0] == "m":
                        half = int(step[1])
                        pe.wait_ge(s["m_cut"], 2 * i + 1 if half == 0 else 2 * i)
                        for k in range(TB):
                            last = pe.transpose(to[0:3 * HALF, :].bitcast(BF16)[:, k * P:k * P + P],
                                                m_cut[:, half, k].rearrange("p c h -> p (c h)"), ident_bf[:])
                    elif step[0] == "n":
                        pe.wait_ge(s["sums_read"], TB * (i - 1))
                        k = int(step[1])
                        for g in range(TB):
                            last = pe.transpose(to[:, g * P:g * P + P], o_t[par][:, g, k * P:k * P + P], ident)
                    elif step == "to":
                        for k in range(TB):
                            last = pe.transpose(to[:, k * P:k * P + P], o_tok[:, k, :], ident)
                    elif step == "wo":
                        for k in range(TB):
                            last = pe.matmul(to[:, k * P:k * P + P], o_hd[:, k * P:k * P + P], wout[:], start=True, stop=True)
                    last.then_inc(s["misc_mm"], 1)

                def maxima(i, par, hh, unit, blocks):
                    half = hh // HALF
                    if hh % HALF == 0 and unit == 0:
                        pe.wait_ge(stack_in[half], 16 * 2 * len(Q_PART) * (i + 1))
                    number = 3 * (H * i + hh) + unit
                    to = bank[number % 2 if isinstance(i, int) else (3 * hh + unit) % 2]
                    if not (isinstance(i, int) and number < 2):
                        pe.wait_ge(s["max_read"], number - 1)
                    for col, k in zip((0, 3 * P), blocks):
                        n_keys = (k + 1) * P
                        pe.matmul(to[:, col:col + n_keys], q_stack[par][0:STACK, hh, k * P:k * P + P], k_stack[par][0:STACK, hh, 0:n_keys],
                                  start=True, stop=False)
                        last = pe.matmul(to[:, col + k * P:col + n_keys], ident_bf[:], mask_q[:], start=False, stop=True)
                    last.then_inc(s["max_mm"], 1)

                def exponents(i, par, hh, which):
                    prev = 1 - par
                    rows = STACK + 3
                    if hh % HALF == 0:
                        pe.wait_ge(m_in[hh // HALF], 16 * i)
                    for kind, h, u in UNITS[hh][which:which + 1]:
                        number = N_UNITS * (i - 1) + u
                        b0 = 2 + 2 * (u % 2)
                        if not (isinstance(i, int) and number < 2):
                            pe.wait_ge(s["prob"], number - 1)
                        for head, k, to in (((h, 0, bank[b0][:]), (h, 1, bank[b0 + 1][:, 0:3 * P]), (h, 3, bank[b0 + 1][:, 3 * P:])) if kind == "a"
                                            else ((h - 1, 2, bank[b0][:, 0:2 * P]), (h, 2, bank[b0][:, 2 * P:]))):
                            pe.matmul(to, k_stack[prev][0:rows, head, k * P:k * P + P], q_stack[prev][0:rows, head, k * P:], start=True, stop=False)
                            last = pe.matmul(to[:, 0:P], ident_bf[:], mask_k[:], start=False, stop=True)
                        last.then_inc(s["exp_mm"], 1)

                def sums(b, g, number, vpar, blocks):
                    if blocks[0] == 0:
                        pe.wait_ge(s["prob"], N_UNITS * b + 6 * g + 6)
                        pe.wait_ge(s["values"], b + 1)
                        if later(number):
                            pe.wait_ge(s["sums_read"], number)
                    for k in blocks:
                        for j in range(4):
                            last = pe.matmul(bank[6][32 * j:32 * j + 32, k * P:], v_aug[vpar][:, k, 4 * g + j, :],
                                             prob_e[g % 2][:, j, E_AT[k]:E_AT[k] + S - k * P], start=(k == 0), stop=(k == TB - 1))
                    if blocks[-1] == TB - 1:
                        last.then_inc(s["sums_mm"], 1)

                def body(i, par):
                    for hh in range(H):
                        for turn, (unit, blocks) in enumerate(MAX_UNITS):
                            if maxing(i):
                                maxima(i, par, hh, unit, blocks)
                            if exping(i) and turn < len(UNITS[hh]):
                                exponents(i, par, hh, turn)
                            if turn == 0:
                                for b, g, number in groups(i, hh):
                                    sums(b, g, number, par if g == 3 else 1 - par, SUM_BLOCKS[hh % 4])
                            if turn == (1 if hh % 2 == 0 else 2):
                                for step, m in odd_jobs(i, hh):
                                    step_(i, par, step, m)

                turns(pe, body)

            def vector(dve):
                steps = Chain(dve, s["steps"])
                STEPS_A_TURN = 12
                if n == stages.index("a"):
                    dve.wait_ge(attw_in, 48)
                    nc.vector.tensor_copy(ident_bf[:], ident)
                    nc.vector.tensor_copy(mask_q[:], rot[:, R_MQ:R_MQ + P])
                    nc.vector.tensor_copy(mask_k[:], rot[:, R_MK:R_MK + P])
                    for m in range(2):
                        w = wqkv[:, m * D:m * D + D].rearrange("p (a h d) -> p a d h", a=2, d=DH)
                        for half in range(2):
                            last = nc.vector.tensor_copy(wqk[:, m, :].rearrange("p (a d h) -> p a d h", a=2, d=DH)[:, half], w[:, half])
                    last.then_inc(att_w, 1)

                def body(i, par):
                    for hh in range(H):
                        if hh == 6 and active(i, "xt"):
                            dve.wait_ge(swap_in, 16 * 4 * (i + 2))
                            nc.vector.tensor_tensor(swapped[:], swapped[:], sin.unsqueeze(1).to_broadcast([P, 2, S]), ALU.mult).then_inc(s["sines"], 1)
                        if maxing(i):
                            for unit, blocks in MAX_UNITS:
                                number = 3 * (H * i + hh) + unit
                                frm = bank[number % 2 if isinstance(i, int) else (3 * hh + unit) % 2]
                                dve.wait_ge(s["max_mm"], number + 1)
                                for col, k in zip((0, 3 * P), blocks):
                                    last = nc.vector.tensor_reduce(neg_m[:, par, k, hh:hh + 1], frm[:, col:col + (k + 1) * P], AX.X, ALU.max, negate=True)
                                last.then_inc(s["max_read"], 1)
                            if hh % HALF == HALF - 1:
                                half = hh // HALF
                                dve.wait_ge(s["max_read"], 3 * (H * i + hh) + 3)
                                v = neg_m[:, par, :, HALF * half:HALF * half + HALF]
                                c = [m_cut[:, half, :, r, :] for r in range(3)]
                                steps(nc.vector.tensor_copy(c[0], v))
                                steps(nc.vector.tensor_tensor(m_left[:], v, c[0], ALU.subtract))
                                steps(nc.vector.tensor_copy(c[1], m_left[:]))
                                steps(nc.vector.tensor_tensor(c[2], m_left[:], c[1], ALU.subtract))
                                dve.sem_inc(s["m_cut"], 1)
                        for step, m in odd_jobs(i, hh):
                            if step[0] == "m":
                                half = int(step[1])
                                dve.wait_ge(s["misc_mm"], m + 1)
                                prior = (i - 1 if half else i)
                                if not (isinstance(prior, int) and prior < 1):
                                    dve.wait_ge(m_in[half], 16 * prior)
                                nc.vector.tensor_copy(m_rows[:, half, :], bank[7][0:3 * HALF, :].bitcast(BF16)[:, 0:S]).then_inc(s["m_rows"], 1)
                                dve.wait_ge(s["m_rows"], 2 * i if half else 2 * i + 1)
                                dve.sem_inc(s["misc_read"], 1)
                            elif step[0] == "n":
                                k = int(step[1])
                                dve.wait_ge(s["misc_mm"], m + 1)
                                got = bank[7][:].rearrange("p (h c) -> p h c", c=32)
                                steps(nc.vector.reciprocal(o_den[:], got[:, :, DH]))
                                nc.vector.tensor_tensor(o_tok[:, k, :].rearrange("p (h c) -> p h c", c=DH), got[:, :, 0:DH],
                                                        o_den[:].unsqueeze(2).to_broadcast([P, H, DH]), ALU.mult).then_inc(s["misc_read"], 1)
                            elif step == "wo":
                                dve.wait_ge(s["misc_mm"], m + 1)
                                tiles = x[:, bass.ds(TB * (i - 2), TB), :]
                                nc.vector.tensor_tensor(tiles, tiles, bank[7][:].rearrange("p (k d) -> p k d", k=TB), ALU.add).then_inc(x_done[n + 1], TB)
                                dve.wait_ge(x_done[n + 1], TB * (i - 1))
                                dve.sem_inc(s["misc_read"], 1)

                body(-1, 1)
                rotate(dve, nc.vector, 0)
                for i in (0, 1):
                    body(i, i % 2)
                with dve.Fori(1, 3) as r:
                    first = steps.n
                    steps.shift = 2 * STEPS_A_TURN * (r - 1)
                    for par in range(2):
                        body(2 * r + par, par)
                    assert steps.n - first == 2 * STEPS_A_TURN
                steps.shift = 0
                steps.n += 2 * STEPS_A_TURN
                for i in range(6, B + 2):
                    if i == B + 1:
                        for g in range(GROUPS - 1):
                            stats_after(dve, n + 1, g)
                    body(i, i % 2)
                stats_after(dve, n + 1, GROUPS - 1)

            def scalar(act):
                def normalise(b, h):
                    for k in range(TB):
                        t = bass.ds(TB * b + k, 1)
                        nc.scalar.activation(xh[:, TB * h + k, :], x[:, t, :], ACT.Identity, bias=shift_by[:, t],
                                             scale=rstd[:, t]).then_inc(s["normed"], 1)

                stats_root(act, n, 0)
                stats_root(act, n, 1)
                act.wait_ge(ready_sem, GROUPS * n + 1)
                normalise(0, 0)
                for g in range(2, GROUPS):
                    stats_root(act, n, g)

                def body(i, par):
                    if isinstance(i, int) and i == B + 1:
                        for g in range(GROUPS - 1):
                            stats_root(act, n + 1, g)
                    nxt = 1 - par
                    for hh in range(H):
                        if hh == 12 and (not isinstance(i, int) or i + 2 < B):
                            act.wait_ge(s["misc_mm"], uses_before(i) + 1)
                            if isinstance(i, int) and i < 0:
                                act.wait_ge(ready_sem, GROUPS * n + GROUPS)
                            normalise(i + 2, par)
                        if exping(i):
                            for kind, h, u in UNITS[hh]:
                                number = N_UNITS * (i - 1) + u
                                b0 = 2 + 2 * (u % 2)
                                g = hh // 4
                                if hh % 4 == 0 and kind == "a" and not (isinstance(i, int) and 4 * (i - 1) + g - 1 < 1):
                                    act.wait_ge(s["sums_mm"], 4 * (i - 1) + g - 1)
                                act.wait_ge(s["exp_mm"], number + 1)
                                if kind == "a":
                                    frm = psum_pair[u % 2]
                                    to = prob_e[g % 2][:, h % 4, 0:2 * S]
                                else:
                                    frm = bank[b0][:].rearrange("p (h c) -> p h c", h=2)
                                    to = prob_e[g % 2][:, h % 4 - 1:h % 4 + 1, E_AT[2]:E_AT[2] + 2 * P]
                                nc.scalar.activation(to, frm, ACT.Exp, scale=DH ** -0.5).then_inc(s["prob"], 1)
                        for b, g, number in groups(i, hh):
                            if hh % 4 != 3:
                                continue
                            vpar = par if g == 3 else 1 - par
                            act.wait_ge(s["sums_mm"], number + 1)
                            nc.scalar.copy(o_t[vpar][:, g, :], bank[6][:]).then_inc(s["sums_read"], 1)
                        for step, m in odd_jobs(i, hh):
                            if step == "xt":
                                act.wait_ge(s["misc_mm"], m + 1)
                                nc.scalar.copy(xT[:, nxt, :], bank[7][:]).then_inc(s["misc_read"], 1)
                            elif step[0] == "p":
                                r = int(step[1])
                                act.wait_ge(s["misc_mm"], m + 1)
                                if later(i + 1):
                                    act.wait_ge(s["rope_read"], i + 1)
                                nc.scalar.copy(raw[:, r, :], bank[7][:]).then_inc(s["misc_read"], 1)
                            elif step == "v":
                                act.wait_ge(s["misc_mm"], m + 1)
                                act.wait_ge(s["set_up"], 6)
                                nc.scalar.copy(v_aug[par][:, :, :, 0:DH], bank[7][:].rearrange("p (k h d) -> p k h d", k=TB, h=H)).then_inc(s["values"], 1)
                                act.wait_ge(s["values"], i + 1)
                                act.sem_inc(s["misc_read"], 1)
                            elif step == "to":
                                act.wait_ge(s["misc_mm"], m + 1)
                                nc.scalar.copy(o_hd[:], bank[7][:]).then_inc(s["misc_read"], 1)

                turns(act, body)

            def gpsimd(pool):
                if n and stages[n - 1] == "m":
                    pool.wait_ge(mix_sems["h_mm"], MG * stages[:n].count("m"))
                elif n:
                    pool.wait_ge(x_done[n], T)
                pool.wait_ge(zeroed, 2)
                setup = Chain(pool, s["set_up"])
                for i in range(2):
                    setup(pool.memset(k_stack[i][32:64].rearrange("p h t -> p (h t)").bitcast(F32), ONE_ONE))
                for i in range(2):
                    setup(pool.memset(v_aug[i][:], 0.0))
                    setup(pool.memset(v_aug[i][:, :, :, DH:DH + 1], 1.0))
                for b in (1, 2):
                    rotate(pool, pool, b)
                with pool.Fori(3, 7) as b:
                    rotate(pool, pool, b)
                rotate(pool, pool, 7)

            def rotate(pool, issue, b):
                off = [k for k, st in enumerate(x for x in STEPS if active(b - 1, x[1])) if st[1] == "p1"][0]
                pool.wait_ge(s["misc_read"], uses_before(b - 1) + off + 1)
                pool.wait_ge(swap_in, 16 * 4 * (b + 1))
                for m in range(2):
                    issue.tensor_tensor(raw[:, m, :], raw[:, m, :], cos, ALU.mult).then_inc(s["rope_v"], 1)
                pool.wait_ge(s["sines"], b + 1)
                for m in range(2):
                    part = [cut[:, m, r, :] for r in range(3)]
                    done = 12 * b + 5 * m + 2
                    v, w = raw[:, m, :], swapped[:, m, :]
                    pool.wait_ge(s["rope_v"], done)
                    if m == 0 and later(b):
                        for half in range(2):
                            pool.wait_ge(stack_in[half], 16 * 2 * len(Q_PART) * b)
                    issue.tensor_tensor(part[0], v, w, ALU.add).then_inc(s["rope_v"], 1)
                    pool.wait_ge(s["rope_v"], done + 1)
                    issue.tensor_tensor(v, v, w, ALU.add).then_inc(s["rope_v"], 1)
                    pool.wait_ge(s["rope_v"], done + 2)
                    issue.tensor_tensor(part[1], v, part[0], ALU.subtract).then_inc(s["rope_v"], 1)
                    pool.wait_ge(s["rope_v"], done + 3)
                    issue.tensor_tensor(v, v, part[0], ALU.subtract).then_inc(s["rope_v"], 1)
                    pool.wait_ge(s["rope_v"], done + 4)
                    issue.tensor_tensor(part[2], v, part[1], ALU.subtract).then_inc(s["rope_v"], 1)
                    pool.wait_ge(s["rope_v"], done + 5)
                pool.sem_inc(s["rope_read"], 1)
                pool.sem_inc(s["parts"], 1)

            def sync(sp):
                sp.wait_ge(s["set_up"], 2)

                def maximum(b, par, half):
                    sp.wait_ge(s["m_rows"], 2 * b + 1 + half)
                    sp.dma_start(q_stack[par][STACK:STACK + 3, HALF * half:HALF * half + HALF, :], m_rows[:, half, :]).then_inc(m_in[half], 16)

                def swap(i):
                    off = [k for k, st in enumerate(x for x in STEPS if active(i, x[1])) if st[1] == "p1"][0]
                    sp.wait_ge(s["misc_read"], uses_before(i) + off + 1)
                    for r in range(4):
                        to = 32 * (r ^ 1)
                        sp.dma_start(swapped[to:to + 32], raw[32 * r:32 * r + 32]).then_inc(swap_in, 16)

                def stack(b, par, half):
                    if half == 0:
                        sp.wait_ge(s["parts"], b + 1)
                    if not (isinstance(b, int) and b < 2):
                        sp.wait_ge(s["exp_mm"], N_UNITS * (b - 2) + N_UNITS // 2 * (half + 1))
                    for r in range(len(Q_PART)):
                        for m, to, part in ((0, q_stack, Q_PART), (1, k_stack, K_PART)):
                            sp.dma_start(to[par][DH * r:DH * r + DH, HALF * half:HALF * half + HALF, :],
                                         cut[64 * half:64 * half + 64, m, part[r], :]).then_inc(stack_in[half], 16)

                def body(i, par):
                    if not isinstance(i, int) or 1 <= i <= B:
                        maximum(i - 1, 1 - par, 1)
                    if active(i, "xt"):
                        swap(i)
                    if maxing(i):
                        maximum(i, par, 0)
                    if active(i, "xt"):
                        for half in range(2):
                            stack(i + 1, 1 - par, half)

                turns(sp, body)

            return dict(sync=sync, vector=vector, scalar=scalar, tensor=tensor, gpsimd=gpsimd)

        kinds = {"f": ffn, "s": scan, "m": mix, "a": attention}
        parts = [kinds[k](n) for n, k in enumerate(stages)]
        block = ctx.enter_context(nc.Block())

        @block.sync
        def _(sp):
            load_sync(sp)
            for part in parts:
                part["sync"](sp)
            to = out.rearrange("b (k p) d -> p (b k) d", p=P)
            for g in range(GROUPS):
                sp.wait_ge(x_done[len(stages)], GT * g + GT)
                sp.dma_start(to[:, GT * g:GT * g + GT, :], x[:, GT * g:GT * g + GT, :]).then_inc(stored_out, 16)
            sp.wait_ge(stored_out, 16 * GROUPS)

        @block.scalar
        def _(act):
            load_scalar(act)
            for part in parts:
                part["scalar"](act)

        @block.vector
        def _(dve):
            for g in range(GROUPS):
                stats_after(dve, 0, g)
            setup_vector(dve, Chain(dve, sem("setup_v")))
            for part in parts:
                part["vector"](dve)

        @block.gpsimd
        def _(pool):
            setup_gpsimd(pool)
            for part in parts:
                part["gpsimd"](pool)

        @block.tensor
        def _(pe):
            setup_tensor(pe)
            for part in parts:
                part["tensor"](pe)


STAGES = "fsfmam"


def kernel(**inputs):
    import concourse.bacc as bacc
    from concourse.bass_utils import run_bass_kernel_spmd

    nc = bacc.Bacc("TRN2", target_bir_lowering=False, num_devices=1)
    arrays = {f"in_{k}": np.ascontiguousarray(v) for k, v in inputs.items()}
    arrays["in_consts"] = shape_constants()
    arrays["in_rotary"] = rotary_constants()
    ap = {k: nc.dram_tensor(k, v.shape, F32, kind="ExternalInput").ap() for k, v in arrays.items()}
    out = nc.dram_tensor("out", (B, S, D), F32, kind="ExternalOutput").ap()
    xhat_dram = nc.dram_tensor("xhat_rows", (B * S, D), F32).ap()
    yrow_dram = nc.dram_tensor("result_rows", (B * S, D), F32).ap()
    build(nc, {k[3:]: v for k, v in ap.items()}, ap["in_consts"], ap["in_rotary"], out, xhat_dram, yrow_dram, STAGES)
    return run_bass_kernel_spmd(nc, [arrays], core_ids=[0]).results[0]["out"]
```
